# Optimizing a Trainium2 kernel written in Bass

```python
import numpy as np
import jax
import jax.numpy as jnp

def _softmax(x, axis=-1):
    return jax.nn.softmax(x, axis=axis)

def _gelu(x):
    return jax.nn.gelu(x, approximate=True)

def _silu(x):
    return jax.nn.silu(x)

def _sigmoid(x):
    return jax.nn.sigmoid(x)

def _layernorm(x, axis=-1, eps=1e-05):
    m = jnp.mean(x, axis=axis, keepdims=True)
    v = jnp.var(x, axis=axis, keepdims=True)
    return (x - m) / jnp.sqrt(v + eps)

def _scatter_add(tgt, idx, src, axis=0):
    return tgt.at[idx].add(src)

def _segment_sum(src, seg, n):
    return jax.ops.segment_sum(src, seg, n)
kernel_name = 'mk_decoder_postln_d2_seqx_r8_83b1b7'

def setup_inputs(seed: int=0):
    np.random.seed(seed)
    _w = jnp.asarray

    def _rec_inputs():
        import jax
        import jax.numpy as jnp
        _rk = jax.random.key(seed)
        x = -0.000125 + 0.9999 * jax.random.normal(jax.random.fold_in(_rk, 1), (8, 128, 512), jnp.float32)
        _lenS = 128 - jax.random.randint(jax.random.fold_in(_rk, 7), (8,), 0, max(1, 128 // 4) + 1, jnp.int32)
        _lenS2 = 128 - jax.random.randint(jax.random.fold_in(_rk, 8), (8,), 0, max(1, 128 // 4) + 1, jnp.int32)
        _ctx_4096P = jax.random.normal(jax.random.fold_in(_rk, 11), (8, 16, 512), jnp.float32)
        _ctx_4096c = jax.random.dirichlet(jax.random.fold_in(_rk, 511), 0.3 * jnp.ones((16,), jnp.float32), (8, 128))
        _ctx_4096t = jnp.einsum('bsk,bkd->bsd', _ctx_4096c, _ctx_4096P)
        _ctx_4096t = _ctx_4096t * jax.lax.rsqrt(jnp.mean(jnp.square(_ctx_4096t)) + 1e-12) * 0.953939
        ctx_4096 = -1.52775e-05 + 0.999936 * (_ctx_4096t + 0.3 * jax.random.normal(jax.random.fold_in(_rk, 611), (8, 128, 512), jnp.float32))
        return (x, ctx_4096)
    x, ctx_4096 = _rec_inputs()

    def _L0_attn_setup():
        import jax, jax.numpy as jnp
        import numpy as np
        import math
        B, L, D, H = (32, 64, 512, 32)
        HD = D // H
        key = jax.random.key(seed)
        ks = jax.random.split(key, 9)
        s = 1.0 / math.sqrt(D)
        return {'x': jax.random.normal(ks[0], (B, L, D), jnp.float32), 'Wq': jax.random.normal(ks[1], (D, D), jnp.float32) * s, 'bq': jax.random.normal(ks[2], (D,), jnp.float32) * s, 'Wk': jax.random.normal(ks[3], (D, D), jnp.float32) * s, 'bk': jax.random.normal(ks[4], (D,), jnp.float32) * s, 'Wv': jax.random.normal(ks[5], (D, D), jnp.float32) * s, 'bv': jax.random.normal(ks[6], (D,), jnp.float32) * s, 'Wo': jax.random.normal(ks[7], (D, D), jnp.float32) * s, 'bo': jax.random.normal(ks[8], (D,), jnp.float32) * s}
    _L0_attn_all = _L0_attn_setup()
    _L0_attn_in = {k: v for k, v in _L0_attn_all.items() if k in ('Wq', 'bq', 'Wk', 'bk', 'Wv', 'bv', 'Wo', 'bo')}
    del _L0_attn_all

    def _L0_xattn_setup():
        import jax, jax.numpy as jnp
        import numpy as np
        H = 8
        C = 2

        def _autocorrelation(Q, K, V):
            B, L, D = Q.shape
            d = D // H
            q = Q.reshape(B, L, H, d).transpose(0, 2, 1, 3)
            k = K.reshape(B, L, H, d).transpose(0, 2, 1, 3)
            v = V.reshape(B, L, H, d).transpose(0, 2, 1, 3)
            qf = jnp.fft.fft(q, axis=2)
            kf = jnp.fft.fft(k, axis=2)
            corr = jnp.fft.ifft(qf * jnp.conj(kf), axis=2).real
            topk = int(C * np.log(L))
            w, idx = jax.lax.top_k(corr.transpose(0, 1, 3, 2), topk)
            w = jax.nn.softmax(w, axis=-1)
            pos = jnp.arange(L)[:, None]
            out = jnp.zeros_like(v)
            for i in range(topk):
                g = jnp.minimum(idx[:, :, None, :, i] + pos, L - 1)
                out = out + w[:, :, None, :, i] * jnp.take_along_axis(v, g, axis=2)
            return out.transpose(0, 2, 1, 3).reshape(B, L, D)
        key = jax.random.key(seed)
        k1, k2, k3 = jax.random.split(key, 3)
        B, L, D = (16, 64, 512)
        Q = jax.random.normal(k1, (B, L, D), dtype=jnp.float32)
        K = jax.random.normal(k2, (B, L, D), dtype=jnp.float32)
        V = jax.random.normal(k3, (B, L, D), dtype=jnp.float32)
        return {'Q': Q, 'K': K, 'V': V}
    _L0_xattn_all = _L0_xattn_setup()
    _L0_xattn_in = {k: v for k, v in _L0_xattn_all.items() if k in ()}
    del _L0_xattn_all

    def _L0_ffn_setup():
        import jax, jax.numpy as jnp
        import numpy as np
        N_EXPERTS = 28
        TOP_K = 2
        RANK = 8
        LORA_ALPHA = 16
        SCALING = LORA_ALPHA / RANK
        TEMP = 1.0
        key = jax.random.key(seed)
        ks = jax.random.split(key, 5)
        B, S, D_IN, D_OUT = (4, 256, 512, 512)
        x = jax.random.normal(ks[0], (B, S, D_IN), dtype=jnp.float32)
        base_W = jax.random.normal(ks[1], (D_OUT, D_IN), dtype=jnp.float32) * (1.0 / np.sqrt(D_IN))
        gate_W = jax.random.normal(ks[2], (N_EXPERTS, D_IN), dtype=jnp.float32) * (1.0 / np.sqrt(D_IN))
        lora_A = jax.random.normal(ks[3], (N_EXPERTS, RANK, D_IN), dtype=jnp.float32) * (1.0 / np.sqrt(D_IN))
        lora_B = jax.random.normal(ks[4], (N_EXPERTS, D_OUT, RANK), dtype=jnp.float32) * 0.01
        return {'x': x, 'base_W': base_W, 'gate_W': gate_W, 'lora_A': lora_A, 'lora_B': lora_B}
    _L0_ffn_all = _L0_ffn_setup()
    _L0_ffn_in = {k: v for k, v in _L0_ffn_all.items() if k in ('base_W', 'gate_W', 'lora_A', 'lora_B')}
    del _L0_ffn_all

    def _L1_attn_setup():
        import jax, jax.numpy as jnp
        import numpy as np
        D_MODEL = 512
        N_HEADS = 32
        HEAD_DIM = D_MODEL // N_HEADS
        CLIP_QKV = 8.0
        ALIBI_BIAS_MAX = 8.0
        LN_EPS = 1e-05

        def _alibi_slopes(n_heads: int, bias_max: float) -> jnp.ndarray:
            next_pow2 = 2 ** int(np.ceil(np.log2(n_heads)))
            m = np.arange(1, next_pow2 + 1, dtype=np.float32) * (bias_max / next_pow2)
            slopes = 1.0 / np.power(2.0, m)
            if next_pow2 != n_heads:
                slopes = np.concatenate([slopes[1::2], slopes[::2]])[:n_heads]
            return jnp.asarray(slopes)

        def _layer_norm(x, w, b):
            mu = jnp.mean(x, axis=-1, keepdims=True)
            var = jnp.mean(jnp.square(x - mu), axis=-1, keepdims=True)
            return (x - mu) * jax.lax.rsqrt(var + LN_EPS) * w + b
        key = jax.random.key(seed)
        ks = jax.random.split(key, 3)
        B, S = (1, 256)
        hidden_states = jax.random.normal(ks[0], (B, S, D_MODEL), dtype=jnp.float32)
        Wqkv = jax.random.normal(ks[1], (3 * D_MODEL, D_MODEL), dtype=jnp.float32) * 0.02
        Wout = jax.random.normal(ks[2], (D_MODEL, D_MODEL), dtype=jnp.float32) * 0.02
        return {'hidden_states': hidden_states, 'Wqkv': Wqkv, 'q_ln_w': jnp.ones((D_MODEL,), jnp.float32), 'q_ln_b': jnp.zeros((D_MODEL,), jnp.float32), 'k_ln_w': jnp.ones((D_MODEL,), jnp.float32), 'k_ln_b': jnp.zeros((D_MODEL,), jnp.float32), 'Wout': Wout}
    _L1_attn_all = _L1_attn_setup()
    _L1_attn_in = {k: v for k, v in _L1_attn_all.items() if k in ('Wqkv', 'q_ln_w', 'q_ln_b', 'k_ln_w', 'k_ln_b', 'Wout')}
    del _L1_attn_all

    def _L1_xattn_setup():
        import jax, jax.numpy as jnp
        import numpy as np
        B, Q, D = (8, 64, 512)
        CTX = 512
        H, KV, HD = (16, 4, 96)
        G = H // KV
        key = jax.random.key(seed)
        ks = jax.random.split(key, 6)
        s = 0.02
        return {'latents': jax.random.normal(ks[0], (B, Q, D), jnp.float32), 'context': jax.random.normal(ks[1], (B, CTX, D), jnp.float32), 'Wq': jax.random.normal(ks[2], (H * HD, D), jnp.float32) * s, 'Wk': jax.random.normal(ks[3], (KV * HD, D), jnp.float32) * s, 'Wv': jax.random.normal(ks[4], (KV * HD, D), jnp.float32) * s, 'Wo': jax.random.normal(ks[5], (D, H * HD), jnp.float32) * s}
    _L1_xattn_all = _L1_xattn_setup()
    _L1_xattn_in = {k: v for k, v in _L1_xattn_all.items() if k in ('Wq', 'Wk', 'Wv', 'Wo')}
    del _L1_xattn_all

    def _L1_ffn_setup():
        import jax, jax.numpy as jnp
        import numpy as np
        ALPHA = 32
        R = 16
        SCALING = ALPHA / R
        key = jax.random.key(seed)
        k1, k2, k3, k4 = jax.random.split(key, 4)
        B_, S, D = (4, 256, 512)
        H, r, O = (8, R, 512)
        x = jax.random.normal(k1, (B_, S, D), dtype=jnp.float32)
        A = jax.random.normal(k2, (H, r, D), dtype=jnp.float32) * 0.02
        Bm = jax.random.normal(k3, (H, O, r), dtype=jnp.float32) * 0.02
        Wr = jax.random.normal(k4, (H, D), dtype=jnp.float32) * 0.02
        br = jnp.zeros((H,), dtype=jnp.float32)
        return {'x': x, 'A': A, 'B': Bm, 'Wr': Wr, 'br': br}
    _L1_ffn_all = _L1_ffn_setup()
    _L1_ffn_in = {k: v for k, v in _L1_ffn_all.items() if k in ('A', 'B', 'Wr', 'br')}
    del _L1_ffn_all
    return {'x': x, 'ctx_4096': ctx_4096, 'L0_attn_Wq': _L0_attn_in['Wq'], 'L0_attn_bq': _L0_attn_in['bq'], 'L0_attn_Wk': _L0_attn_in['Wk'], 'L0_attn_bk': _L0_attn_in['bk'], 'L0_attn_Wv': _L0_attn_in['Wv'], 'L0_attn_bv': _L0_attn_in['bv'], 'L0_attn_Wo': _L0_attn_in['Wo'], 'L0_attn_bo': _L0_attn_in['bo'], 'L0_ffn_base_W': _L0_ffn_in['base_W'], 'L0_ffn_gate_W': _L0_ffn_in['gate_W'], 'L0_ffn_lora_A': _L0_ffn_in['lora_A'], 'L0_ffn_lora_B': _L0_ffn_in['lora_B'], 'L1_attn_Wqkv': _L1_attn_in['Wqkv'], 'L1_attn_q_ln_w': _L1_attn_in['q_ln_w'], 'L1_attn_q_ln_b': _L1_attn_in['q_ln_b'], 'L1_attn_k_ln_w': _L1_attn_in['k_ln_w'], 'L1_attn_k_ln_b': _L1_attn_in['k_ln_b'], 'L1_attn_Wout': _L1_attn_in['Wout'], 'L1_xattn_Wq': _L1_xattn_in['Wq'], 'L1_xattn_Wk': _L1_xattn_in['Wk'], 'L1_xattn_Wv': _L1_xattn_in['Wv'], 'L1_xattn_Wo': _L1_xattn_in['Wo'], 'L1_ffn_A': _L1_ffn_in['A'], 'L1_ffn_B': _L1_ffn_in['B'], 'L1_ffn_Wr': _L1_ffn_in['Wr'], 'L1_ffn_br': _L1_ffn_in['br']}

def reference(x, ctx_4096, L0_attn_Wq, L0_attn_bq, L0_attn_Wk, L0_attn_bk, L0_attn_Wv, L0_attn_bv, L0_attn_Wo, L0_attn_bo, L0_ffn_base_W, L0_ffn_gate_W, L0_ffn_lora_A, L0_ffn_lora_B, L1_attn_Wqkv, L1_attn_q_ln_w, L1_attn_q_ln_b, L1_attn_k_ln_w, L1_attn_k_ln_b, L1_attn_Wout, L1_xattn_Wq, L1_xattn_Wk, L1_xattn_Wv, L1_xattn_Wo, L1_ffn_A, L1_ffn_B, L1_ffn_Wr, L1_ffn_br):
    import jax
    import jax.numpy as jnp

    def _L0_attn_ref(x, Wq, bq, Wk, bk, Wv, bv, Wo, bo):
        import jax, jax.numpy as jnp
        import numpy as np
        import math
        B, L, D, H = (32, 64, 512, 32)
        HD = D // H
        b, l, d = x.shape
        h, hd = (H, HD)
        q = (x @ Wq.T + bq).reshape(b, l, h, hd).transpose(0, 2, 1, 3)
        k = (x @ Wk.T + bk).reshape(b, l, h, hd).transpose(0, 2, 1, 3)
        v = (x @ Wv.T + bv).reshape(b, l, h, hd).transpose(0, 2, 1, 3)
        scores = jnp.einsum('bhqd,bhkd->bhqk', q, k) / math.sqrt(hd)
        causal = jnp.tril(jnp.ones((l, l), bool))
        scores = jnp.where(causal, scores, -jnp.inf)
        att = jax.nn.softmax(scores, axis=-1)
        out = jnp.einsum('bhqk,bhkd->bhqd', att, v)
        out = out.transpose(0, 2, 1, 3).reshape(b, l, d)
        return out @ Wo.T + bo

    def _L0_xattn_ref(Q, K, V):
        import jax, jax.numpy as jnp
        import numpy as np
        H = 8
        C = 2

        def _autocorrelation(Q, K, V):
            B, L, D = Q.shape
            d = D // H
            q = Q.reshape(B, L, H, d).transpose(0, 2, 1, 3)
            k = K.reshape(B, L, H, d).transpose(0, 2, 1, 3)
            v = V.reshape(B, L, H, d).transpose(0, 2, 1, 3)
            qf = jnp.fft.fft(q, axis=2)
            kf = jnp.fft.fft(k, axis=2)
            corr = jnp.fft.ifft(qf * jnp.conj(kf), axis=2).real
            topk = int(C * np.log(L))
            w, idx = jax.lax.top_k(corr.transpose(0, 1, 3, 2), topk)
            w = jax.nn.softmax(w, axis=-1)
            pos = jnp.arange(L)[:, None]
            out = jnp.zeros_like(v)
            for i in range(topk):
                g = jnp.minimum(idx[:, :, None, :, i] + pos, L - 1)
                out = out + w[:, :, None, :, i] * jnp.take_along_axis(v, g, axis=2)
            return out.transpose(0, 2, 1, 3).reshape(B, L, D)
        return _autocorrelation(Q, K, V)

    def _L0_ffn_ref(x, base_W, gate_W, lora_A, lora_B):
        import jax, jax.numpy as jnp
        import numpy as np
        N_EXPERTS = 28
        TOP_K = 2
        RANK = 8
        LORA_ALPHA = 16
        SCALING = LORA_ALPHA / RANK
        TEMP = 1.0
        B, S, D_in = x.shape
        xf = x.reshape(B * S, D_in)
        base = xf @ base_W.T
        logits = xf @ gate_W.T
        top_vals, top_idx = jax.lax.top_k(logits, TOP_K)
        top_probs = jax.nn.softmax(top_vals / TEMP, axis=-1)
        N = xf.shape[0]
        gate_full = jnp.zeros((N, N_EXPERTS), dtype=xf.dtype).at[jnp.arange(N)[:, None], top_idx].add(top_probs)
        h = jnp.einsum('nd,erd->ner', xf, lora_A)
        h = h * (gate_full * SCALING)[:, :, None]
        lora_out = jnp.einsum('ner,eor->no', h, lora_B)
        out = base + lora_out
        return out.reshape(B, S, -1)

    def _L1_attn_ref(hidden_states, Wqkv, q_ln_w, q_ln_b, k_ln_w, k_ln_b, Wout):
        import jax, jax.numpy as jnp
        import numpy as np
        D_MODEL = 512
        N_HEADS = 32
        HEAD_DIM = D_MODEL // N_HEADS
        CLIP_QKV = 8.0
        ALIBI_BIAS_MAX = 8.0
        LN_EPS = 1e-05

        def _alibi_slopes(n_heads: int, bias_max: float) -> jnp.ndarray:
            next_pow2 = 2 ** int(np.ceil(np.log2(n_heads)))
            m = np.arange(1, next_pow2 + 1, dtype=np.float32) * (bias_max / next_pow2)
            slopes = 1.0 / np.power(2.0, m)
            if next_pow2 != n_heads:
                slopes = np.concatenate([slopes[1::2], slopes[::2]])[:n_heads]
            return jnp.asarray(slopes)

        def _layer_norm(x, w, b):
            mu = jnp.mean(x, axis=-1, keepdims=True)
            var = jnp.mean(jnp.square(x - mu), axis=-1, keepdims=True)
            return (x - mu) * jax.lax.rsqrt(var + LN_EPS) * w + b
        B, S, _ = hidden_states.shape
        qkv = jnp.einsum('bsd,ed->bse', hidden_states, Wqkv)
        qkv = jnp.clip(qkv, -CLIP_QKV, CLIP_QKV)
        q, k, v = jnp.split(qkv, [D_MODEL, 2 * D_MODEL], axis=-1)
        q = _layer_norm(q, q_ln_w, q_ln_b)
        k = _layer_norm(k, k_ln_w, k_ln_b)
        q = q.reshape(B, S, N_HEADS, HEAD_DIM)
        k = k.reshape(B, S, N_HEADS, HEAD_DIM)
        v = v.reshape(B, S, N_HEADS, HEAD_DIM)
        scale = HEAD_DIM ** (-0.5)
        scores = jnp.einsum('bqhd,bkhd->bhqk', q, k) * scale
        slopes = _alibi_slopes(N_HEADS, ALIBI_BIAS_MAX)
        pos = jnp.arange(S)
        rel = (pos[None, :] - pos[:, None]).astype(jnp.float32)
        scores = scores + slopes[None, :, None, None] * rel[None, None]
        causal = pos[None, :] <= pos[:, None]
        scores = jnp.where(causal[None, None], scores, jnp.float32(-1e+30))
        probs = jax.nn.softmax(scores, axis=-1)
        out = jnp.einsum('bhqk,bkhd->bqhd', probs, v).reshape(B, S, D_MODEL)
        return jnp.einsum('bsd,ed->bse', out, Wout)

    def _L1_xattn_ref(latents, context, Wq, Wk, Wv, Wo):
        import jax, jax.numpy as jnp
        import numpy as np
        B, Q, D = (8, 64, 512)
        CTX = 512
        H, KV, HD = (16, 4, 96)
        G = H // KV
        b, q_len, _ = latents.shape
        hidden = jnp.concatenate([context, latents], axis=1)
        s_len = hidden.shape[1]
        q = (latents @ Wq.T).reshape(b, q_len, H, HD)
        k = (hidden @ Wk.T).reshape(b, s_len, KV, HD)
        v = (hidden @ Wv.T).reshape(b, s_len, KV, HD)
        q = q.transpose(0, 2, 1, 3).reshape(b, KV, G, q_len, HD)
        k = k.transpose(0, 2, 1, 3)
        v = v.transpose(0, 2, 1, 3)
        scale = 1.0 / jnp.sqrt(jnp.asarray(HD, q.dtype))
        scores = jnp.einsum('bkgqd,bksd->bkgqs', q, k) * scale
        attn = jax.nn.softmax(scores.astype(jnp.float32), axis=-1).astype(q.dtype)
        out = jnp.einsum('bkgqs,bksd->bkgqd', attn, v)
        out = out.reshape(b, H, q_len, HD).transpose(0, 2, 1, 3).reshape(b, q_len, H * HD)
        return out @ Wo.T

    def _L1_ffn_ref(x, A, B, Wr, br):
        import jax, jax.numpy as jnp
        import numpy as np
        ALPHA = 32
        R = 16
        SCALING = ALPHA / R
        H = A.shape[0]
        router_logits = jnp.einsum('bsd,hd->bsh', x, Wr) + br
        scores = H * jax.nn.softmax(router_logits, axis=-1)
        low = jnp.einsum('bsd,hrd->bshr', x, A)
        out = jnp.einsum('bshr,hor,bsh->bso', low, B, scores)
        return SCALING * out
    x = _layernorm(x + _L0_attn_ref(x, L0_attn_Wq, L0_attn_bq, L0_attn_Wk, L0_attn_bk, L0_attn_Wv, L0_attn_bv, L0_attn_Wo, L0_attn_bo), axis=-1)
    x = _layernorm(x + _L0_xattn_ref(x, ctx_4096, ctx_4096), axis=-1)
    x = _layernorm(x + _L0_ffn_ref(x, L0_ffn_base_W, L0_ffn_gate_W, L0_ffn_lora_A, L0_ffn_lora_B), axis=-1)
    x = _layernorm(x + _L1_attn_ref(x, L1_attn_Wqkv, L1_attn_q_ln_w, L1_attn_q_ln_b, L1_attn_k_ln_w, L1_attn_k_ln_b, L1_attn_Wout), axis=-1)
    x = _layernorm(x + _L1_xattn_ref(x, ctx_4096, L1_xattn_Wq, L1_xattn_Wk, L1_xattn_Wv, L1_xattn_Wo), axis=-1)
    x = _layernorm(x + _L1_ffn_ref(x, L1_ffn_A, L1_ffn_B, L1_ffn_Wr, L1_ffn_br), axis=-1)
    return x

_drawn_inputs = setup_inputs


def setup_inputs(seed=0):
    import zlib

    import numpy as np

    out = dict(_drawn_inputs(seed))
    spreads = {'L1_attn_q_ln_w': (1.0, 0.6),
     'L1_attn_q_ln_b': (0.0, 0.8),
     'L1_attn_k_ln_w': (1.0, 0.6),
     'L1_attn_k_ln_b': (0.0, 0.8),
     'L1_ffn_br': (0.0, 0.501)}
    factors = {'L0_attn_bq': 4.389, 'L0_attn_bk': 8.0, 'L1_xattn_Wq': 5.977, 'L1_xattn_Wk': 6.007}
    for name, (base, spread) in spreads.items():
        noise = np.random.default_rng([zlib.crc32(name.encode()), seed]).standard_normal(out[name].shape)
        drawn = base * np.exp(spread * noise) if base else spread * noise
        out[name] = jnp.asarray(drawn.astype(out[name].dtype))
    for name, factor in factors.items():
        out[name] = (out[name] * factor).astype(out[name].dtype)
    return out
```

```python
from contextlib import ExitStack

import numpy as np
import concourse.bass as bass
from concourse import mybir

F32 = mybir.dt.float32
ALU = mybir.AluOpType
ACT = mybir.ActivationFunctionType
AX = mybir.AxisListType.X

P = 128
B, L, D = 8, 128, 512
KT = D // P
SLOTS = 2
TRIPS = B // SLOTS

H, HD = 32, 16
HT = P // HD
CH = 4
NCH = H // CH
XH, XKV, XD = 16, 4, 96
XG = XH // XKV
XT = 2 * L
TOPK = int(2 * np.log(L))
NE, ER = 28, 8
GH = NE // 2
LH, LR = 8, 16
EPS = 1e-5
GONE = -3.0e38
PICKED = -1.0e38

TANK = 4736


def shape_constants():
    t = np.arange(L)
    ck, sk = np.arange(L // 2 + 1), np.arange(1, L // 2)
    cos_e = lambda n, f: np.cos(2 * np.pi * np.outer(n, f) / L)
    sin_e = lambda n, f: np.sin(2 * np.pi * np.outer(n, f) / L)
    same = np.concatenate([cos_e(t, ck), sin_e(t, sk)], 1)
    swap = np.concatenate([sin_e(t, ck), cos_e(t, sk)], 1)
    weight = np.where((ck == 0) | (ck == L // 2), 1.0, 2.0)
    inv1 = np.concatenate([weight * cos_e(t, ck), 2 * cos_e(t, sk)], 1).T / L
    inv2 = np.concatenate([-weight * sin_e(t, ck), 2 * sin_e(t, sk)], 1).T / L
    ctx_even = same.copy()
    ctx_even[L - 1, 0] += L
    odd = np.arange(1, 2 * L, 2)[: L // 2]
    ang = lambda n: 2 * np.pi * np.outer(n, odd) / (2 * L)
    lag_odd = np.concatenate([np.cos(ang(t)), np.sin(ang(t))], 1)
    full = np.arange(2 * L)
    co, so = np.cos(ang(full)), np.sin(ang(full))
    hold = lambda m: np.concatenate([m[: L - 1], m[L - 1:].sum(0, keepdims=True)], 0)
    ctx_odd = np.concatenate([hold(co), hold(so)], 1)
    ctx_odd_swap = np.concatenate([hold(so), hold(co)], 1)
    oute1 = np.concatenate([weight * cos_e(t, ck), 2 * cos_e(t, sk)], 1).T / (2 * L)
    oute2 = np.concatenate([weight * sin_e(t, ck), -2 * sin_e(t, sk)], 1).T / (2 * L)
    outo1 = np.concatenate([2 * np.cos(ang(t)), 2 * np.cos(ang(t))], 1).T / (2 * L)
    outo2 = np.concatenate([2 * np.sin(ang(t)), -2 * np.sin(ang(t))], 1).T / (2 * L)
    tables = [same, ctx_even, swap, ctx_odd, ctx_odd_swap, lag_odd, inv1, inv2, oute1, oute2, outo1, outo2]
    dft = np.stack(tables, 1).astype(np.float32)

    slopes = (1.0 / np.power(2.0, np.arange(1, H + 1, dtype=np.float32) * (8.0 / H))).astype(np.float64)
    rel = t[None, :] - t[:, None]
    causal = rel <= 0
    masks = np.stack([np.eye(P), np.where(causal, 0.0, -1e30), np.where(causal, rel, -1e36)], 1)
    head_rows = (np.arange(P)[:, None] // HD == np.arange(HT)[None, :]).astype(np.float32)
    neg_scale = np.stack([np.full(H, -1.0 / np.sqrt(HD)), -slopes], 0)
    row_head = np.arange(KT)[None, :] * HT + np.arange(P)[:, None] // HD
    q_scale = (1.0 / np.sqrt(HD)) / slopes[row_head]
    small = np.concatenate([head_rows, np.broadcast_to(neg_scale.reshape(1, -1), (P, 2 * H)), q_scale], 1)
    return {
        "dft": dft, "masks": masks.astype(np.float32),
        "small": np.ascontiguousarray(small.astype(np.float32)),
    }, [float(s) for s in slopes]


def nth(trip, per_batch, j):
    return trip * per_batch + j


def decoder(nc, a, out, slopes):
    es = ExitStack()
    with es:
        def sb(name, shape):
            return es.enter_context(nc.sbuf_tensor(name, shape, F32))

        def sem(name):
            return es.enter_context(nc.semaphore(name))

        def per_slot(name):
            return [sem(f"{name}{s}") for s in range(SLOTS)]

        w_qkv0 = sb("w_qkv0", [P, 3, KT, D])
        w_o0 = sb("w_o0", [P, KT, D])
        NG = NE + NE * ER
        w_gl = sb("w_gl", [P, KT, NG])
        w_base = sb("w_base", [P, KT, D])
        w_lb = sb("w_lb", [GH * ER, 2, D])
        w_qkv1 = sb("w_qkv1", [P, KT, 3 * D])
        w_o1 = sb("w_o1", [P, KT, D])
        w_xq = sb("w_xq", [P, KT, XH * XD])
        w_xk = sb("w_xk", [P, KT, XKV * XD])
        w_xv = sb("w_xv", [P, KT, XKV * XD])
        NXO = XH * XD // P
        w_xo = sb("w_xo", [P, NXO, D])
        NL = LH * LR + LH
        w_al = sb("w_al", [P, KT, NL])
        w_bl = sb("w_bl", [P, D])
        bo_row = sb("bo_row", [P, D])
        cols = sb("cols", [P, 7, KT])
        br_row = sb("br_row", [P, LH])
        dft = sb("dft_sb", [P, 12, P])
        masks = sb("masks_sb", [P, 3, P])
        small = sb("small_sb", [P, HT + 2 * H + KT])
        (DX, DC, DCS, DO, DOS, DL, I1, I2, E1, E2, O1, O2) = [dft[:, i, :] for i in range(12)]
        ident, mask0, rel1 = (masks[:, i, :] for i in range(3))
        head_rows = small[:, 0:HT]
        neg_scale = [small[:, HT + H * l:HT + H * (l + 1)] for l in range(2)]
        q_scale = small[:, HT + 2 * H:]
        eps = sb("eps", [P, 2])
        half = sb("half", [P, 2])

        xs = [sb(f"x{s}", [P, D]) for s in range(SLOTS)]
        hidT = [sb(f"hidT{s}", [P, KT, XT]) for s in range(SLOTS)]
        tank = [sb(f"tank{s}", [P, TANK]) for s in range(SLOTS)]
        st = [sb(f"stats{s}", [P, 160]) for s in range(SLOTS)]
        lag2 = [sb(f"lag2_{s}", [P, KT, 8]) for s in range(SLOTS)]
        gate2 = [sb(f"gate2_{s}", [P, 8]) for s in range(SLOTS)]
        gates = [sb(f"gates{s}", [P, 3, NE + 8]) for s in range(SLOTS)]
        bank = [[es.enter_context(nc.psum_tensor(f"bank{s}_{i}", [P, 512], F32)) for i in range(4)]
                for s in range(SLOTS)]

        def view(s, at, n, parts=P):
            return tank[s][0:parts, at:at + n]

        qT = [view(s, 0, 512) for s in range(SLOTS)]
        kT = [view(s, 512, 512) for s in range(SLOTS)]
        kM = [view(s, 1024, 512) for s in range(SLOTS)]
        vv = [view(s, 1536, 512) for s in range(SLOTS)]
        pp = [[view(s, 2048 + 512 * i, 512) for i in range(2)] for s in range(SLOTS)]
        pT = [[view(s, 3072 + 512 * i, 512) for i in range(2)] for s in range(SLOTS)]
        spec = [[view(s, 512 * i, 512) for i in range(4)] for s in range(SLOTS)]
        pr = [[view(s, 2048 + 512 * i, 512) for i in range(2)] for s in range(SLOTS)]
        lagv = [view(s, 3072, 512) for s in range(SLOTS)]
        lage = [view(s, 3584, 512) for s in range(SLOTS)]
        ctx = [view(s, 4096, 512) for s in range(SLOTS)]
        hg = [view(s, 0, NE * ER) for s in range(SLOTS)]
        hgT = [view(s, 512, 2 * P, GH * ER) for s in range(SLOTS)]
        low = [view(s, 0, P) for s in range(SLOTS)]
        lowT = [view(s, 512, P) for s in range(SLOTS)]
        xkT = [view(s, 0, XKV * XT, XD) for s in range(SLOTS)]
        xv = [view(s, 1024, 2 * XKV * XD) for s in range(SLOTS)]
        xq = [view(s, 1792, XG * XD) for s in range(SLOTS)]
        xqT = [view(s, 2176, XG * P, XD) for s in range(SLOTS)]
        xp = [view(s, 2688, XG * XT) for s in range(SLOTS)]
        xpT = [view(s, 3712, XG * XT) for s in range(SLOTS)]
        xo = [view(s, 2688, XG * XD) for s in range(SLOTS)]
        xoT = [view(s, 3712, XG * XD) for s in range(SLOTS)]

        ld_qkv0, ld_c, ld_o0, ld_moe, ld_qkv1, ld_xa, ld_l1 = (
            sem(n) for n in ("ld_qkv0", "ld_c", "ld_o0", "ld_moe", "ld_qkv1", "ld_xa", "ld_l1"))
        loaded = per_slot("loaded")
        stored = per_slot("stored")
        consts_ready = sem("consts_ready")
        dve_step = sem("dve_step")
        pool_step = sem("pool_step")
        qw_ready = sem("qw_ready")
        x_biased = per_slot("x_biased")
        proj_psum = per_slot("proj_psum")
        qkn_ready = per_slot("qkn_ready")
        qk_var = per_slot("qk_var")
        qk_rstd = per_slot("qk_rstd")
        qkT_psum = per_slot("qkT_psum")
        qT_ready = per_slot("qT_ready")
        kT_ready = per_slot("kT_ready")
        v_ready = per_slot("v_ready")
        kM_ready = per_slot("kM_ready")
        scores_psum = per_slot("scores_psum")
        max_ready = per_slot("max_ready")
        probs_ready = per_slot("probs_ready")
        probsT_psum = per_slot("probsT_psum")
        probsT_ready = per_slot("probsT_ready")
        pv_done = per_slot("pv_done")
        attn_ready = per_slot("attn_ready")
        attnT_psum = per_slot("attnT_psum")
        attnT_ready = per_slot("attnT_ready")
        branch_psum = per_slot("branch_psum")
        ln_var = per_slot("ln_var")
        ln_rstd = per_slot("ln_rstd")
        x_ready = per_slot("x_ready")
        xT_psum = per_slot("xT_psum")
        xT_ready = per_slot("xT_ready")
        ctxf_psum = per_slot("ctxf_psum")
        ctxf_ready = per_slot("ctxf_ready")
        xf_psum = per_slot("xf_psum")
        cross_ready = per_slot("cross_ready")
        corr_psum = per_slot("corr_psum")
        lagmax_ready = per_slot("lagmax_ready")
        lagexp_ready = per_slot("lagexp_ready")
        lagw_ready = per_slot("lagw_ready")
        lagwT_psum = per_slot("lagwT_psum")
        lagwT_ready = per_slot("lagwT_ready")
        lagf_psum = per_slot("lagf_psum")
        shift_ready = per_slot("shift_ready")
        gate_psum = per_slot("gate_psum")
        gatemax_ready = per_slot("gatemax_ready")
        gateexp_ready = per_slot("gateexp_ready")
        hg_ready = per_slot("hg_ready")
        hgT_psum = per_slot("hgT_psum")
        hgT_ready = per_slot("hgT_ready")
        xkv_psum = per_slot("xkv_psum")
        xkv_ready = per_slot("xkv_ready")
        xq_psum = per_slot("xq_psum")
        xq_ready = per_slot("xq_ready")
        xqT_psum = per_slot("xqT_psum")
        xqT_ready = per_slot("xqT_ready")
        xs_psum = per_slot("xs_psum")
        xmax_ready = per_slot("xmax_ready")
        xp_ready = per_slot("xp_ready")
        xpT_psum = per_slot("xpT_psum")
        xpT_ready = per_slot("xpT_ready")
        xo_psum = per_slot("xo_psum")
        xo_ready = per_slot("xo_ready")
        xoT_psum = per_slot("xoT_psum")
        xoT_ready = per_slot("xoT_ready")
        route_psum = per_slot("route_psum")
        routemax_ready = per_slot("routemax_ready")
        routeexp_ready = per_slot("routeexp_ready")
        low_ready = per_slot("low_ready")
        lowT_psum = per_slot("lowT_psum")
        lowT_ready = per_slot("lowT_ready")

        BN, MV, RSTD = slice(0, 6), slice(6, 8), slice(8, 9)
        QKBN, QKMV, QKRSTD = slice(12, 24), slice(24, 28), slice(28, 30)
        NEGMAX, ROWMAX, ROWSUM = slice(32, 64), slice(64, 96), slice(96, 128)
        LAGNEG, LAGSUM = slice(128, 132), slice(132, 136)
        TOP2 = slice(136, 144)
        ONE_A, ONE_B, ONE_C = slice(144, 145), slice(145, 146), slice(146, 147)
        EIGHT_A, EIGHT_B = slice(148, 156), slice(148, 156)

        block = es.enter_context(nc.Block())
        both = range(SLOTS)

        @block.sync
        def _(sp):
            def load(b, s):
                sp.dma_start(xs[s][:, :], a["x"][b]).then_inc(loaded[s], 16)
                sp.dma_start(hidT[s][:, :, L:XT], a["xT"][b]).then_inc(loaded[s], 16)
                sp.dma_start(ctx[s], a["ctx"][b]).then_inc(loaded[s], 16)
                sp.dma_start(hidT[s][:, :, 0:L], a["ctxT"][b]).then_inc(loaded[s], 16)

            for s in both:
                load(s, s)
            for i in range(3):
                sp.dma_start(w_qkv0[:, i], a["w_qkv0"][:, i]).then_inc(ld_qkv0, 16)
            sp.dma_start(cols[:, :, :], a["cols"]).then_inc(ld_c, 16)
            sp.dma_start(small[:, :], a["small"]).then_inc(ld_c, 16)
            sp.dma_start(masks[:, :, :], a["masks"]).then_inc(ld_c, 16)
            sp.dma_start(dft[:, :, :], a["dft"]).then_inc(ld_c, 16)
            sp.dma_start(bo_row[:, :], a["bo"].partition_broadcast(P)).then_inc(ld_c, 16)
            sp.dma_start(br_row[:, :], a["br"].partition_broadcast(P)).then_inc(ld_c, 16)
            sp.dma_start(w_o0[:, :, :], a["w_o0"]).then_inc(ld_o0, 16)
            sp.dma_start(w_gl[:, :, :], a["w_gl"]).then_inc(ld_moe, 16)
            sp.dma_start(w_base[:, :, :], a["w_base"]).then_inc(ld_moe, 16)
            sp.dma_start(w_lb[:, :, :], a["w_lb"]).then_inc(ld_moe, 16)
            sp.dma_start(w_qkv1[:, :, :], a["w_qkv1"]).then_inc(ld_qkv1, 16)
            sp.dma_start(w_o1[:, :, :], a["w_o1"]).then_inc(ld_qkv1, 16)
            sp.dma_start(w_xk[:, :, :], a["w_xk"]).then_inc(ld_xa, 16)
            sp.dma_start(w_xv[:, :, :], a["w_xv"]).then_inc(ld_xa, 16)
            sp.dma_start(w_xq[:, :, :], a["w_xq"]).then_inc(ld_xa, 16)
            sp.dma_start(w_xo[:, :, :], a["w_xo"]).then_inc(ld_xa, 16)
            sp.dma_start(w_al[:, :, :], a["w_al"]).then_inc(ld_l1, 16)
            sp.dma_start(w_bl[:, :], a["w_bl"]).then_inc(ld_l1, 16)
            with sp.Fori(0, TRIPS - 1) as trip:
                for s in both:
                    sp.wait_ge(x_ready[s], nth(trip, 6, 6))
                    sp.dma_start(out[bass.ds(trip * SLOTS + s, 1)].rearrange("b p d -> (b p) d"), xs[s][:, :]).then_inc(stored[s], 16)
                    sp.wait_ge(stored[s], nth(trip, 16, 16))
                    nb = trip * SLOTS + (SLOTS + s)
                    sp.dma_start(xs[s][:, :], a["x"][bass.ds(nb, 1)].rearrange("b p d -> (b p) d")).then_inc(loaded[s], 16)
                    sp.dma_start(hidT[s][:, :, L:XT], a["xT"][bass.ds(nb, 1)].rearrange("b p k t -> (b p) k t")).then_inc(loaded[s], 16)
                    sp.dma_start(ctx[s], a["ctx"][bass.ds(nb, 1)].rearrange("b p d -> (b p) d")).then_inc(loaded[s], 16)
                    sp.dma_start(hidT[s][:, :, 0:L], a["ctxT"][bass.ds(nb, 1)].rearrange("b p k t -> (b p) k t")).then_inc(loaded[s], 16)
            for s in both:
                sp.wait_ge(x_ready[s], 6 * TRIPS)
                sp.dma_start(out[B - SLOTS + s], xs[s][:, :]).then_inc(stored[s], 16)
            for s in both:
                sp.wait_ge(stored[s], 16 * TRIPS)

        @block.tensor
        def _(pe):
            mm = nc.tensor.matmul

            def q_k_v_first(trip, s):
                pe.wait_ge(loaded[s], nth(trip, 64, 64))
                if s == 0:
                    pe.wait_ge(ld_qkv0, 48)
                    pe.wait_ge(ld_c, 96)
                xT = hidT[s][:, :, L:XT]
                for i in range(2):
                    for m in range(KT):
                        for k in range(KT):
                            ins = mm(bank[s][i][:, m * P:(m + 1) * P], w_qkv0[:, i, k, m * P:(m + 1) * P], xT[:, k, :],
                                     start=k == 0, stop=k == KT - 1)
                    ins.then_inc(proj_psum[s], 1)
                for k in range(KT):
                    ins = mm(bank[s][2][:, :], xT[:, k, :], w_qkv0[:, 2, k, :], start=k == 0, stop=k == KT - 1)
                ins.then_inc(proj_psum[s], 1)

            def q_k_v_second(trip, s):
                if s == 0:
                    pe.wait_ge(ld_qkv1, 32)
                pe.wait_ge(xT_ready[s], nth(trip, 4, 2))
                for i in range(3):
                    if i == 2:
                        pass
                    for k in range(KT):
                        ins = mm(bank[s][i][:, :], hidT[s][:, k, L:XT], w_qkv1[:, k, i * D:(i + 1) * D],
                                 start=k == 0, stop=k == KT - 1)
                    ins.then_inc(proj_psum[s], 1)

            def normed_to_features(trip, s):
                pe.wait_ge(qkn_ready[s], nth(trip, 1, 1))
                for i in range(2):
                    for m in range(KT):
                        ins = nc.tensor.transpose(bank[s][i][:, m * P:(m + 1) * P], pp[s][i][:, m * P:(m + 1) * P], ident)
                    ins.then_inc(qkT_psum[s], 1)

            def scores(trip, s, l, c):
                pe.wait_ge(kM_ready[s], nth(trip, 2 * NCH, l * NCH + c + 1))
                if c == 0:
                    pe.wait_ge(qT_ready[s], nth(trip, 2, l + 1))
                if c >= 2:
                    pe.wait_ge(max_ready[s], nth(trip, 2 * NCH, l * NCH + c - 1))
                m = c * CH // HT
                mm(bank[s][c % 2][:, :], qT[s][:, m * P:(m + 1) * P], kM[s], start=True, stop=True
                   ).then_inc(scores_psum[s], 1)

            def probs_transpose(trip, s, l, c):
                pe.wait_ge(probs_ready[s], nth(trip, 2 * NCH, l * NCH + c + 1))
                if c == 0:
                    pe.wait_ge(v_ready[s], nth(trip, 2, l + 1))
                else:
                    pe.wait_ge(probsT_ready[s], nth(trip, 2 * NCH, l * NCH + c))
                for j in range(CH):
                    ins = nc.tensor.transpose(bank[s][2][:, j * P:(j + 1) * P], pp[s][c % 2][:, j * P:(j + 1) * P], ident)
                ins.then_inc(probsT_psum[s], 1)

            def weigh_values(trip, s, l, c):
                pe.wait_ge(probsT_ready[s], nth(trip, 2 * NCH, l * NCH + c + 1))
                for j in range(CH):
                    h = c * CH + j
                    ins = mm(bank[s][3][:, h * HD:(h + 1) * HD], pT[s][c % 2][:, j * P:(j + 1) * P],
                             vv[s][:, h * HD:(h + 1) * HD], start=True, stop=True)
                ins.then_inc(pv_done[s], 1)

            def attention(trip, l):
                for c in range(NCH + 2):
                    for s in both:
                        if c < NCH:
                            scores(trip, s, l, c)
                    for s in both:
                        if 1 <= c <= NCH:
                            probs_transpose(trip, s, l, c - 1)
                    for s in both:
                        if c >= 2:
                            weigh_values(trip, s, l, c - 2)

            def heads_to_features(trip, s, l):
                pe.wait_ge(attn_ready[s], nth(trip, 2, l + 1))
                for m in range(KT):
                    ins = nc.tensor.transpose(bank[s][2][:, m * P:(m + 1) * P], pp[s][0][:, m * P:(m + 1) * P], ident)
                ins.then_inc(attnT_psum[s], 1)

            def attention_out(trip, s, l):
                if l == 0 and s == 0:
                    pe.wait_ge(ld_o0, 16)
                pe.wait_ge(attnT_ready[s], nth(trip, 2, l + 1))
                w = (w_o0, w_o1)[l]
                for k in range(KT):
                    ins = mm(bank[s][0][:, :], pT[s][0][:, k * P:(k + 1) * P], w[:, k, :], start=k == 0, stop=k == KT - 1)
                ins.then_inc(branch_psum[s], 1)

            def x_to_features(trip, s, n, layer):
                pe.wait_ge(x_ready[s], nth(trip, 6, layer))
                for m in range(KT):
                    ins = nc.tensor.transpose(bank[s][2][:, m * P:(m + 1) * P], xs[s][:, m * P:(m + 1) * P], ident)
                ins.then_inc(xT_psum[s], 1)

            def context_spectra(trip, s, parts):
                for i in parts:
                    if i == 3:
                        pe.wait_ge(ctxf_ready[s], nth(trip, 4, 1))
                    mm(bank[s][1 + i % 3][:, :], (DC, DCS, DO, DOS)[i], ctx[s], start=True, stop=True
                       ).then_inc(ctxf_psum[s], 1)

            def x_spectrum(trip, s):
                pe.wait_ge(x_ready[s], nth(trip, 6, 1))
                mm(bank[s][0][:, :], DX, xs[s][:, :], start=True, stop=True).then_inc(xf_psum[s], 1)

            def correlation(trip, s):
                pe.wait_ge(cross_ready[s], nth(trip, 1, 1))
                pe.wait_ge(ctxf_ready[s], nth(trip, 4, 2))
                for m in range(KT):
                    mm(bank[s][2][:, m * P:(m + 1) * P], pr[s][0][:, m * P:(m + 1) * P], I1, start=True, stop=False)
                    ins = mm(bank[s][2][:, m * P:(m + 1) * P], pr[s][1][:, m * P:(m + 1) * P], I2, start=False, stop=True)
                ins.then_inc(corr_psum[s], 1)

            def lag_weights_to_lags(trip, s):
                pe.wait_ge(lagw_ready[s], nth(trip, 1, 1))
                for m in range(KT):
                    ins = nc.tensor.transpose(bank[s][0][:, m * P:(m + 1) * P], pr[s][0][:, m * P:(m + 1) * P], ident)
                ins.then_inc(lagwT_psum[s], 1)

            def lag_spectrum(trip, s):
                pe.wait_ge(lagwT_ready[s], nth(trip, 1, 1))
                pe.wait_ge(ctxf_ready[s], nth(trip, 4, 4))
                mm(bank[s][3][:, :], DX, pr[s][1], start=True, stop=True).then_inc(lagf_psum[s], 1)
                mm(bank[s][0][:, :], DL, pr[s][1], start=True, stop=True).then_inc(lagf_psum[s], 1)

            def shifted_sum(trip, s):
                for i, (table, src) in enumerate(((E1, lagv), (E2, lage), (O1, None), (O2, None))):
                    if i % 2 == 0:
                        pe.wait_ge(shift_ready[s], nth(trip, 2, i // 2 + 1))
                    rhs = src[s] if i < 2 else pr[s][i - 2]
                    ins = mm(bank[s][1][:, :], table, rhs, start=i == 0, stop=i == 3)
                ins.then_inc(branch_psum[s], 1)

            def gates_and_base(trip, s):
                if s == 0:
                    pe.wait_ge(ld_moe, 48)
                pe.wait_ge(xT_ready[s], nth(trip, 4, 1))
                for k in range(KT):
                    ins = mm(bank[s][0][:, 0:NG], hidT[s][:, k, L:XT], w_gl[:, k, :], start=k == 0, stop=k == KT - 1)
                ins.then_inc(gate_psum[s], 1)
                for k in range(KT):
                    mm(bank[s][1][:, :], hidT[s][:, k, L:XT], w_base[:, k, :], start=k == 0, stop=False)

            def gated_to_rank(trip, s):
                pe.wait_ge(hg_ready[s], nth(trip, 1, 1))
                n = GH * ER
                for i in range(2):
                    ins = nc.tensor.transpose(bank[s][2][0:n, i * P:(i + 1) * P], hg[s][:, i * n:(i + 1) * n], ident)
                ins.then_inc(hgT_psum[s], 1)

            def experts_out(trip, s):
                pe.wait_ge(hgT_ready[s], nth(trip, 1, 1))
                for i in range(2):
                    ins = mm(bank[s][1][:, :], hgT[s][:, i * P:(i + 1) * P], w_lb[:, i, :], start=False, stop=i == 1)
                ins.then_inc(branch_psum[s], 1)

            def cross_keys_values(trip, s):
                if s == 0:
                    pe.wait_ge(ld_xa, 64)
                pe.wait_ge(xT_ready[s], nth(trip, 4, 3))
                for g in range(XKV):
                    for k in range(KT):
                        ins = mm(bank[s][g // 2][0:XD, (g % 2) * XT:(g % 2 + 1) * XT], w_xk[:, k, g * XD:(g + 1) * XD],
                                 hidT[s][:, k, :], start=k == 0, stop=k == KT - 1)
                    if g % 2:
                        ins.then_inc(xkv_psum[s], 1)
                for t in range(2):
                    for k in range(KT):
                        ins = mm(bank[s][2 + t][:, 0:XKV * XD], hidT[s][:, k, t * L:(t + 1) * L], w_xv[:, k, :],
                                 start=k == 0, stop=k == KT - 1)
                    ins.then_inc(xkv_psum[s], 1)

            def cross_q(trip, s, g):
                if g == 0:
                    pe.wait_ge(xkv_ready[s], nth(trip, 4, 3))
                else:
                    pe.wait_ge(xqT_ready[s], nth(trip, 4, g))
                for k in range(KT):
                    ins = mm(bank[s][2][:, 0:XG * XD], hidT[s][:, k, L:XT], w_xq[:, k, g * XG * XD:(g + 1) * XG * XD],
                             start=k == 0, stop=k == KT - 1)
                ins.then_inc(xq_psum[s], 1)

            def cross_qT(trip, s, g):
                pe.wait_ge(xq_ready[s], nth(trip, 4, g + 1))
                for j in range(XG):
                    ins = nc.tensor.transpose(bank[s][2][0:XD, j * P:(j + 1) * P], xq[s][:, j * XD:(j + 1) * XD], ident)
                ins.then_inc(xqT_psum[s], 1)

            def cross_scores(trip, s, g):
                pe.wait_ge(xqT_ready[s], nth(trip, 4, g + 1))
                if g == 0:
                    pe.wait_ge(xkv_ready[s], nth(trip, 4, 2))
                for i in range(2):
                    if g > 0 and i == 1:
                        pe.wait_ge(xoT_ready[s], nth(trip, 4, g))
                    for j in range(2):
                        ins = mm(bank[s][i][:, j * XT:(j + 1) * XT], xqT[s][:, (2 * i + j) * P:(2 * i + j + 1) * P],
                                 xkT[s][:, g * XT:(g + 1) * XT], start=True, stop=True)
                    ins.then_inc(xs_psum[s], 1)

            def cross_probsT(trip, s, g):
                for i in range(2):
                    pe.wait_ge(xp_ready[s], nth(trip, 8, 2 * g + i + 1))
                    for j in range(4):
                        at = (4 * i + j) * P
                        ins = nc.tensor.transpose(bank[s][i][:, j * P:(j + 1) * P], xp[s][:, at:at + P], ident)
                    ins.then_inc(xpT_psum[s], 1)

            def cross_values(trip, s, g):
                pe.wait_ge(xpT_ready[s], nth(trip, 8, 2 * g + 2))
                if g == 0:
                    pe.wait_ge(xkv_ready[s], nth(trip, 4, 4))
                for j in range(XG):
                    for t in range(2):
                        at = (2 * j + t) * P
                        ins = mm(bank[s][0][:, j * XD:(j + 1) * XD], xpT[s][:, at:at + P],
                                 xv[s][:, t * XKV * XD + g * XD:t * XKV * XD + (g + 1) * XD], start=t == 0, stop=t == 1)
                ins.then_inc(xo_psum[s], 1)

            def cross_oT(trip, s, g):
                pe.wait_ge(xo_ready[s], nth(trip, 4, g + 1))
                for m in range(XG * XD // P):
                    ins = nc.tensor.transpose(bank[s][1][:, m * P:(m + 1) * P], xo[s][:, m * P:(m + 1) * P], ident)
                ins.then_inc(xoT_psum[s], 1)

            def cross_out(trip, s, g):
                pe.wait_ge(xoT_ready[s], nth(trip, 4, g + 1))
                n = XG * XD // P
                for m in range(n):
                    ins = mm(bank[s][3][:, :], xoT[s][:, m * P:(m + 1) * P], w_xo[:, g * n + m, :],
                             start=(g == 0 and m == 0), stop=(g == XKV - 1 and m == n - 1))
                if g == XKV - 1:
                    ins.then_inc(branch_psum[s], 1)

            def routes_and_low(trip, s):
                if s == 0:
                    pe.wait_ge(ld_l1, 32)
                pe.wait_ge(xT_ready[s], nth(trip, 4, 4))
                for k in range(KT):
                    ins = mm(bank[s][0][:, 0:NL], hidT[s][:, k, L:XT], w_al[:, k, :], start=k == 0, stop=k == KT - 1)
                ins.then_inc(route_psum[s], 1)

            def low_to_rank(trip, s):
                pe.wait_ge(low_ready[s], nth(trip, 1, 1))
                nc.tensor.transpose(bank[s][2][:, 0:P], low[s], ident).then_inc(lowT_psum[s], 1)

            def heads_out(trip, s):
                pe.wait_ge(lowT_ready[s], nth(trip, 1, 1))
                mm(bank[s][3][:, :], lowT[s], w_bl[:, :], start=True, stop=True).then_inc(branch_psum[s], 1)

            with pe.Fori(0, TRIPS) as trip:
                for s in both:
                    q_k_v_first(trip, s)
                attention(trip, 0)
                for s in both:
                    heads_to_features(trip, s, 0)
                for s in both:
                    attention_out(trip, s, 0)
                for s in both:
                    context_spectra(trip, s, (0, 1, 2))
                for s in both:
                    context_spectra(trip, s, (3,))
                for s in both:
                    x_spectrum(trip, s)
                for step in (correlation, lag_weights_to_lags, lag_spectrum, shifted_sum):
                    for s in both:
                        step(trip, s)
                for s in both:
                    x_to_features(trip, s, 1, 2)
                for step in (gates_and_base, gated_to_rank, experts_out):
                    for s in both:
                        step(trip, s)
                for s in both:
                    x_to_features(trip, s, 2, 3)
                for s in both:
                    q_k_v_second(trip, s)
                for s in both:
                    normed_to_features(trip, s)
                attention(trip, 1)
                for s in both:
                    heads_to_features(trip, s, 1)
                for s in both:
                    attention_out(trip, s, 1)
                for s in both:
                    x_to_features(trip, s, 3, 4)
                for s in both:
                    cross_keys_values(trip, s)
                for s in both:
                    cross_q(trip, s, 0)
                for s in both:
                    cross_qT(trip, s, 0)
                for g in range(XKV):
                    for s in both:
                        cross_scores(trip, s, g)
                    if g + 1 < XKV:
                        for s in both:
                            cross_q(trip, s, g + 1)
                    if g > 0:
                        for s in both:
                            cross_out(trip, s, g - 1)
                    for s in both:
                        cross_probsT(trip, s, g)
                    if g + 1 < XKV:
                        for s in both:
                            cross_qT(trip, s, g + 1)
                    for s in both:
                        cross_values(trip, s, g)
                    for s in both:
                        cross_oT(trip, s, g)
                for s in both:
                    cross_out(trip, s, XKV - 1)
                for s in both:
                    x_to_features(trip, s, 4, 5)
                for step in (routes_and_low, low_to_rank, heads_out):
                    for s in both:
                        step(trip, s)

        @block.scalar
        def _(act):
            av = nc.scalar.activation

            def v_first(trip, s):
                act.wait_ge(proj_psum[s], nth(trip, 6, 3))
                nc.scalar.copy(vv[s], bank[s][2][:, :]).then_inc(v_ready[s], 1)

            def probs(trip, s, l, c):
                act.wait_ge(max_ready[s], nth(trip, 2 * NCH, l * NCH + c + 1))
                for j in range(CH):
                    h = c * CH + j
                    blockp = pp[s][c % 2][:, j * P:(j + 1) * P]
                    ins = av(blockp, blockp, ACT.Exp, bias=st[s][:, NEGMAX.start + h:NEGMAX.start + h + 1],
                             scale=(HD ** -0.5 if l == 0 else slopes[h]),
                             accum_out=st[s][:, ROWSUM.start + h:ROWSUM.start + h + 1])
                ins.then_inc(probs_ready[s], 1)

            def context_spectra(trip, s, parts):
                for i in parts:
                    act.wait_ge(ctxf_psum[s], nth(trip, 4, i + 1))
                    nc.scalar.copy(spec[s][i], bank[s][1 + i % 3][:, :]).then_inc(ctxf_ready[s], 1)

            def lag_exp(trip, s):
                act.wait_ge(lagmax_ready[s], nth(trip, 1, 1))
                for m in range(KT):
                    ins = av(lage[s][:, m * P:(m + 1) * P], bank[s][2][:, m * P:(m + 1) * P], ACT.Exp,
                             bias=st[s][:, LAGNEG.start + m:LAGNEG.start + m + 1], scale=1.0)
                ins.then_inc(lagexp_ready[s], 1)

            def lag_weightsT(trip, s):
                act.wait_ge(lagwT_psum[s], nth(trip, 1, 1))
                nc.scalar.copy(pr[s][1], bank[s][0][:, :]).then_inc(lagwT_ready[s], 1)

            def xT(trip, s, n):
                act.wait_ge(xT_psum[s], nth(trip, 4, n))
                nc.scalar.copy(hidT[s][:, :, L:XT], bank[s][2][:, :].rearrange("p (k t) -> p k t", k=KT)
                               ).then_inc(xT_ready[s], 1)

            def gate_exp(trip, s):
                act.wait_ge(gatemax_ready[s], nth(trip, 1, 1))
                av(gates[s][:, 2, 0:NE], gates[s][:, 0, 0:NE], ACT.Exp, bias=st[s][:, ONE_A], scale=1.0
                   ).then_inc(gateexp_ready[s], 1)

            def gatedT(trip, s):
                act.wait_ge(hgT_psum[s], nth(trip, 1, 1))
                nc.scalar.copy(hgT[s], bank[s][2][0:GH * ER, 0:2 * P]).then_inc(hgT_ready[s], 1)

            def cross_keys_values(trip, s):
                for i in range(2):
                    act.wait_ge(xkv_psum[s], nth(trip, 4, i + 1))
                    nc.scalar.copy(xkT[s][:, 2 * i * XT:2 * (i + 1) * XT], bank[s][i][0:XD, :]).then_inc(xkv_ready[s], 1)
                for t in range(2):
                    act.wait_ge(xkv_psum[s], nth(trip, 4, t + 3))
                    n = XKV * XD
                    nc.scalar.copy(xv[s][:, t * n:(t + 1) * n], bank[s][2 + t][:, 0:n]).then_inc(xkv_ready[s], 1)

            def cross_q(trip, s, g):
                act.wait_ge(xq_psum[s], nth(trip, 4, g + 1))
                nc.scalar.copy(xq[s], bank[s][2][:, 0:XG * XD]).then_inc(xq_ready[s], 1)

            def cross_probs(trip, s, g):
                for i in range(2):
                    act.wait_ge(xmax_ready[s], nth(trip, 8, 2 * g + i + 1))
                    for j in range(2):
                        h = 2 * i + j
                        ins = av(xp[s][:, h * XT:(h + 1) * XT], bank[s][i][:, j * XT:(j + 1) * XT], ACT.Exp,
                                 bias=st[s][:, NEGMAX.start + h:NEGMAX.start + h + 1], scale=XD ** -0.5,
                                 accum_out=st[s][:, ROWSUM.start + h:ROWSUM.start + h + 1])
                    ins.then_inc(xp_ready[s], 1)

            def cross_oT(trip, s, g):
                act.wait_ge(xoT_psum[s], nth(trip, 4, g + 1))
                nc.scalar.copy(xoT[s], bank[s][1][:, 0:XG * XD]).then_inc(xoT_ready[s], 1)

            def route_exp(trip, s):
                act.wait_ge(routemax_ready[s], nth(trip, 1, 1))
                av(st[s][:, EIGHT_B], st[s][:, EIGHT_A], ACT.Exp, bias=st[s][:, ONE_A], scale=1.0,
                   accum_out=st[s][:, ONE_B]).then_inc(routeexp_ready[s], 1)

            def lowT_copy(trip, s):
                act.wait_ge(lowT_psum[s], nth(trip, 1, 1))
                nc.scalar.copy(lowT[s], bank[s][2][:, 0:P]).then_inc(lowT_ready[s], 1)

            with act.Fori(0, TRIPS) as trip:
                for s in both:
                    v_first(trip, s)
                for c in range(NCH):
                    for s in both:
                        probs(trip, s, 0, c)
                for s in both:
                    context_spectra(trip, s, (0, 1, 2))
                for s in both:
                    context_spectra(trip, s, (3,))
                for step in (lag_exp, lag_weightsT):
                    for s in both:
                        step(trip, s)
                for s in both:
                    xT(trip, s, 1)
                for step in (gate_exp, gatedT):
                    for s in both:
                        step(trip, s)
                for s in both:
                    xT(trip, s, 2)
                for c in range(NCH):
                    for s in both:
                        probs(trip, s, 1, c)
                for s in both:
                    xT(trip, s, 3)
                for s in both:
                    cross_keys_values(trip, s)
                for s in both:
                    cross_q(trip, s, 0)
                for g in range(XKV):
                    for s in both:
                        cross_probs(trip, s, g)
                    if g + 1 < XKV:
                        for s in both:
                            cross_q(trip, s, g + 1)
                    for s in both:
                        cross_oT(trip, s, g)
                for s in both:
                    xT(trip, s, 4)
                for step in (route_exp, lowT_copy):
                    for s in both:
                        step(trip, s)

        @block.gpsimd
        def _(pool):

            nc.gpsimd.memset(eps[:, :], EPS).then_inc(consts_ready, 1)
            nc.gpsimd.memset(half[:, :], -0.5).then_inc(consts_ready, 1)
            for s in both:
                nc.gpsimd.memset(lag2[s][:, :, :], GONE).then_inc(consts_ready, 1)
                nc.gpsimd.memset(gate2[s][:, :], GONE).then_inc(consts_ready, 1)
                nc.gpsimd.memset(gates[s][:, :, :], GONE).then_inc(consts_ready, 1)
            pool.wait_ge(consts_ready, 2 + 3 * SLOTS)
            pool.wait_ge(ld_c, 96)

            def mask_keys(trip, s, l, c):
                if c == 0:
                    pool.wait_ge(kT_ready[s], nth(trip, 2, l + 1))
                else:
                    pool.wait_ge(scores_psum[s], nth(trip, 2 * NCH, l * NCH + c))
                m, j = c * CH // HT, c * CH % HT
                nc.gpsimd.tensor_tensor(kM[s].rearrange("p (h t) -> p h t", h=CH),
                                        kT[s][:, m * P:(m + 1) * P].unsqueeze(1).broadcast_to([P, CH, P]),
                                        head_rows[:, j:j + CH].unsqueeze(2).broadcast_to([P, CH, P]),
                                        ALU.mult).then_inc(kM_ready[s], 1)

            def rstd(trip, s, n):
                pool.wait_ge(ln_var[s], nth(trip, 6, n))
                nc.gpsimd.tensor_tensor(st[s][:, RSTD], st[s][:, MV][:, 1:2], half[:, 0:1], ALU.pow
                                        ).then_inc(ln_rstd[s], 1)

            def rstd_qk(trip, s):
                pool.wait_ge(qk_var[s], nth(trip, 1, 1))
                nc.gpsimd.tensor_tensor(st[s][:, QKRSTD], st[s][:, QKMV].rearrange("p (a b) -> p a b", b=2)[:, :, 1],
                                        half[:, 0:2], ALU.pow).then_inc(qk_rstd[s], 1)

            def bias_x(trip, s):
                pool.wait_ge(loaded[s], nth(trip, 64, 64))
                nc.gpsimd.tensor_tensor(xs[s][:, :], xs[s][:, :], bo_row[:, :], ALU.add).then_inc(x_biased[s], 1)

            with pool.Fori(0, TRIPS) as trip:
                for s in both:
                    bias_x(trip, s)
                for l in range(2):
                    if l == 1:
                        for s in both:
                            rstd_qk(trip, s)
                    for c in range(NCH):
                        for s in both:
                            mask_keys(trip, s, l, c)
                    for n in ((1, 2, 3) if l == 0 else (4, 5, 6)):
                        for s in both:
                            rstd(trip, s, n)

        @block.vector
        def _(dve):
            DVE_STEPS = 144
            v = nc.vector
            taken = [0]

            def steps_done(trip, ins):
                taken[0] += 1
                ins.then_inc(dve_step, 1)
                dve.wait_ge(dve_step, nth(trip, DVE_STEPS, taken[0]))

            def hold():
                dve.nop(nofuse=True)

            def tiles(ap, k=KT):
                return ap.rearrange("p (k t) -> p k t", k=k)

            def qT_kT_first(trip, s):
                for i, (dst, ready) in enumerate(((qT, qT_ready), (kT, kT_ready))):
                    dve.wait_ge(proj_psum[s], nth(trip, 6, i + 1))
                    v.tensor_tensor(tiles(dst[s]), tiles(bank[s][i][:, :]),
                                    cols[:, i, :].unsqueeze(2).broadcast_to([P, KT, P]), ALU.add).then_inc(ready[s], 1)

            def clip_norm(trip, s):
                for i in range(2):
                    dve.wait_ge(proj_psum[s], nth(trip, 6, 4 + i))
                    steps_done(trip, v.tensor_scalar(pp[s][i], bank[s][i][:, :], -8.0, 8.0, ALU.max, ALU.min))
                    bn = st[s][:, QKBN.start + 6 * i:QKBN.start + 6 * i + 6]
                    mv = st[s][:, QKMV.start + 2 * i:QKMV.start + 2 * i + 2]
                    steps_done(trip, v.bn_stats(bn, pp[s][i]))
                    hold()
                    steps_done(trip, v.bn_aggr(mv, bn))
                var = st[s][:, QKMV].rearrange("p (a b) -> p a b", b=2)[:, :, 1]
                v.tensor_scalar(var, var, EPS, None, ALU.add).then_inc(qk_var[s], 1)
                dve.wait_ge(proj_psum[s], nth(trip, 6, 6))
                v.tensor_scalar(vv[s], bank[s][2][:, :], -8.0, 8.0, ALU.max, ALU.min).then_inc(v_ready[s], 1)

            def apply_norm(trip, s):
                dve.wait_ge(qk_rstd[s], nth(trip, 1, 1))
                for i in range(2):
                    ins = v.tensor_scalar(pp[s][i], pp[s][i], st[s][:, QKMV.start + 2 * i:QKMV.start + 2 * i + 1],
                                          st[s][:, QKRSTD.start + i:QKRSTD.start + i + 1], ALU.subtract, ALU.mult)
                ins.then_inc(qkn_ready[s], 1)

            def qT_kT_second(trip, s):
                for i, (dst, ready) in enumerate(((qT, qT_ready), (kT, kT_ready))):
                    dve.wait_ge(qkT_psum[s], nth(trip, 2, i + 1))
                    for m in range(KT):
                        ins = v.tensor_scalar(dst[s][:, m * P:(m + 1) * P], bank[s][i][:, m * P:(m + 1) * P],
                                              cols[:, 3 + 2 * i, m:m + 1], cols[:, 4 + 2 * i, m:m + 1], ALU.mult, ALU.add)
                    ins.then_inc(ready[s], 1)

            def maxima(trip, s, l, c):
                dve.wait_ge(scores_psum[s], nth(trip, 2 * NCH, l * NCH + c + 1))
                if c >= 2:
                    dve.wait_ge(probsT_psum[s], nth(trip, 2 * NCH, l * NCH + c - 1))
                hold()
                for j in range(CH):
                    h = c * CH + j
                    ins = v.tensor_tensor_reduce(pp[s][c % 2][:, j * P:(j + 1) * P], bank[s][c % 2][:, j * P:(j + 1) * P],
                                                 (mask0, rel1)[l], 1.0, GONE, ALU.add, ALU.max,
                                                 st[s][:, ROWMAX.start + h:ROWMAX.start + h + 1])
                steps_done(trip, ins)
                n = slice(NEGMAX.start + c * CH, NEGMAX.start + (c + 1) * CH)
                r = slice(ROWMAX.start + c * CH, ROWMAX.start + (c + 1) * CH)
                v.tensor_tensor(st[s][:, n], st[s][:, r], neg_scale[l][:, c * CH:(c + 1) * CH], ALU.mult
                                ).then_inc(max_ready[s], 1)

            def probsT(trip, s, l, c):
                dve.wait_ge(probsT_psum[s], nth(trip, 2 * NCH, l * NCH + c + 1))
                if c >= 2:
                    dve.wait_ge(pv_done[s], nth(trip, 2 * NCH, l * NCH + c - 1))
                v.tensor_copy(pT[s][c % 2], bank[s][2][:, :]).then_inc(probsT_ready[s], 1)

            def heads(trip, s, l):
                dve.wait_ge(pv_done[s], nth(trip, 2 * NCH, (l + 1) * NCH))
                rows = st[s][:, ROWSUM]
                steps_done(trip, v.reciprocal(rows, rows))
                v.tensor_tensor(pp[s][0].rearrange("p (h d) -> p h d", h=H), bank[s][3][:, :].rearrange("p (h d) -> p h d", h=H),
                                rows.unsqueeze(2).broadcast_to([P, H, HD]), ALU.mult).then_inc(attn_ready[s], 1)

            def headsT(trip, s, l):
                dve.wait_ge(attnT_psum[s], nth(trip, 2, l + 1))
                if l == 0:
                    v.tensor_tensor(tiles(pT[s][0]), tiles(bank[s][2][:, :]),
                                    cols[:, 2, :].unsqueeze(2).broadcast_to([P, KT, P]), ALU.add).then_inc(attnT_ready[s], 1)
                else:
                    v.tensor_copy(pT[s][0], bank[s][2][:, :]).then_inc(attnT_ready[s], 1)

            def residual(trip, s, n, at):
                dve.wait_ge(branch_psum[s], nth(trip, 6, n))
                if n == 1:
                    dve.wait_ge(x_biased[s], nth(trip, 1, 1))
                steps_done(trip, v.tensor_tensor(xs[s][:, :], bank[s][at][:, :], xs[s][:, :], ALU.add))
                steps_done(trip, v.bn_stats(st[s][:, BN], xs[s][:, :]))
                hold()
                steps_done(trip, v.bn_aggr(st[s][:, MV], st[s][:, BN]))
                var = st[s][:, MV][:, 1:2]
                v.tensor_scalar(var, var, EPS, None, ALU.add).then_inc(ln_var[s], 1)

            def norm_x(trip, s, n):
                dve.wait_ge(ln_rstd[s], nth(trip, 6, n))
                v.tensor_scalar(xs[s][:, :], xs[s][:, :], st[s][:, MV][:, 0:1], st[s][:, RSTD], ALU.subtract, ALU.mult
                                ).then_inc(x_ready[s], 1)

            def cross_products(trip, s):
                dve.wait_ge(xf_psum[s], nth(trip, 1, 1))
                dve.wait_ge(ctxf_ready[s], nth(trip, 4, 2))
                v.tensor_tensor(pr[s][0], bank[s][0][:, :], spec[s][0], ALU.mult)
                v.tensor_tensor(pr[s][1], bank[s][0][:, :], spec[s][1], ALU.mult).then_inc(cross_ready[s], 1)

            def top_lags(trip, s):
                dve.wait_ge(corr_psum[s], nth(trip, 1, 1))
                hold()
                m8 = st[s][:, NEGMAX].rearrange("p (k e) -> p k e", k=KT)
                n8 = st[s][:, ROWMAX].rearrange("p (k e) -> p k e", k=KT)
                for m in range(KT):
                    ins = v.max(m8[:, m, :], bank[s][2][:, m * P:(m + 1) * P])
                steps_done(trip, ins)
                steps_done(trip, v.tensor_scalar(st[s][:, LAGNEG], m8[:, :, 0], -1.0, None, ALU.mult))
                hold()
                for m in range(KT):
                    ins = v.match_replace(lagv[s][:, m * P:(m + 1) * P], m8[:, m, :], bank[s][2][:, m * P:(m + 1) * P], GONE)
                ins.then_inc(lagmax_ready[s], 1)
                dve.wait_ge(lagmax_ready[s], nth(trip, 1, 1))
                hold()
                for m in range(KT):
                    ins = v.max(n8[:, m, :], lagv[s][:, m * P:(m + 1) * P])
                steps_done(trip, ins)
                steps_done(trip, v.tensor_copy(lag2[s][:, :, 0:TOPK - 8], n8[:, :, 0:TOPK - 8]))
                hold()
                for m in range(KT):
                    ins = v.match_replace(lagv[s][:, m * P:(m + 1) * P], lag2[s][:, m, :], lagv[s][:, m * P:(m + 1) * P], GONE)
                steps_done(trip, ins)

            def lag_softmax(trip, s):
                dve.wait_ge(lagexp_ready[s], nth(trip, 1, 1))
                for m in range(KT):
                    at = slice(m * P, (m + 1) * P)
                    ins = v.scalar_tensor_tensor(out=lage[s][:, at], in0=lagv[s][:, at], scalar=PICKED, in1=lage[s][:, at],
                                                 op0=ALU.is_le, op1=ALU.mult,
                                                 accum_out=st[s][:, LAGSUM.start + m:LAGSUM.start + m + 1])
                steps_done(trip, ins)
                steps_done(trip, v.reciprocal(st[s][:, LAGSUM], st[s][:, LAGSUM]))
                v.tensor_tensor(tiles(pr[s][0]), tiles(lage[s]), st[s][:, LAGSUM].unsqueeze(2).broadcast_to([P, KT, P]), ALU.mult
                                ).then_inc(lagw_ready[s], 1)

            def shift_products(trip, s):
                for i in range(2):
                    dve.wait_ge(lagf_psum[s], nth(trip, 2, i + 1 if i == 0 else 2))
                    src = bank[s][(3, 0)[i]][:, :]
                    d0, d1 = (lagv[s], lage[s]) if i == 0 else pr[s]
                    v.tensor_tensor(d0, src, spec[s][2 * i], ALU.mult)
                    if i == 1:
                        dve.wait_ge(ctxf_ready[s], nth(trip, 4, 4))
                    v.tensor_tensor(d1, src, spec[s][2 * i + 1], ALU.mult).then_inc(shift_ready[s], 1)

            def top_gates(trip, s):
                dve.wait_ge(gate_psum[s], nth(trip, 1, 1))
                logits = gates[s][:, 0, :]
                steps_done(trip, v.tensor_copy(logits[:, 0:NE], bank[s][0][:, 0:NE]))
                hold()
                steps_done(trip, v.max(st[s][:, TOP2], logits))
                v.tensor_scalar(st[s][:, ONE_A], st[s][:, TOP2][:, 0:1], -1.0, None, ALU.mult).then_inc(gatemax_ready[s], 1)
                steps_done(trip, v.tensor_copy(gate2[s][:, 0:2], st[s][:, TOP2][:, 0:2]))
                hold()
                steps_done(trip, v.match_replace(gates[s][:, 1, :], gate2[s][:, :], logits, GONE))

            def gated(trip, s):
                dve.wait_ge(gateexp_ready[s], nth(trip, 1, 1))
                e = gates[s][:, 2, 0:NE]
                steps_done(trip, v.scalar_tensor_tensor(out=e, in0=gates[s][:, 1, 0:NE], scalar=PICKED, in1=e, op0=ALU.is_le,
                                                        op1=ALU.mult, accum_out=st[s][:, ONE_B]))
                steps_done(trip, v.reciprocal(st[s][:, ONE_C], st[s][:, ONE_B]))
                steps_done(trip, v.tensor_scalar(e, e, st[s][:, ONE_C], 16.0 / ER, ALU.mult, ALU.mult))
                v.tensor_tensor(hg[s].rearrange("p (e r) -> p e r", e=NE), bank[s][0][:, NE:NG].rearrange("p (e r) -> p e r", e=NE),
                                e.unsqueeze(2).broadcast_to([P, NE, ER]), ALU.mult).then_inc(hg_ready[s], 1)

            def cross_qT(trip, s, g):
                dve.wait_ge(xqT_psum[s], nth(trip, 4, g + 1))
                v.tensor_copy(xqT[s], bank[s][2][0:XD, :]).then_inc(xqT_ready[s], 1)

            def cross_max(trip, s, g):
                for i in range(2):
                    dve.wait_ge(xs_psum[s], nth(trip, 8, 2 * g + i + 1))
                    r = st[s][:, ROWMAX.start + 2 * i:ROWMAX.start + 2 * i + 2]
                    steps_done(trip, v.tensor_reduce(r, bank[s][i][:, :].rearrange("p (h t) -> p h t", h=2), AX, ALU.max))
                    v.tensor_scalar(st[s][:, NEGMAX.start + 2 * i:NEGMAX.start + 2 * i + 2], r, -(XD ** -0.5), None, ALU.mult
                                    ).then_inc(xmax_ready[s], 1)

            def cross_probsT(trip, s, g):
                for i in range(2):
                    dve.wait_ge(xpT_psum[s], nth(trip, 8, 2 * g + i + 1))
                    v.tensor_copy(xpT[s][:, i * 512:(i + 1) * 512], bank[s][i][:, :]).then_inc(xpT_ready[s], 1)

            def cross_heads(trip, s, g):
                dve.wait_ge(xo_psum[s], nth(trip, 4, g + 1))
                sums = st[s][:, ROWSUM][:, 0:XG]
                steps_done(trip, v.reciprocal(sums, sums))
                v.tensor_tensor(xo[s].rearrange("p (h d) -> p h d", h=XG), bank[s][0][:, 0:XG * XD].rearrange("p (h d) -> p h d", h=XG),
                                sums.unsqueeze(2).broadcast_to([P, XG, XD]), ALU.mult).then_inc(xo_ready[s], 1)

            def routes(trip, s):
                dve.wait_ge(route_psum[s], nth(trip, 1, 1))
                e = st[s][:, EIGHT_A]
                steps_done(trip, v.tensor_tensor(e, bank[s][0][:, LH * LR:NL], br_row[:, :], ALU.add))
                steps_done(trip, v.tensor_reduce(st[s][:, ONE_C], e, AX, ALU.max))
                v.tensor_scalar(st[s][:, ONE_A], st[s][:, ONE_C], -1.0, None, ALU.mult).then_inc(routemax_ready[s], 1)

            def routed(trip, s):
                dve.wait_ge(routeexp_ready[s], nth(trip, 1, 1))
                e = st[s][:, EIGHT_A]
                steps_done(trip, v.reciprocal(st[s][:, ONE_C], st[s][:, ONE_B]))
                steps_done(trip, v.tensor_scalar(e, e, st[s][:, ONE_C], LH * 32.0 / LR, ALU.mult, ALU.mult))
                v.tensor_tensor(low[s].rearrange("p (h r) -> p h r", h=LH), bank[s][0][:, 0:LH * LR].rearrange("p (h r) -> p h r", h=LH),
                                e.unsqueeze(2).broadcast_to([P, LH, LR]), ALU.mult).then_inc(low_ready[s], 1)

            def attention(trip, l):
                for c in range(NCH + 1):
                    for s in both:
                        if c < NCH:
                            maxima(trip, s, l, c)
                    for s in both:
                        if c >= 1:
                            probsT(trip, s, l, c - 1)
                for s in both:
                    heads(trip, s, l)
                for s in both:
                    headsT(trip, s, l)

            def close_layer(trip, n, at):
                for s in both:
                    residual(trip, s, n, at)
                for s in both:
                    norm_x(trip, s, n)

            dve.wait_ge(ld_c, 96)
            dve.wait_ge(consts_ready, 2 + 3 * SLOTS)
            for i in (3, 4):
                v.tensor_tensor(cols[:, i, :], cols[:, i, :], q_scale, ALU.mult).then_inc(qw_ready, 1)
            dve.wait_ge(qw_ready, 2)

            with dve.Fori(0, TRIPS) as trip:
                for s in both:
                    qT_kT_first(trip, s)
                attention(trip, 0)
                close_layer(trip, 1, 0)
                for step in (cross_products, top_lags, lag_softmax, shift_products):
                    for s in both:
                        step(trip, s)
                close_layer(trip, 2, 1)
                for step in (top_gates, gated):
                    for s in both:
                        step(trip, s)
                close_layer(trip, 3, 1)
                for step in (clip_norm, apply_norm, qT_kT_second):
                    for s in both:
                        step(trip, s)
                attention(trip, 1)
                close_layer(trip, 4, 0)
                for s in both:
                    cross_qT(trip, s, 0)
                for g in range(XKV):
                    for s in both:
                        cross_max(trip, s, g)
                    for s in both:
                        cross_probsT(trip, s, g)
                    if g + 1 < XKV:
                        for s in both:
                            cross_qT(trip, s, g + 1)
                    for s in both:
                        cross_heads(trip, s, g)
                close_layer(trip, 5, 3)
                for step in (routes, routed):
                    for s in both:
                        step(trip, s)
                close_layer(trip, 6, 3)
            assert taken[0] == DVE_STEPS, taken[0]


def features_first(w):
    n, k = w.shape
    return np.ascontiguousarray(w.T.reshape(k // P, P, n).transpose(1, 0, 2))


def kernel(**inputs):
    import concourse.bacc as bacc
    from concourse.bass_utils import run_bass_kernel_spmd

    i = {k: np.asarray(v) for k, v in inputs.items()}
    consts, slopes = shape_constants()
    turned = lambda t: np.ascontiguousarray(t.transpose(0, 2, 1).reshape(B, KT, P, L).transpose(0, 2, 1, 3))
    by_feature = lambda b: b.reshape(KT, P).T
    lora_a = i["L0_ffn_lora_A"].reshape(NE * ER, D)
    lora_b = i["L0_ffn_lora_B"].transpose(0, 2, 1).reshape(2, GH * ER, D).transpose(1, 0, 2)
    arrays = {
        "x": i["x"], "ctx": i["ctx_4096"], "xT": turned(i["x"]), "ctxT": turned(i["ctx_4096"]),
        "w_qkv0": np.stack([features_first(i[f"L0_attn_W{n}"]) for n in "qkv"], 1),
        "w_o0": features_first(i["L0_attn_Wo"]),
        "cols": np.stack([by_feature(i[n]) for n in (
            "L0_attn_bq", "L0_attn_bk", "L0_attn_bv", "L1_attn_q_ln_w", "L1_attn_q_ln_b",
            "L1_attn_k_ln_w", "L1_attn_k_ln_b")], 1),
        "bo": i["L0_attn_bo"], "br": i["L1_ffn_br"],
        "w_gl": features_first(np.concatenate([i["L0_ffn_gate_W"], lora_a], 0)),
        "w_base": features_first(i["L0_ffn_base_W"]),
        "w_lb": lora_b,
        "w_qkv1": features_first(i["L1_attn_Wqkv"]),
        "w_o1": features_first(i["L1_attn_Wout"]),
        "w_xq": features_first(i["L1_xattn_Wq"]), "w_xk": features_first(i["L1_xattn_Wk"]),
        "w_xv": features_first(i["L1_xattn_Wv"]), "w_xo": features_first(i["L1_xattn_Wo"]),
        "w_al": features_first(np.concatenate([i["L1_ffn_A"].reshape(LH * LR, D), i["L1_ffn_Wr"]], 0)),
        "w_bl": i["L1_ffn_B"].transpose(0, 2, 1).reshape(LH * LR, D),
        **consts,
    }
    arrays = {k: np.ascontiguousarray(v) for k, v in arrays.items()}
    nc = bacc.Bacc("TRN2", target_bir_lowering=False, num_devices=1)
    aps = {k: nc.dram_tensor(f"{k}_dram", v.shape, F32, kind="ExternalInput").ap() for k, v in arrays.items()}
    out = nc.dram_tensor("out_dram", (B, L, D), F32, kind="ExternalOutput").ap()
    decoder(nc, aps, out, slopes)
    r = run_bass_kernel_spmd(nc, [{f"{k}_dram": v for k, v in arrays.items()}], core_ids=[0])
    return r.results[0]["out_dram"]
```

```python
from contextlib import ExitStack

import numpy as np
import concourse.bass as bass
from concourse import mybir

F32 = mybir.dt.float32
F32R = mybir.dt.float32r
ALU = mybir.AluOpType
ACT = mybir.ActivationFunctionType
AX = mybir.AxisListType.X

P = 128
B, L, D = 8, 128, 512
KT = D // P
SLOTS = 2
TRIPS = B // SLOTS
LAYERS = 6

H, HD = 32, 16
HT = P // HD
PAD = 2 * HD
CH = 4
NCH = H // CH
XH, XKV, XD = 16, 4, 96
XG = XH // XKV
WIDE, NARROW = 64, 32
XT = 2 * L
TOPK = int(2 * np.log(L))
NE, ER = 28, 8
GH = NE // 2
LH, LR = 8, 16
EPS = 1e-5
GONE = -3.0e38
PICKED = -1.0e38

TANK = 4608
PIECE = 512


def shape_constants():
    t = np.arange(L)
    ck, sk = np.arange(L // 2 + 1), np.arange(1, L // 2)
    cos_e = lambda n, f: np.cos(2 * np.pi * np.outer(n, f) / L)
    sin_e = lambda n, f: np.sin(2 * np.pi * np.outer(n, f) / L)
    same = np.concatenate([cos_e(t, ck), sin_e(t, sk)], 1)
    swap = np.concatenate([sin_e(t, ck), cos_e(t, sk)], 1)
    weight = np.where((ck == 0) | (ck == L // 2), 1.0, 2.0)
    inv1 = np.concatenate([weight * cos_e(t, ck), 2 * cos_e(t, sk)], 1).T / L
    inv2 = np.concatenate([-weight * sin_e(t, ck), 2 * sin_e(t, sk)], 1).T / L
    ctx_even = same.copy()
    ctx_even[L - 1, 0] += L
    odd = np.arange(1, 2 * L, 2)[: L // 2]
    ang = lambda n: 2 * np.pi * np.outer(n, odd) / (2 * L)
    lag_odd = np.concatenate([np.cos(ang(t)), np.sin(ang(t))], 1)
    full = np.arange(2 * L)
    co, so = np.cos(ang(full)), np.sin(ang(full))
    hold = lambda m: np.concatenate([m[: L - 1], m[L - 1:].sum(0, keepdims=True)], 0)
    ctx_odd = np.concatenate([hold(co), hold(so)], 1)
    ctx_odd_swap = np.concatenate([hold(so), hold(co)], 1)
    oute1 = np.concatenate([weight * cos_e(t, ck), 2 * cos_e(t, sk)], 1).T / (2 * L)
    oute2 = np.concatenate([weight * sin_e(t, ck), -2 * sin_e(t, sk)], 1).T / (2 * L)
    outo1 = np.concatenate([2 * np.cos(ang(t)), 2 * np.cos(ang(t))], 1).T / (2 * L)
    outo2 = np.concatenate([2 * np.sin(ang(t)), -2 * np.sin(ang(t))], 1).T / (2 * L)
    tables = [same, ctx_even, swap, ctx_odd, ctx_odd_swap, lag_odd, inv1, inv2, oute1, oute2, outo1, outo2]
    dft = np.stack(tables, 1).astype(np.float32)

    slopes = (1.0 / np.power(2.0, np.arange(1, H + 1, dtype=np.float32) * (8.0 / H))).astype(np.float64)
    rel = t[None, :] - t[:, None]
    causal = rel <= 0
    masks = np.stack([np.eye(P), np.where(causal, 0.0, -1e30), np.where(causal, rel, -1e36)], 1)
    even_odd = np.concatenate([np.arange(e, HT, 2) for e in range(HT // CH)])
    head_rows = (np.arange(P)[:, None] // HD == even_odd[None, :]).astype(np.float32)
    neg_scale = np.stack([np.full(H, -1.0 / np.sqrt(HD)), -slopes], 0)
    row_head = np.arange(KT)[None, :] * HT + np.arange(P)[:, None] // HD
    q_scale = (1.0 / np.sqrt(HD)) / slopes[row_head]
    small = np.concatenate([head_rows, np.broadcast_to(neg_scale.reshape(1, -1), (P, 2 * H)), q_scale], 1)
    return {
        "dft": dft, "masks": masks.astype(np.float32),
        "small": np.ascontiguousarray(small.astype(np.float32)),
    }, [float(s) for s in slopes]


def nth(trip, per_trip, j, before=0):
    return trip * per_trip + (j + before)


def decoder(nc, a, out, slopes):
    A0, AC, MOE, A1, XA, FF = range(LAYERS)
    TURNED = {A0: 0, MOE: 1, A1: 2, XA: 3, FF: 4}
    es = ExitStack()
    with es:
        def sb(name, shape, dt=F32):
            return es.enter_context(nc.sbuf_tensor(name, shape, dt))

        def sem(name):
            return es.enter_context(nc.semaphore(name))

        def per_slot(name):
            return [sem(f"{name}{s}") for s in range(SLOTS)]

        both = range(SLOTS)
        NG = NE + NE * ER
        NX, NKV = XH * XD, XKV * XD
        NXO = NX // P
        NL = LH * LR + LH

        WORDS = 32832
        wr = sb("wr", [P, WORDS], F32R)

        def region(at, k, n, parts=P):
            hi = wr[0:parts, at:at + k * n].rearrange("p (k n) -> p k n", k=k)
            lo = wr[0:parts, at + k * n:at + 2 * k * n].rearrange("p (k n) -> p k n", k=k)
            return hi, lo

        LOW, HIGH = 0, 16384
        AT_Q0, AT_O0 = LOW, LOW + 3 * 2 * KT * D
        AT_GL = HIGH
        AT_BASE = AT_GL + 2 * KT * NG
        AT_LB = AT_BASE + 2 * KT * D
        AT_QKV1 = LOW
        AT_O1 = AT_QKV1 + 2 * KT * 3 * D
        AT_XQ = HIGH
        AT_XK = AT_XQ + 2 * KT * NX
        AT_AL = AT_XK + 2 * KT * NKV
        AT_XV = LOW
        AT_XO = AT_XV + 2 * KT * NKV
        AT_BL = AT_XO + 2 * NXO * D
        w_qkv0 = [region(AT_Q0 + i * 2 * KT * D, KT, D) for i in range(3)]
        w_o0 = region(AT_O0, KT, D)
        w_gl, w_base = region(AT_GL, KT, NG), region(AT_BASE, KT, D)
        w_lb = region(AT_LB, 2, D, GH * ER)
        w_qkv1, w_o1 = region(AT_QKV1, KT, 3 * D), region(AT_O1, KT, D)
        w_xq, w_xk = region(AT_XQ, KT, NX), region(AT_XK, KT, NKV)
        w_xv, w_xo = region(AT_XV, KT, NKV), region(AT_XO, NXO, D)
        w_al, w_bl = region(AT_AL, KT, NL), region(AT_BL, 1, D)
        raw = [sb(f"raw{i}", [P, PIECE]) for i in range(2)]

        table = sb("table", [P, 12 * P])
        bo_row, bv_row = table[:, 0:D], table[:, D:2 * D]
        (DX, DC, DCS, DO, DOS, DL, I1, I2, E1, E2, O1, O2) = [table[:, i * P:(i + 1) * P] for i in range(12)]
        cols = sb("cols_sb", [P, 6, KT])
        br_row = sb("br_row", [P, LH])
        masks = sb("masks_sb", [P, 3, P])
        small = sb("small_sb", [P, HT + 2 * H + KT])
        ident, mask0, rel1 = (masks[:, i, :] for i in range(3))
        head_rows = small[:, 0:HT]
        neg_scale = [small[:, HT + H * l:HT + H * (l + 1)] for l in range(2)]
        q_scale = small[:, HT + 2 * H:]
        half = sb("half", [P, 2])

        xin = [sb(f"xin{s}", [P, D]) for s in both]
        xres = [sb(f"xres{s}", [P, D]) for s in both]
        cin = [sb(f"cin{s}", [P, D]) for s in both]
        tank = [sb(f"tank{s}", [P, TANK]) for s in both]
        st = [sb(f"stats{s}", [P, 160]) for s in both]
        lag2 = [sb(f"lag2_{s}", [P, KT, 8]) for s in both]
        gate2 = [sb(f"gate2_{s}", [P, 8]) for s in both]
        gates = [sb(f"gates{s}", [P, 3, NE + 8]) for s in both]
        hTh = sb("hTh", [P, KT, SLOTS, 2, P], F32R)
        hTl = sb("hTl", [P, KT, SLOTS, 2, P], F32R)
        bank = [[es.enter_context(nc.psum_tensor(f"bank{s}_{i}", [P, 512], F32)) for i in range(4)] for s in both]
        between = [nc.dram_tensor(f"between{i}", (B, L, D), F32, kind="Internal").ap() for i in range(2)]

        def view(s, at, n, parts=P):
            return tank[s][0:parts, at:at + n]

        qT = [view(s, 0, 512) for s in both]
        kT = [view(s, 512, 512) for s in both]
        kM = [view(s, 1024, 512) for s in both]
        pp = [[view(s, 1536 + 512 * i, 512) for i in range(2)] for s in both]
        pT = [[view(s, 2560 + 512 * i, 512) for i in range(2)] for s in both]
        vv = [view(s, 3584, H * PAD) for s in both]
        sums, hd = ([pp[s][i] for s in both] for i in range(2))

        def values_of(s, e):
            return vv[s].rearrange("p (h x) -> p h x", x=2 * PAD)[:, :, e * (PAD + HD):e * (PAD + HD) + HD]

        def every_other(ap, e):
            return ap.rearrange("p (h e d) -> p h e d", e=2, d=HD)[:, :, e, :]
        spec = [[view(s, 512 * i, 512) for i in range(4)] for s in both]
        pr = [[view(s, 2048 + 512 * i, 512) for i in range(2)] for s in both]
        lagv = [view(s, 3072, 512) for s in both]
        lage = [view(s, 3584, 512) for s in both]
        hg = [view(s, 0, NE * ER) for s in both]
        low = [view(s, 0, P) for s in both]
        xkT = [view(s, 0, XKV * XT, XD) for s in both]
        xv = [view(s, 1024, 2 * NKV) for s in both]
        xqT = [view(s, 1792, XG * P, XD) for s in both]
        xp = [view(s, 2304, XG * XT) for s in both]
        xpT = [view(s, 3328, XG * XT) for s in both]
        places = ([(j * WIDE // P, j * WIDE % P, j, 0, WIDE) for j in range(XG)]
                  + [(XG * WIDE // P, j * NARROW, j, WIDE, NARROW) for j in range(XG)])
        xq = [cin[s][:, 0:XG * XD] for s in both]

        ld_w0 = [sem(f"ld_w0_{n}") for n in ("q", "k", "vo")]
        ld_masks = sem("ld_masks")
        ld_c = sem("ld_c")
        consts_ready = sem("consts_ready")
        w0_hi = sem("w0_hi")
        w0_ready = sem("w0_ready")
        raw_loaded = [sem(f"raw_loaded{i}") for i in range(2)]
        w_split = sem("w_split")
        w_hi = sem("w_hi")
        dve_step = sem("dve_step")
        x_loaded = per_slot("x_loaded")
        c_loaded = per_slot("c_loaded")
        stored = per_slot("stored")
        r_loaded = per_slot("r_loaded")
        x_biased = sem("x_biased")
        xT_psum = per_slot("xT_psum")
        xT_hi = per_slot("xT_hi")
        xT_ready = per_slot("xT_ready")
        branch_psum = per_slot("branch_psum")
        ln_var = per_slot("ln_var")
        ln_rstd = per_slot("ln_rstd")
        x_ready = per_slot("x_ready")
        qk0_psum = sem("qk0_psum")
        qk0_ready = sem("qk0_ready")
        v0_psum = per_slot("v0_psum")
        proj_psum = per_slot("proj_psum")
        qkn_ready = per_slot("qkn_ready")
        qk_var = per_slot("qk_var")
        qk_rstd = per_slot("qk_rstd")
        qkT_psum = per_slot("qkT_psum")
        qT_ready = per_slot("qT_ready")
        kT_ready = per_slot("kT_ready")
        v_ready = per_slot("v_ready")
        kM_ready = per_slot("kM_ready")
        scores_psum = per_slot("scores_psum")
        max_ready = per_slot("max_ready")
        probs_ready = per_slot("probs_ready")
        probsT_psum = per_slot("probsT_psum")
        probsT_ready = per_slot("probsT_ready")
        pv_done = per_slot("pv_done")
        sums_ready = per_slot("sums_ready")
        sumsT_psum = per_slot("sumsT_psum")
        sumsT_ready = per_slot("sumsT_ready")
        heads_ready = per_slot("heads_ready")
        oT_hi = per_slot("oT_hi")
        oT_ready = per_slot("oT_ready")
        ctxf_psum = per_slot("ctxf_psum")
        ctxf_ready = per_slot("ctxf_ready")
        xf_psum = per_slot("xf_psum")
        cross_ready = per_slot("cross_ready")
        corr_psum = per_slot("corr_psum")
        lagmax_ready = per_slot("lagmax_ready")
        lagexp_ready = per_slot("lagexp_ready")
        lagw_ready = per_slot("lagw_ready")
        lagwT_psum = per_slot("lagwT_psum")
        lagwT_ready = per_slot("lagwT_ready")
        lagf_psum = per_slot("lagf_psum")
        shift_ready = per_slot("shift_ready")
        mix_psum = per_slot("mix_psum")
        mixmax_ready = per_slot("mixmax_ready")
        mixexp_ready = per_slot("mixexp_ready")
        mixed_ready = per_slot("mixed_ready")
        mixedT_psum = per_slot("mixedT_psum")
        mixedT_hi = per_slot("mixedT_hi")
        mixedT_ready = per_slot("mixedT_ready")
        cT_hi = per_slot("cT_hi")
        cT_ready = per_slot("cT_ready")
        xk_psum = sem("xk_psum")
        xk_ready = sem("xk_ready")
        xv_psum = per_slot("xv_psum")
        xv_ready = per_slot("xv_ready")
        xq_psum = per_slot("xq_psum")
        xq_ready = per_slot("xq_ready")
        xqT_psum = per_slot("xqT_psum")
        xqT_ready = per_slot("xqT_ready")
        xs_psum = per_slot("xs_psum")
        xmax_ready = per_slot("xmax_ready")
        xp_ready = per_slot("xp_ready")
        xpn_ready = per_slot("xpn_ready")
        xpT_psum = per_slot("xpT_psum")
        xpT_ready = per_slot("xpT_ready")
        xo_psum = per_slot("xo_psum")
        xo_hi = per_slot("xo_hi")
        xo_ready = per_slot("xo_ready")

        FREE = len(raw)
        PIECES_A0 = 2 * TRIPS
        PIECES_MOE = PIECES_A0 + 2
        PIECES_A1 = PIECES_MOE + 4 * TRIPS
        PIECES_XQ = PIECES_A1 + 4 * TRIPS
        PIECES_XV = PIECES_XQ + KT
        PIECES_XO = PIECES_XV + NXO
        PIECES_FF = PIECES_XO + KT + 1

        BN, MV, RSTD = slice(0, 6), slice(6, 8), slice(8, 9)
        QKBN, QKMV, QKRSTD = slice(12, 24), slice(24, 28), slice(28, 30)
        NEGMAX, ROWMAX, ROWSUM = slice(32, 64), slice(64, 96), slice(96, 128)
        LAGNEG, LAGSUM = slice(128, 132), slice(132, 136)
        TOP2 = slice(136, 144)
        ONE_A, ONE_B, ONE_C = slice(144, 145), slice(145, 146), slice(146, 147)
        EIGHT = slice(148, 156)

        def seq(trip, y, j=1):
            return nth(trip, 1, j, y * TRIPS)

        def turned(trip, y, ahead=0):
            return nth(trip, 1, 1 + ahead, TURNED[y] * TRIPS)

        def one_of(trip):
            return nth(trip, 1, 1)

        def heads_of(c):
            first = c * CH // HT * HT + c % (HT // CH)
            return range(first, first + HT - HT // CH + 1, HT // CH)

        def head_columns(at, c):
            h = heads_of(c)
            return slice(at.start + h.start, at.start + h.stop, h.step)

        def chunk(trip, l, j):
            return nth(trip, NCH, j, l * TRIPS * NCH)

        def attn(trip, l):
            return nth(trip, 1, 1, l * TRIPS)

        def mix(trip, y):
            return nth(trip, 1, 1, TRIPS if y == FF else 0)

        def f32(ap):
            return ap.bitcast(F32)

        def tiles(ap, k=KT):
            return ap.rearrange("p (k t) -> p k t", k=k)

        def tile_of(name, at, n, trip):
            count = -(-n // PIECE)
            w = n // count
            return [(a[name][:, bass.ds(trip, 1), j * w:(j + 1) * w].rearrange("p k n -> p (k n)"), w, P,
                     trip * n + (at + j * w), KT * n) for j in range(count)]

        def all_tiles(name, at, k, n, parts=P):
            return [(a[name][:, i, :], n, parts, at + i * n, k * n) for i in range(k)]

        def pieces_during_A0(trip):
            return tile_of("w_gl", AT_GL, NG, trip) + tile_of("w_base", AT_BASE, D, trip)

        def pieces_after_A0():
            return all_tiles("w_lb", AT_LB, 2, D, GH * ER)

        def pieces_during_AC(trip):
            return tile_of("w_qkv1", AT_QKV1, 3 * D, trip) + tile_of("w_o1", AT_O1, D, trip)

        def pieces_during_A1(trip):
            return tile_of("w_xq", AT_XQ, NX, trip) + tile_of("w_xk", AT_XK, NKV, trip)

        def pieces_from_A1():
            return (all_tiles("w_xv", AT_XV, KT, NKV) + all_tiles("w_xo", AT_XO, NXO, D)
                    + all_tiles("w_al", AT_AL, KT, NL) + all_tiles("w_bl", AT_BL, 1, D))

        block = es.enter_context(nc.Block())

        @block.sync
        def _(sp):
            def row(src, b):
                return src[bass.ds(b, 1)].rearrange("b p d -> (b p) d")

            def load_x(src, b, s):
                sp.dma_start(xin[s][:, :], row(src, b)).then_inc(x_loaded[s], 16)

            def load_residual(src, b, s):
                sp.dma_start(xres[s][:, :], row(src, b)).then_inc(r_loaded[s], 16)

            def fetch(pieces, trip, per_trip, before, which):
                for p, (src, n, parts, _, _) in list(enumerate(pieces))[which]:
                    sp.wait_ge(w_split, nth(trip, per_trip, FREE + p - 1, before))
                    hold()
                    sp.dma_start(raw[p % 2][0:parts, 0:n], src).then_inc(raw_loaded[p % 2], 16)

            def load_context(src, b, s):
                sp.dma_start(cin[s][:, :], row(src, b)).then_inc(c_loaded[s], 16)

            def hold():
                sp.nop(nofuse=True)

            def x_used(y, trip, s):
                if y == AC:
                    sp.wait_ge(xf_psum[s], one_of(trip))
                else:
                    sp.wait_ge(xT_psum[s], turned(trip, y))
                hold()

            def context_used(y, trip, s):
                if y == AC:
                    sp.wait_ge(ctxf_psum[s], nth(trip, 4, 4))
                else:
                    sp.wait_ge(xqT_psum[s], nth(trip, XKV, XKV))
                hold()

            def store(y, trip, s):
                sp.wait_ge(x_ready[s], seq(trip, y))
                dst = out if y == FF else between[y % 2]
                sp.dma_start(row(dst, trip * SLOTS + s), xres[s][:, :]).then_inc(stored[s], 16)

            for s in both:
                load_x(a["x"], s, s)
            sp.dma_start(masks[:, :, :], a["masks"]).then_inc(ld_masks, 16)
            for i, n in enumerate("qkvo"):
                sp.dma_start(tank[i // 2][:, i % 2 * KT * D:(i % 2 + 1) * KT * D], a["w0_" + n]).then_inc(ld_w0[min(i, 2)], 16)
                if i == 0:
                    sp.dma_start(cols[:, :, :], a["cols"]).then_inc(ld_c, 16)
                    sp.dma_start(bo_row, a["bo"].partition_broadcast(P)).then_inc(ld_c, 16)
                    sp.dma_start(bv_row, a["bv"].partition_broadcast(P)).then_inc(ld_c, 16)
                    sp.dma_start(br_row[:, :], a["br"].partition_broadcast(P)).then_inc(ld_c, 16)
                    for s in both:
                        sp.dma_start(small[:, s * 38:(s + 1) * 38], a["small"][:, s * 38:(s + 1) * 38]).then_inc(stored[s], 16)
            for s in both:
                load_residual(a["x"], s, s)
                load_context(a["ctx"], s, s)
            during = {A0: (pieces_during_A0, 2, 0), AC: (pieces_during_AC, 4, PIECES_MOE), A1: (pieces_during_A1, 4, PIECES_A1)}

            def trips_on(y, t, n):
                return (y + 1, t + n - TRIPS) if isinstance(t, int) and t + n >= TRIPS else (y, t + n)

            def source(y):
                return a["x"] if y == A0 else between[(y - 1) % 2]

            def fetch_during(y, t, which):
                if y in during:
                    pieces, per_trip, before = during[y]
                    fetch(pieces(t), t, per_trip, before, which)

            def load_x_after(y1, t1, y2, t2, s):
                if y2 < LAYERS:
                    x_used(y1, t1, s)
                    load_x(source(y2), t2 * SLOTS + s, s)

            def keep_fed(y, t):
                last = isinstance(t, int) and t == TRIPS - 1
                if y == AC or y == XA and not last:
                    for s in both:
                        context_used(y, t, s)
                        load_context(a["ctx" if y == AC and not last else "ctxT"],
                                     s if last else t * SLOTS + (SLOTS + s), s)
                if y == A0 and last:
                    sp.wait_ge(x_biased, SLOTS * TRIPS)
                    for s in both:
                        sp.wait_ge(v_ready[s], TRIPS)
                    sp.dma_start(table[:, :], a["dft"]).then_inc(ld_c, 16)
                if y == A1 and last:
                    fetch(pieces_from_A1(), 0, 0, PIECES_XQ, slice(0, KT))
                y1, t1 = trips_on(y, t, 1)
                y2, t2 = trips_on(y, t, 2)
                if y1 != AC:
                    for s in both:
                        load_x_after(y1, t1, y2, t2, s)
                for s in both:
                    store(y, t, s)
                if y1 == AC:
                    for s in both:
                        load_x_after(y1, t1, y2, t2, s)
                if y == A0 and last:
                    fetch(pieces_after_A0(), 0, 0, PIECES_A0, slice(0, 2))
                if y1 < LAYERS:
                    fetch_during(y1, t1, slice(0, 2))
                    for s in both:
                        sp.wait_ge(stored[s], nth(t, 16, 32, y * TRIPS * 16))
                        hold()
                        load_residual(source(y1), t1 * SLOTS + s, s)
                    fetch_during(y1, t1, slice(2, 4))
                if y == A1 and last:
                    fetch(pieces_from_A1(), 0, 0, PIECES_XQ, slice(KT, None))

            fetch_during(A0, 0, slice(0, 2))
            for s in both:
                x_used(A0, 0, s)
                load_x(a["x"], SLOTS + s, s)
            for y in range(LAYERS):
                with sp.Fori(0, TRIPS - 2) as trip:
                    keep_fed(y, trip)
                for t in range(TRIPS - 2, TRIPS):
                    keep_fed(y, t)
            for s in both:
                sp.wait_ge(stored[s], 16 + 16 * LAYERS * TRIPS)

        @block.tensor
        def _(pe):
            mm = nc.tensor.matmul

            def mm3(dst, lhs, rhs, start, stop):
                mm(dst, lhs[1], rhs[0], start=start, stop=False)
                mm(dst, lhs[0], rhs[1], start=False, stop=False)
                return mm(dst, lhs[0], rhs[0], start=False, stop=stop)

            def pair(w, *at):
                return w[0][at], w[1][at]

            ALL = slice(None)

            def xT(s, k):
                return hTh[:, k, s, 1, :], hTl[:, k, s, 1, :]

            def x_to_features(trip, s, y, ahead, b):
                pe.wait_ge(x_loaded[s], nth(trip, 16, 16 + 16 * ahead, 16 * y * TRIPS))
                for m in range(KT):
                    ins = nc.tensor.transpose(bank[s][b][:, m * P:(m + 1) * P], xin[s][:, m * P:(m + 1) * P], ident)
                ins.then_inc(xT_psum[s], 1)

            def q_k_first(trip):
                for s in both:
                    pe.wait_ge(xT_ready[s], turned(trip, A0))
                for i in range(2):
                    pe.wait_ge(w0_ready, 2 + i + 1)
                    for m in range(KT):
                        dst = bank[i][m // 2][:, m % 2 * 256:(m % 2 + 1) * 256]
                        for k in range(KT):
                            ins = mm3(dst, pair(w_qkv0[i], ALL, k, slice(m * P, (m + 1) * P)),
                                      (hTh[:, k, :, 1, :], hTl[:, k, :, 1, :]), k == 0, k == KT - 1)
                        if m % 2:
                            ins.then_inc(qk0_psum, 1)

            def v_first(trip, s):
                pe.wait_ge(w0_ready, 2 + 3)
                for k in range(KT):
                    ins = mm3(bank[s][2][:, :], xT(s, k), pair(w_qkv0[2], ALL, k), k == 0, k == KT - 1)
                ins.then_inc(v0_psum[s], 1)

            def project_second(trip, s, i, tiles_of=range(KT)):
                if i == 0:
                    pe.wait_ge(xT_ready[s], turned(trip, A1))
                for k in tiles_of:
                    ins = mm3(bank[s][i][:, :], xT(s, k), pair(w_qkv1, ALL, k, slice(i * D, (i + 1) * D)), k == 0, k == KT - 1)
                if KT - 1 in tiles_of:
                    ins.then_inc(proj_psum[s], 1)

            def normed_to_features(trip, s):
                pe.wait_ge(qkn_ready[s], one_of(trip))
                for i in (1, 0):
                    for m in range(KT):
                        ins = nc.tensor.transpose(bank[s][i][:, m * P:(m + 1) * P], pp[s][i][:, m * P:(m + 1) * P], ident)
                    ins.then_inc(qkT_psum[s], 1)

            def scores(trip, s, l, c):
                pe.wait_ge(kM_ready[s], chunk(trip, l, c + 1))
                if c == 0 and l == 1:
                    pe.wait_ge(qT_ready[s], one_of(trip))
                if c >= 2:
                    pe.wait_ge(max_ready[s], chunk(trip, l, c - 1))
                m = c * CH // HT
                mm(bank[s][c % 2][:, :], qT[s][:, m * P:(m + 1) * P], kM[s], start=True, stop=True
                   ).then_inc(scores_psum[s], 1)

            def probs_transpose(trip, s, l, c):
                pe.wait_ge(probs_ready[s], chunk(trip, l, c + 1))
                if c == 0:
                    pe.wait_ge(v_ready[s], attn(trip, l))
                else:
                    pe.wait_ge(probsT_ready[s], chunk(trip, l, c))
                for j in range(CH):
                    ins = nc.tensor.transpose(bank[s][2][:, j * P:(j + 1) * P], pp[s][c % 2][:, j * P:(j + 1) * P], ident)
                ins.then_inc(probsT_psum[s], 1)

            def weigh_values(trip, s, l, c):
                pe.wait_ge(probsT_ready[s], chunk(trip, l, c + 1))
                m, e = c // 2, c % 2
                for j, h in enumerate(heads_of(c)):
                    ins = mm(bank[s][3][j * PAD:(j + 1) * PAD, m * P:(m + 1) * P], vv[s][:, h * PAD:(h + 1) * PAD],
                             pT[s][c % 2][:, j * P:(j + 1) * P], start=e == 0, stop=e == 1)
                ins.then_inc(pv_done[s], 1)

            def sums_to_features(trip, s, l):
                pe.wait_ge(sums_ready[s], nth(trip, 2, 2, 2 * l * TRIPS))
                for m in range(KT):
                    ins = nc.tensor.transpose(bank[s][0][:, m * P:(m + 1) * P], sums[s][:, m * P:(m + 1) * P], ident)
                ins.then_inc(sumsT_psum[s], 1)

            def attention_out(trip, s, l):
                pe.wait_ge(oT_ready[s], attn(trip, l))
                if l == 0:
                    pe.wait_ge(w0_ready, 2 + 4)
                w = (w_o0, w_o1)[l]
                for k in range(KT):
                    ins = mm3(bank[s][3][:, :], (hTh[:, k, s, 0, :], hTl[:, k, s, 0, :]), pair(w, ALL, k), k == 0, k == KT - 1)
                ins.then_inc(branch_psum[s], 1)

            def context_spectra(trip, s, part):
                for i in (2 * part, 2 * part + 1):
                    if part == 1:
                        pe.wait_ge(cross_ready[s], one_of(trip))
                    mm(bank[s][(2, 0, 1, 3)[i]][:, :], (DC, DCS, DO, DOS)[i], cin[s][:, :], start=True, stop=True
                       ).then_inc(ctxf_psum[s], 1)

            def x_spectrum(trip, s):
                pe.wait_ge(x_loaded[s], nth(trip, 16, 16, 16 * AC * TRIPS))
                pe.wait_ge(ln_var[s], seq(trip, AC, 0))
                mm(bank[s][3][:, :], DX, xin[s][:, :], start=True, stop=True).then_inc(xf_psum[s], 1)

            def correlation(trip, s):
                pe.wait_ge(cross_ready[s], one_of(trip))
                for m in range(KT):
                    mm(bank[s][2][:, m * P:(m + 1) * P], pr[s][0][:, m * P:(m + 1) * P], I1, start=True, stop=False)
                    ins = mm(bank[s][2][:, m * P:(m + 1) * P], pr[s][1][:, m * P:(m + 1) * P], I2, start=False, stop=True)
                ins.then_inc(corr_psum[s], 1)

            def lag_weights_to_lags(trip, s):
                pe.wait_ge(lagw_ready[s], one_of(trip))
                for m in range(KT):
                    ins = nc.tensor.transpose(bank[s][0][:, m * P:(m + 1) * P], pr[s][0][:, m * P:(m + 1) * P], ident)
                ins.then_inc(lagwT_psum[s], 1)

            def lag_spectrum(trip, s):
                pe.wait_ge(lagwT_ready[s], one_of(trip))
                pe.wait_ge(ctxf_ready[s], nth(trip, 4, 4))
                mm(bank[s][3][:, :], DX, pr[s][1], start=True, stop=True).then_inc(lagf_psum[s], 1)
                mm(bank[s][0][:, :], DL, pr[s][1], start=True, stop=True).then_inc(lagf_psum[s], 1)

            def shifted_sum(trip, s):
                for i, (t, src) in enumerate(((E1, lagv[s]), (E2, lage[s]), (O1, pr[s][0]), (O2, pr[s][1]))):
                    if i % 2 == 0:
                        pe.wait_ge(shift_ready[s], nth(trip, 2, i // 2 + 1))
                    ins = mm(bank[s][1][:, :], t, src, start=i == 0, stop=i == 3)
                ins.then_inc(branch_psum[s], 1)

            def gates_and_rank(trip, s):
                pe.wait_ge(xT_ready[s], turned(trip, MOE))
                for k in range(KT):
                    ins = mm3(bank[s][0][:, 0:NG], xT(s, k), pair(w_gl, ALL, k), k == 0, k == KT - 1)
                ins.then_inc(mix_psum[s], 1)

            def base(trip, s):
                pe.wait_ge(ln_var[s], seq(trip, MOE, 0))
                for k in range(KT):
                    mm3(bank[s][1][:, :], xT(s, k), pair(w_base, ALL, k), k == 0, False)

            def gated_to_rank(trip, s):
                pe.wait_ge(mixed_ready[s], mix(trip, MOE))
                n = GH * ER
                for i in range(2):
                    ins = nc.tensor.transpose(bank[s][2][0:n, i * P:(i + 1) * P], hg[s][:, i * n:(i + 1) * n], ident)
                ins.then_inc(mixedT_psum[s], 1)

            def experts_out(trip, s):
                pe.wait_ge(mixedT_ready[s], mix(trip, MOE))
                for i in range(2):
                    lhs = hTh[0:GH * ER, i, s, 0, :], hTl[0:GH * ER, i, s, 0, :]
                    ins = mm3(bank[s][1][:, :], lhs, pair(w_lb, ALL, i), False, i == 1)
                ins.then_inc(branch_psum[s], 1)

            def cross_keys(trip):
                for s in both:
                    pe.wait_ge(cT_ready[s], one_of(trip))
                for g in range(XKV):
                    for k in range(KT):
                        ins = mm3(bank[g % 2][g // 2][0:XD, :], pair(w_xk, ALL, k, slice(g * XD, (g + 1) * XD)),
                                  (hTh[:, k].rearrange("p s h t -> p (s h t)"), hTl[:, k].rearrange("p s h t -> p (s h t)")),
                                  k == 0, k == KT - 1)
                    ins.then_inc(xk_psum, 1)

            def cross_kept_values(trip, s, n):
                t = 1 - n
                if n == 0:
                    pe.wait_ge(ln_var[s], seq(trip, XA, 0))
                else:
                    pe.wait_ge(xv_ready[s], nth(trip, 2, 1))
                for k in range(KT):
                    ins = mm3(bank[s][3][:, 0:NKV], (hTh[:, k, s, t, :], hTl[:, k, s, t, :]), pair(w_xv, ALL, k), k == 0, k == KT - 1)
                ins.then_inc(xv_psum[s], 1)

            def cross_q(trip, s, g):
                if g == 0:
                    pe.wait_ge(xT_ready[s], turned(trip, XA))
                else:
                    pe.wait_ge(xqT_ready[s], nth(trip, XKV, g))
                n = XG * XD
                for k in range(KT):
                    ins = mm3(bank[s][2][:, 0:n], xT(s, k), pair(w_xq, ALL, k, slice(g * n, (g + 1) * n)), k == 0, k == KT - 1)
                ins.then_inc(xq_psum[s], 1)

            def cross_qT(trip, s, g):
                pe.wait_ge(xq_ready[s], nth(trip, XKV, g + 1))
                for j in range(XG):
                    ins = nc.tensor.transpose(bank[s][2][0:XD, j * P:(j + 1) * P], xq[s][:, j * XD:(j + 1) * XD], ident)
                ins.then_inc(xqT_psum[s], 1)

            def cross_scores(trip, s, g):
                pe.wait_ge(xqT_ready[s], nth(trip, XKV, g + 1))
                if g == 0:
                    pe.wait_ge(xk_ready, nth(trip, XKV, XKV))
                if g > 0:
                    pe.wait_ge(xo_ready[s], nth(trip, XKV, g))
                for i in range(2):
                    for j in range(2):
                        ins = mm(bank[s][i][:, j * XT:(j + 1) * XT], xqT[s][:, (2 * i + j) * P:(2 * i + j + 1) * P],
                                 xkT[s][:, g * XT:(g + 1) * XT], start=True, stop=True)
                    ins.then_inc(xs_psum[s], 1)

            def cross_probsT(trip, s, g):
                for i in range(2):
                    pe.wait_ge(xpn_ready[s], nth(trip, 2 * XKV, 2 * g + i + 1))
                    for j in range(4):
                        at = (4 * i + j) * P
                        ins = nc.tensor.transpose(bank[s][i][:, j * P:(j + 1) * P], xp[s][:, at:at + P], ident)
                    ins.then_inc(xpT_psum[s], 1)

            def cross_values(trip, s, g):
                pe.wait_ge(xpT_ready[s], nth(trip, 2 * XKV, 2 * g + 2))
                if g == 0:
                    pe.wait_ge(xv_ready[s], nth(trip, 2, 2))
                for tile in range(XG * XD // P):
                    for t in range(2):
                        for _, row, j, first, n in [at for at in places if at[0] == tile]:
                            ins = mm(bank[s][0][row:row + n, tile * P:(tile + 1) * P],
                                     xv[s][:, t * NKV + g * XD + first:t * NKV + g * XD + first + n],
                                     xpT[s][:, (2 * j + t) * P:(2 * j + t + 1) * P], start=t == 0, stop=t == 1)
                ins.then_inc(xo_psum[s], 1)

            def cross_out(trip, s, g):
                pe.wait_ge(xo_ready[s], nth(trip, XKV, g + 1))
                pe.wait_ge(w_split, FREE + PIECES_XV + XG * XD // P * (g + 1))
                n = XG * XD // P
                for m in range(n):
                    ins = mm3(bank[s][3][:, :], (hTh[:, m, s, 0, :], hTl[:, m, s, 0, :]), pair(w_xo, ALL, g * n + m),
                              g == 0 and m == 0, g == XKV - 1 and m == n - 1)
                if g == XKV - 1:
                    ins.then_inc(branch_psum[s], 1)

            def routes_and_low(trip, s):
                pe.wait_ge(xT_ready[s], turned(trip, FF))
                for k in range(KT):
                    ins = mm3(bank[s][0][:, 0:NL], xT(s, k), pair(w_al, ALL, k), k == 0, k == KT - 1)
                ins.then_inc(mix_psum[s], 1)

            def low_to_rank(trip, s):
                pe.wait_ge(mixed_ready[s], mix(trip, FF))
                nc.tensor.transpose(bank[s][2][:, 0:P], low[s], ident).then_inc(mixedT_psum[s], 1)

            def heads_out(trip, s):
                pe.wait_ge(mixedT_ready[s], mix(trip, FF))
                mm3(bank[s][3][:, :], (hTh[:, 0, s, 0, :], hTl[:, 0, s, 0, :]), pair(w_bl, ALL, 0), True, True).then_inc(branch_psum[s], 1)

            def each(step, trip, *args):
                for s in both:
                    step(trip, s, *args)

            def self_attention(trip, l, next_x):
                for c in range(1, NCH):
                    each(scores, trip, l, c)
                    each(probs_transpose, trip, l, c - 1)
                    if c >= 2:
                        each(weigh_values, trip, l, c - 2)
                each(weigh_values, trip, l, NCH - 2)
                each(probs_transpose, trip, l, NCH - 1)
                for s in both:
                    sums_to_features(trip, s, l)
                    weigh_values(trip, s, l, NCH - 1)
                if next_x is not None:
                    each(x_to_features, trip, next_x, 1, 1)
                each(attention_out, trip, l)

            def first_layer(trip, more):
                q_k_first(trip)
                v_first(trip, 0)
                each(scores, trip, 0, 0)
                v_first(trip, 1)
                self_attention(trip, 0, A0 if more else None)

            def last_layer(trip, more):
                each(routes_and_low, trip)
                if more:
                    each(x_to_features, trip, FF, 1, 1)
                each(low_to_rank, trip)
                each(heads_out, trip)

            pe.wait_ge(ld_masks, 16)
            each(x_to_features, 0, A0, 0, 1)
            with pe.Fori(0, TRIPS - 1) as trip:
                first_layer(trip, True)
            first_layer(TRIPS - 1, False)
            pe.wait_ge(ld_c, 80)
            with pe.Fori(0, TRIPS) as trip:
                for s in both:
                    pe.wait_ge(c_loaded[s], nth(trip, 16, 16))
                    context_spectra(trip, s, 0)
                each(x_spectrum, trip)
                each(correlation, trip)
                each(context_spectra, trip, 1)
                for s in both:
                    lag_weights_to_lags(trip, s)
                    lag_spectrum(trip, s)
                each(shifted_sum, trip)
            each(x_to_features, 0, MOE, 0, 3)
            pe.wait_ge(w_split, FREE + PIECES_MOE)
            with pe.Fori(0, TRIPS) as trip:
                each(gates_and_rank, trip)
                each(base, trip)
                each(x_to_features, trip, MOE, 1, 3)
                each(gated_to_rank, trip)
                each(experts_out, trip)
            pe.wait_ge(w_split, FREE + PIECES_A1)
            for s in both:
                pe.wait_ge(ln_var[s], A1 * TRIPS)
            with pe.Fori(0, TRIPS) as trip:
                for s in both:
                    for i in range(2):
                        project_second(trip, s, i)
                project_second(trip, 0, 2)
                normed_to_features(trip, 0)
                project_second(trip, 1, 2, range(KT // 2))
                normed_to_features(trip, 1)
                scores(trip, 0, 1, 0)
                project_second(trip, 1, 2, range(KT // 2, KT))
                scores(trip, 1, 1, 0)
                self_attention(trip, 1, A1)
            pe.wait_ge(w_split, FREE + PIECES_XQ)
            with pe.Fori(0, TRIPS) as trip:
                each(cross_q, trip, 0)
                cross_keys(trip)
                pe.wait_ge(w_split, FREE + PIECES_XV)
                each(cross_kept_values, trip, 0)
                each(cross_qT, trip, 0)
                each(cross_kept_values, trip, 1)
                for g in range(XKV):
                    each(cross_scores, trip, g)
                    if g + 1 < XKV:
                        each(cross_q, trip, g + 1)
                    else:
                        each(x_to_features, trip, XA, 1, 2)
                    if g > 0:
                        each(cross_out, trip, g - 1)
                    each(cross_probsT, trip, g)
                    for s in both:
                        if g + 1 < XKV:
                            cross_qT(trip, s, g + 1)
                        cross_values(trip, s, g)
                each(cross_out, trip, XKV - 1)
            pe.wait_ge(w_split, FREE + PIECES_FF)
            with pe.Fori(0, TRIPS - 1) as trip:
                last_layer(trip, True)
            last_layer(TRIPS - 1, False)

        @block.scalar
        def _(act):
            av = nc.scalar.activation
            copy = nc.scalar.copy

            def xT_split(trip, s, y, ahead, b):
                act.wait_ge(xT_psum[s], turned(trip, y, ahead))
                copy(hTh[:, :, s, 1, :], tiles(bank[s][b][:, :])).then_inc(xT_hi[s], 1)

            def qT_second(trip, s):
                act.wait_ge(qkT_psum[s], nth(trip, 2, 2))
                for m in range(KT):
                    ins = av(qT[s][:, m * P:(m + 1) * P], bank[s][0][:, m * P:(m + 1) * P], ACT.Identity,
                             bias=cols[:, 3, m:m + 1], scale=cols[:, 2, m:m + 1])
                ins.then_inc(qT_ready[s], 1)

            def probs(trip, s, l, c):
                act.wait_ge(max_ready[s], chunk(trip, l, c + 1))
                for j, h in enumerate(heads_of(c)):
                    blockp = pp[s][c % 2][:, j * P:(j + 1) * P]
                    ins = av(blockp, blockp, ACT.Exp, bias=st[s][:, NEGMAX.start + h:NEGMAX.start + h + 1],
                             scale=(HD ** -0.5 if l == 0 else slopes[h]),
                             accum_out=st[s][:, ROWSUM.start + h:ROWSUM.start + h + 1])
                ins.then_inc(probs_ready[s], 1)

            def repeat_sums(trip, s, l):
                act.wait_ge(sums_ready[s], nth(trip, 2, 1, 2 * l * TRIPS))
                copy(sums[s].rearrange("p (h d) -> p h d", h=H), st[s][:, ROWSUM].unsqueeze(2).broadcast_to([P, H, HD])
                     ).then_inc(sums_ready[s], 1)

            def sumsT(trip, s, l):
                act.wait_ge(sumsT_psum[s], attn(trip, l))
                copy(sums[s], bank[s][0][:, :]).then_inc(sumsT_ready[s], 1)

            def oT_split(trip, s, l):
                act.wait_ge(heads_ready[s], attn(trip, l))
                copy(hTh[:, :, s, 0, :], tiles(hd[s])).then_inc(oT_hi[s], 1)

            def context_spectra(trip, s, part):
                for i in (2 * part, 2 * part + 1):
                    act.wait_ge(ctxf_psum[s], nth(trip, 4, i + 1))
                    copy(spec[s][i], bank[s][(2, 0, 1, 3)[i]][:, :]).then_inc(ctxf_ready[s], 1)

            def lag_exp(trip, s):
                act.wait_ge(lagmax_ready[s], one_of(trip))
                for m in range(KT):
                    ins = av(lage[s][:, m * P:(m + 1) * P], bank[s][2][:, m * P:(m + 1) * P], ACT.Exp,
                             bias=st[s][:, LAGNEG.start + m:LAGNEG.start + m + 1], scale=1.0)
                ins.then_inc(lagexp_ready[s], 1)

            def lag_weightsT(trip, s):
                act.wait_ge(lagwT_psum[s], one_of(trip))
                copy(pr[s][1], bank[s][0][:, :]).then_inc(lagwT_ready[s], 1)

            def gate_exp(trip, s):
                act.wait_ge(mixmax_ready[s], mix(trip, MOE))
                av(gates[s][:, 2, 0:NE], gates[s][:, 0, 0:NE], ACT.Exp, bias=st[s][:, ONE_A], scale=1.0
                   ).then_inc(mixexp_ready[s], 1)

            def gated_split(trip, s):
                act.wait_ge(mixedT_psum[s], mix(trip, MOE))
                copy(hTh[0:GH * ER, 0:2, s, 0, :], tiles(bank[s][2][0:GH * ER, 0:2 * P], 2)).then_inc(mixedT_hi[s], 1)

            def context_split(trip, s):
                act.wait_ge(c_loaded[s], nth(trip, 16, 16, 16 * TRIPS))
                act.wait_ge(branch_psum[s], seq(trip, XA, 0))
                copy(hTh[:, :, s, 0, :], tiles(cin[s][:, :])).then_inc(cT_hi[s], 1)

            def cross_keys(trip):
                for g in range(XKV):
                    act.wait_ge(xk_psum, nth(trip, XKV, g + 1))
                    for s in both:
                        ins = copy(xkT[s][:, g * XT:(g + 1) * XT], bank[g % 2][g // 2][0:XD, s * XT:(s + 1) * XT])
                    ins.then_inc(xk_ready, 1)

            def cross_kept_values(trip, s, n):
                act.wait_ge(xv_psum[s], nth(trip, 2, n + 1))
                t = 1 - n
                copy(xv[s][:, t * NKV:(t + 1) * NKV], bank[s][3][:, 0:NKV]).then_inc(xv_ready[s], 1)

            def cross_q(trip, s, g):
                act.wait_ge(xq_psum[s], nth(trip, XKV, g + 1))
                if g == 0:
                    act.wait_ge(cT_ready[s], one_of(trip))
                copy(xq[s], bank[s][2][:, 0:XG * XD]).then_inc(xq_ready[s], 1)

            def cross_probs(trip, s, g):
                for i in range(2):
                    act.wait_ge(xmax_ready[s], nth(trip, 2 * XKV, 2 * g + i + 1))
                    for j in range(2):
                        h = 2 * i + j
                        ins = av(xp[s][:, h * XT:(h + 1) * XT], bank[s][i][:, j * XT:(j + 1) * XT], ACT.Exp,
                                 bias=st[s][:, NEGMAX.start + h:NEGMAX.start + h + 1], scale=XD ** -0.5,
                                 accum_out=st[s][:, ROWSUM.start + h:ROWSUM.start + h + 1])
                    ins.then_inc(xp_ready[s], 1)

            def cross_heads(trip, s, g):
                act.wait_ge(xo_psum[s], nth(trip, XKV, g + 1))
                n = XG * XD // P
                copy(hTh[:, 0:n, s, 0, :], tiles(bank[s][0][:, 0:XG * XD], n)).then_inc(xo_hi[s], 1)

            def route_exp(trip, s):
                act.wait_ge(mixmax_ready[s], mix(trip, FF))
                av(st[s][:, EIGHT], st[s][:, EIGHT], ACT.Exp, bias=st[s][:, ONE_A], scale=1.0,
                   accum_out=st[s][:, ONE_B]).then_inc(mixexp_ready[s], 1)

            def low_split(trip, s):
                act.wait_ge(mixedT_psum[s], mix(trip, FF))
                copy(hTh[:, 0, s, 0, :], bank[s][2][:, 0:P]).then_inc(mixedT_hi[s], 1)

            def each(step, trip, *args):
                for s in both:
                    step(trip, s, *args)

            def first_layer(trip, more):
                for c in range(NCH):
                    each(probs, trip, 0, c)
                each(repeat_sums, trip, 0)
                each(sumsT, trip, 0)
                each(oT_split, trip, 0)
                if more:
                    each(xT_split, trip, A0, 1, 1)

            def last_layer(trip, more):
                each(route_exp, trip)
                if more:
                    each(xT_split, trip, FF, 1, 1)
                each(low_split, trip)

            each(xT_split, 0, A0, 0, 1)
            for i in range(4):
                act.wait_ge(ld_w0[min(i, 2)], 16 if i < 2 else 32)
                w = w_qkv0[i] if i < 3 else w_o0
                copy(w[0], tiles(tank[i // 2][:, i % 2 * KT * D:(i % 2 + 1) * KT * D])).then_inc(w0_hi, 1)
            with act.Fori(0, TRIPS - 1) as trip:
                first_layer(trip, True)
            first_layer(TRIPS - 1, False)
            with act.Fori(0, TRIPS) as trip:
                each(context_spectra, trip, 0)
                lag_exp(trip, 0)
                each(context_spectra, trip, 1)
                lag_weightsT(trip, 0)
                lag_exp(trip, 1)
                lag_weightsT(trip, 1)
            each(xT_split, 0, MOE, 0, 3)
            with act.Fori(0, TRIPS) as trip:
                each(gate_exp, trip)
                each(xT_split, trip, MOE, 1, 3)
                each(gated_split, trip)
            with act.Fori(0, TRIPS) as trip:
                each(qT_second, trip)
                for c in range(NCH):
                    each(probs, trip, 1, c)
                each(repeat_sums, trip, 1)
                each(sumsT, trip, 1)
                each(oT_split, trip, 1)
                each(xT_split, trip, A1, 1, 1)
            with act.Fori(0, TRIPS) as trip:
                each(context_split, trip)
                each(cross_q, trip, 0)
                cross_keys(trip)
                each(cross_kept_values, trip, 0)
                each(cross_kept_values, trip, 1)
                for g in range(XKV):
                    each(cross_probs, trip, g)
                    if g + 1 < XKV:
                        each(cross_q, trip, g + 1)
                    else:
                        each(xT_split, trip, XA, 1, 2)
                    each(cross_heads, trip, g)
            with act.Fori(0, TRIPS - 1) as trip:
                last_layer(trip, True)
            last_layer(TRIPS - 1, False)

        @block.gpsimd
        def _(pool):
            nc.gpsimd.memset(half[:, :], -0.5).then_inc(consts_ready, 1)
            for i in range(FREE):
                nc.gpsimd.memset(raw[i][:, 0:1], 0.0).then_inc(w_split, 1)
            for s in both:
                nc.gpsimd.memset(lag2[s][:, :, :], GONE).then_inc(consts_ready, 1)
                nc.gpsimd.memset(gate2[s][:, :], GONE).then_inc(consts_ready, 1)
                nc.gpsimd.memset(gates[s][:, :, :], GONE).then_inc(consts_ready, 1)
            pool.wait_ge(consts_ready, 1 + 3 * SLOTS)
            pool.wait_ge(ld_c, 64)

            def hold():
                pool.nop(nofuse=True)

            def add_bias(trip, s):
                pool.wait_ge(r_loaded[s], nth(trip, 16, 16))
                nc.gpsimd.tensor_tensor(xres[s][:, :], xres[s][:, :], bo_row, ALU.add).then_inc(x_biased, 1)

            def mask_keys(trip, s, l, c):
                if c > 0:
                    pool.wait_ge(scores_psum[s], chunk(trip, l, c))
                elif l == 0:
                    pool.wait_ge(qk0_ready, nth(trip, 2, 2))
                else:
                    pool.wait_ge(kT_ready[s], one_of(trip))
                m, j = c * CH // HT, c * CH % HT
                nc.gpsimd.tensor_tensor(kM[s].rearrange("p (h t) -> p h t", h=CH),
                                        kT[s][:, m * P:(m + 1) * P].unsqueeze(1).broadcast_to([P, CH, P]),
                                        head_rows[:, j:j + CH].unsqueeze(2).broadcast_to([P, CH, P]),
                                        ALU.mult).then_inc(kM_ready[s], 1)

            def rstd(y, trip, s):
                pool.wait_ge(ln_var[s], seq(trip, y))
                nc.gpsimd.tensor_tensor(st[s][:, RSTD], st[s][:, MV][:, 1:2], half[:, 0:1], ALU.pow
                                        ).then_inc(ln_rstd[s], 1)

            def rstd_qk(trip, s):
                pool.wait_ge(qk_var[s], one_of(trip))
                nc.gpsimd.tensor_tensor(st[s][:, QKRSTD], st[s][:, QKMV].rearrange("p (a b) -> p a b", b=2)[:, :, 1],
                                        half[:, 0:2], ALU.pow).then_inc(qk_rstd[s], 1)

            def split(pieces, p, trip, per_trip, before):
                _, n, parts, at, span = pieces[p]
                src = raw[p % 2][0:parts, 0:n]
                hi, lo = (wr[0:parts, bass.ds(x, n)] for x in (at, at + span))
                pool.wait_ge(raw_loaded[p % 2], nth(trip, 8 * per_trip, 16 * (p // 2 + 1), 8 * before))
                hold()
                nc.gpsimd.tensor_copy(hi, src).then_inc(w_hi, 1)
                pool.wait_ge(w_hi, nth(trip, per_trip, p + 1, before))
                nc.gpsimd.tensor_tensor(lo, src, f32(hi), ALU.subtract).then_inc(w_split, 1)

            def each(step, *args):
                for s in both:
                    step(*args, s) if step is rstd else step(args[0], s, *args[1:])

            def zeros_around_values():
                for s in both:
                    nc.gpsimd.memset(vv[s], 0.0).then_inc(consts_ready, 1)

            pool.wait_ge(w0_ready, 2 + 4)
            zeros_around_values()
            with pool.Fori(0, TRIPS) as trip:
                for p in range(2):
                    split(pieces_during_A0(trip), p, trip, 2, 0)
                for c in range(NCH):
                    each(mask_keys, trip, 0, c)
                    if c == 1:
                        each(add_bias, trip)
                each(rstd, A0, trip)
            for p in range(2):
                split(pieces_after_A0(), p, 0, 2, PIECES_A0)
            for s in both:
                pool.wait_ge(branch_psum[s], TRIPS * (A0 + 1))
            with pool.Fori(0, TRIPS) as trip:
                for p in range(4):
                    split(pieces_during_AC(trip), p, trip, 4, PIECES_MOE)
                each(rstd, AC, trip)
            with pool.Fori(0, TRIPS) as trip:
                each(rstd, MOE, trip)
            for s in both:
                pool.wait_ge(branch_psum[s], TRIPS * (MOE + 1))
            zeros_around_values()

            def second_attention(trip):
                for p in range(4):
                    split(pieces_during_A1(trip), p, trip, 4, PIECES_A1)
                    if p == 1:
                        each(rstd_qk, trip)
                    if p == 2:
                        for c in range(NCH):
                            each(mask_keys, trip, 1, c)

            with pool.Fori(0, TRIPS - 1) as trip:
                second_attention(trip)
                each(rstd, A1, trip)
            second_attention(TRIPS - 1)
            rest = pieces_from_A1()
            for s in both:
                pool.wait_ge(proj_psum[s], 3 * TRIPS)
            for p in range(KT - 1):
                split(rest, p, 0, len(rest), PIECES_XQ)
            each(rstd, A1, TRIPS - 1)
            for s in both:
                pool.wait_ge(branch_psum[s], TRIPS * (A1 + 1))
            for p in range(KT - 1, len(rest)):
                split(rest, p, 0, len(rest), PIECES_XQ)
            with pool.Fori(0, TRIPS) as trip:
                each(rstd, XA, trip)
            with pool.Fori(0, TRIPS) as trip:
                each(rstd, FF, trip)

        @block.vector
        def _(dve):
            DVE_STEPS = (22, 20, 20, 34, 38, 14)
            v = nc.vector
            taken = [0] * LAYERS

            def steps_done(y, trip, ins):
                taken[y] += 1
                ins.then_inc(dve_step, 1)
                dve.wait_ge(dve_step, nth(trip, DVE_STEPS[y], taken[y], TRIPS * sum(DVE_STEPS[:y])))

            def hold():
                dve.nop(nofuse=True)

            def xT_split(trip, s, y, ahead, b):
                dve.wait_ge(xT_hi[s], turned(trip, y, ahead))
                v.tensor_tensor(hTl[:, :, s, 1, :], tiles(bank[s][b][:, :]), f32(hTh[:, :, s, 1, :]), ALU.subtract
                                ).then_inc(xT_ready[s], 1)

            def v_first(trip, s):
                dve.wait_ge(v0_psum[s], one_of(trip))
                dve.wait_ge(consts_ready, 1 + 4 * SLOTS)
                for e in range(2):
                    ins = v.tensor_tensor(values_of(s, e), every_other(bank[s][2][:, :], e), every_other(bv_row, e), ALU.add)
                ins.then_inc(v_ready[s], 1)

            def qT_kT_first(trip):
                for i, dst in enumerate((qT, kT)):
                    for b in range(2):
                        dve.wait_ge(qk0_psum, nth(trip, 4, 2 * i + b + 1))
                        src = bank[i][b][:, :].rearrange("p (m s t) -> p m s t", m=2, s=SLOTS)
                        for s in both:
                            ins = v.tensor_tensor(tiles(dst[s])[:, 2 * b:2 * b + 2, :], src[:, :, s, :],
                                                  cols[:, i, 2 * b:2 * b + 2].unsqueeze(2).broadcast_to([P, 2, P]), ALU.add)
                    ins.then_inc(qk0_ready, 1)

            def clip_norm(trip, s):
                for i in range(2):
                    dve.wait_ge(proj_psum[s], nth(trip, 3, 1 + i))
                    steps_done(A1, trip, v.tensor_scalar(pp[s][i], bank[s][i][:, :], -8.0, 8.0, ALU.max, ALU.min))
                    bn = st[s][:, QKBN.start + 6 * i:QKBN.start + 6 * i + 6]
                    mv = st[s][:, QKMV.start + 2 * i:QKMV.start + 2 * i + 2]
                    steps_done(A1, trip, v.bn_stats(bn, pp[s][i]))
                    hold()
                    steps_done(A1, trip, v.bn_aggr(mv, bn))
                var = st[s][:, QKMV].rearrange("p (a b) -> p a b", b=2)[:, :, 1]
                v.tensor_scalar(var, var, EPS, None, ALU.add).then_inc(qk_var[s], 1)

            def v_second(trip, s):
                dve.wait_ge(proj_psum[s], nth(trip, 3, 3))
                dve.wait_ge(consts_ready, 1 + 5 * SLOTS)
                for e in range(2):
                    ins = v.tensor_scalar(values_of(s, e), every_other(bank[s][2][:, :], e), -8.0, 8.0, ALU.max, ALU.min)
                ins.then_inc(v_ready[s], 1)

            def apply_norm(trip, s):
                dve.wait_ge(qk_rstd[s], one_of(trip))
                for i in range(2):
                    ins = v.tensor_scalar(pp[s][i], pp[s][i], st[s][:, QKMV.start + 2 * i:QKMV.start + 2 * i + 1],
                                          st[s][:, QKRSTD.start + i:QKRSTD.start + i + 1], ALU.subtract, ALU.mult)
                ins.then_inc(qkn_ready[s], 1)

            def kT_second(trip, s):
                dve.wait_ge(qkT_psum[s], nth(trip, 2, 1))
                for m in range(KT):
                    ins = v.tensor_scalar(kT[s][:, m * P:(m + 1) * P], bank[s][1][:, m * P:(m + 1) * P],
                                          cols[:, 4, m:m + 1], cols[:, 5, m:m + 1], ALU.mult, ALU.add)
                ins.then_inc(kT_ready[s], 1)

            def maxima(trip, s, l, c):
                dve.wait_ge(scores_psum[s], chunk(trip, l, c + 1))
                if c >= 2:
                    dve.wait_ge(probsT_psum[s], chunk(trip, l, c - 1))
                hold()
                for j, h in enumerate(heads_of(c)):
                    ins = v.tensor_tensor_reduce(pp[s][c % 2][:, j * P:(j + 1) * P], bank[s][c % 2][:, j * P:(j + 1) * P],
                                                 (mask0, rel1)[l], 1.0, GONE, ALU.add, ALU.max,
                                                 st[s][:, ROWMAX.start + h:ROWMAX.start + h + 1])
                steps_done((A0, A1)[l], trip, ins)
                v.tensor_tensor(st[s][:, head_columns(NEGMAX, c)], st[s][:, head_columns(ROWMAX, c)],
                                neg_scale[l][:, head_columns(slice(0, H), c)], ALU.mult).then_inc(max_ready[s], 1)

            def probsT(trip, s, l, c):
                dve.wait_ge(probsT_psum[s], chunk(trip, l, c + 1))
                if c >= 2:
                    dve.wait_ge(pv_done[s], chunk(trip, l, c - 1))
                v.tensor_copy(pT[s][c % 2], bank[s][2][:, :]).then_inc(probsT_ready[s], 1)

            def reciprocal_sums(trip, s, l):
                dve.wait_ge(probs_ready[s], chunk(trip, l, NCH))
                v.reciprocal(st[s][:, ROWSUM], st[s][:, ROWSUM]).then_inc(sums_ready[s], 1)

            def heads(trip, s, l):
                dve.wait_ge(sumsT_ready[s], attn(trip, l))
                dve.wait_ge(pv_done[s], chunk(trip, l, NCH))
                v.tensor_tensor(hd[s], bank[s][3][:, :], sums[s], ALU.mult).then_inc(heads_ready[s], 1)

            def oT_split(trip, s, l):
                dve.wait_ge(oT_hi[s], attn(trip, l))
                v.tensor_tensor(hTl[:, :, s, 0, :], tiles(hd[s]), f32(hTh[:, :, s, 0, :]), ALU.subtract).then_inc(oT_ready[s], 1)

            def residual(y, trip, s, at):
                dve.wait_ge(branch_psum[s], seq(trip, y))
                if y == A0:
                    dve.wait_ge(x_biased, nth(trip, SLOTS, s + 1))
                else:
                    dve.wait_ge(r_loaded[s], nth(trip, 16, 16, 16 * y * TRIPS))
                steps_done(y, trip, v.tensor_tensor(xres[s][:, :], bank[s][at][:, :], xres[s][:, :], ALU.add))
                steps_done(y, trip, v.bn_stats(st[s][:, BN], xres[s][:, :]))
                hold()
                steps_done(y, trip, v.bn_aggr(st[s][:, MV], st[s][:, BN]))
                var = st[s][:, MV][:, 1:2]
                v.tensor_scalar(var, var, EPS, None, ALU.add).then_inc(ln_var[s], 1)

            def norm_x(y, trip, s):
                dve.wait_ge(ln_rstd[s], seq(trip, y))
                v.tensor_scalar(xres[s][:, :], xres[s][:, :], st[s][:, MV][:, 0:1], st[s][:, RSTD], ALU.subtract, ALU.mult
                                ).then_inc(x_ready[s], 1)

            def cross_products(trip, s):
                dve.wait_ge(xf_psum[s], one_of(trip))
                dve.wait_ge(ctxf_ready[s], nth(trip, 4, 2))
                v.tensor_tensor(pr[s][0], bank[s][3][:, :], spec[s][0], ALU.mult)
                v.tensor_tensor(pr[s][1], bank[s][3][:, :], spec[s][1], ALU.mult).then_inc(cross_ready[s], 1)

            def top_lags(trip, s):
                dve.wait_ge(corr_psum[s], one_of(trip))
                hold()
                m8 = st[s][:, NEGMAX].rearrange("p (k e) -> p k e", k=KT)
                n8 = st[s][:, ROWMAX].rearrange("p (k e) -> p k e", k=KT)
                for m in range(KT):
                    ins = v.max(m8[:, m, :], bank[s][2][:, m * P:(m + 1) * P])
                steps_done(AC, trip, ins)
                steps_done(AC, trip, v.tensor_scalar(st[s][:, LAGNEG], m8[:, :, 0], -1.0, None, ALU.mult))
                hold()
                for m in range(KT):
                    ins = v.match_replace(lagv[s][:, m * P:(m + 1) * P], m8[:, m, :], bank[s][2][:, m * P:(m + 1) * P], GONE)
                ins.then_inc(lagmax_ready[s], 1)
                dve.wait_ge(lagmax_ready[s], one_of(trip))
                hold()
                for m in range(KT):
                    ins = v.max(n8[:, m, :], lagv[s][:, m * P:(m + 1) * P])
                steps_done(AC, trip, ins)
                steps_done(AC, trip, v.tensor_copy(lag2[s][:, :, 0:TOPK - 8], n8[:, :, 0:TOPK - 8]))
                hold()
                for m in range(KT):
                    ins = v.match_replace(lagv[s][:, m * P:(m + 1) * P], lag2[s][:, m, :], lagv[s][:, m * P:(m + 1) * P], GONE)
                steps_done(AC, trip, ins)

            def lag_softmax(trip, s):
                dve.wait_ge(lagexp_ready[s], one_of(trip))
                for m in range(KT):
                    at = slice(m * P, (m + 1) * P)
                    ins = v.scalar_tensor_tensor(out=lage[s][:, at], in0=lagv[s][:, at], scalar=PICKED, in1=lage[s][:, at],
                                                 op0=ALU.is_le, op1=ALU.mult,
                                                 accum_out=st[s][:, LAGSUM.start + m:LAGSUM.start + m + 1])
                steps_done(AC, trip, ins)
                steps_done(AC, trip, v.reciprocal(st[s][:, LAGSUM], st[s][:, LAGSUM]))
                v.tensor_tensor(tiles(pr[s][0]), tiles(lage[s]), st[s][:, LAGSUM].unsqueeze(2).broadcast_to([P, KT, P]), ALU.mult
                                ).then_inc(lagw_ready[s], 1)

            def shift_products(trip, s):
                dve.wait_ge(ctxf_ready[s], nth(trip, 4, 4))
                dve.wait_ge(lagf_psum[s], nth(trip, 2, 2))
                for i, (d0, d1) in enumerate(((lagv[s], lage[s]), pr[s])):
                    src = bank[s][(3, 0)[i]][:, :]
                    v.tensor_tensor(d0, src, spec[s][2 * i], ALU.mult)
                    v.tensor_tensor(d1, src, spec[s][2 * i + 1], ALU.mult).then_inc(shift_ready[s], 1)

            def top_gates(trip, s):
                dve.wait_ge(mix_psum[s], mix(trip, MOE))
                logits = gates[s][:, 0, :]
                steps_done(MOE, trip, v.tensor_copy(logits[:, 0:NE], bank[s][0][:, 0:NE]))
                hold()
                steps_done(MOE, trip, v.max(st[s][:, TOP2], logits))
                v.tensor_scalar(st[s][:, ONE_A], st[s][:, TOP2][:, 0:1], -1.0, None, ALU.mult).then_inc(mixmax_ready[s], 1)
                steps_done(MOE, trip, v.tensor_copy(gate2[s][:, 0:2], st[s][:, TOP2][:, 0:2]))
                hold()
                steps_done(MOE, trip, v.match_replace(gates[s][:, 1, :], gate2[s][:, :], logits, GONE))

            def gated(trip, s):
                dve.wait_ge(mixexp_ready[s], mix(trip, MOE))
                e = gates[s][:, 2, 0:NE]
                steps_done(MOE, trip, v.scalar_tensor_tensor(out=e, in0=gates[s][:, 1, 0:NE], scalar=PICKED, in1=e,
                                                             op0=ALU.is_le, op1=ALU.mult, accum_out=st[s][:, ONE_B]))
                steps_done(MOE, trip, v.reciprocal(st[s][:, ONE_C], st[s][:, ONE_B]))
                steps_done(MOE, trip, v.tensor_scalar(e, e, st[s][:, ONE_C], 16.0 / ER, ALU.mult, ALU.mult))
                v.tensor_tensor(hg[s].rearrange("p (e r) -> p e r", e=NE), bank[s][0][:, NE:NG].rearrange("p (e r) -> p e r", e=NE),
                                e.unsqueeze(2).broadcast_to([P, NE, ER]), ALU.mult).then_inc(mixed_ready[s], 1)

            def gated_split(trip, s):
                dve.wait_ge(mixedT_hi[s], mix(trip, MOE))
                n = GH * ER
                v.tensor_tensor(hTl[0:n, 0:2, s, 0, :], tiles(bank[s][2][0:n, 0:2 * P], 2), f32(hTh[0:n, 0:2, s, 0, :]),
                                ALU.subtract).then_inc(mixedT_ready[s], 1)

            def context_split(trip, s):
                dve.wait_ge(cT_hi[s], one_of(trip))
                v.tensor_tensor(hTl[:, :, s, 0, :], tiles(cin[s][:, :]), f32(hTh[:, :, s, 0, :]), ALU.subtract
                                ).then_inc(cT_ready[s], 1)

            def cross_qT(trip, s, g):
                dve.wait_ge(xqT_psum[s], nth(trip, XKV, g + 1))
                v.tensor_copy(xqT[s], bank[s][2][0:XD, :]).then_inc(xqT_ready[s], 1)

            def cross_max(trip, s, g):
                for i in range(2):
                    dve.wait_ge(xs_psum[s], nth(trip, 2 * XKV, 2 * g + i + 1))
                    r = st[s][:, ROWMAX.start + 2 * i:ROWMAX.start + 2 * i + 2]
                    steps_done(XA, trip, v.tensor_reduce(r, bank[s][i][:, :].rearrange("p (h t) -> p h t", h=2), AX, ALU.max))
                    v.tensor_scalar(st[s][:, NEGMAX.start + 2 * i:NEGMAX.start + 2 * i + 2], r, -(XD ** -0.5), None, ALU.mult
                                    ).then_inc(xmax_ready[s], 1)

            def cross_probsT(trip, s, g):
                for i in range(2):
                    dve.wait_ge(xpT_psum[s], nth(trip, 2 * XKV, 2 * g + i + 1))
                    v.tensor_copy(xpT[s][:, i * 512:(i + 1) * 512], bank[s][i][:, :]).then_inc(xpT_ready[s], 1)

            def cross_norm(trip, s, g):
                for i in range(2):
                    dve.wait_ge(xp_ready[s], nth(trip, 2 * XKV, 2 * g + i + 1))
                    sums = st[s][:, ROWSUM.start + 2 * i:ROWSUM.start + 2 * i + 2]
                    steps_done(XA, trip, v.reciprocal(sums, sums))
                    for j in range(2):
                        block = xp[s][:, (2 * i + j) * XT:(2 * i + j + 1) * XT]
                        ins = v.tensor_scalar(block, block, sums[:, j:j + 1], None, ALU.mult)
                    ins.then_inc(xpn_ready[s], 1)

            def cross_heads(trip, s, g):
                dve.wait_ge(xo_hi[s], nth(trip, XKV, g + 1))
                n = XG * XD // P
                v.tensor_tensor(hTl[:, 0:n, s, 0, :], tiles(bank[s][0][:, 0:XG * XD], n), f32(hTh[:, 0:n, s, 0, :]), ALU.subtract
                                ).then_inc(xo_ready[s], 1)

            def routes(trip, s):
                dve.wait_ge(mix_psum[s], mix(trip, FF))
                e = st[s][:, EIGHT]
                steps_done(FF, trip, v.tensor_tensor(e, bank[s][0][:, LH * LR:NL], br_row[:, :], ALU.add))
                steps_done(FF, trip, v.tensor_reduce(st[s][:, ONE_C], e, AX, ALU.max))
                v.tensor_scalar(st[s][:, ONE_A], st[s][:, ONE_C], -1.0, None, ALU.mult).then_inc(mixmax_ready[s], 1)

            def routed(trip, s):
                dve.wait_ge(mixexp_ready[s], mix(trip, FF))
                e = st[s][:, EIGHT]
                steps_done(FF, trip, v.reciprocal(st[s][:, ONE_C], st[s][:, ONE_B]))
                steps_done(FF, trip, v.tensor_scalar(e, e, st[s][:, ONE_C], LH * 32.0 / LR, ALU.mult, ALU.mult))
                v.tensor_tensor(low[s].rearrange("p (h r) -> p h r", h=LH), bank[s][0][:, 0:LH * LR].rearrange("p (h r) -> p h r", h=LH),
                                e.unsqueeze(2).broadcast_to([P, LH, LR]), ALU.mult).then_inc(mixed_ready[s], 1)

            def low_split(trip, s):
                dve.wait_ge(mixedT_hi[s], mix(trip, FF))
                v.tensor_tensor(hTl[:, 0, s, 0, :], bank[s][2][:, 0:P], f32(hTh[:, 0, s, 0, :]), ALU.subtract
                                ).then_inc(mixedT_ready[s], 1)

            def each(step, trip, *args):
                for s in both:
                    step(trip, s, *args)

            def self_attention(trip, l):
                for c in range(NCH):
                    each(maxima, trip, l, c)
                    if c == 0:
                        (v_first, v_second)[l](trip, 1)
                    else:
                        each(probsT, trip, l, c - 1)
                each(reciprocal_sums, trip, l)
                each(probsT, trip, l, NCH - 1)
                each(heads, trip, l)
                each(oT_split, trip, l)

            def close_layer(y, trip, at):
                for s in both:
                    residual(y, trip, s, at)
                for s in both:
                    norm_x(y, trip, s)

            dve.wait_ge(ld_masks, 16)
            dve.wait_ge(ld_c, 64)
            dve.wait_ge(consts_ready, 1 + 3 * SLOTS)
            for s in both:
                dve.wait_ge(stored[s], 16)
            for i in (2, 3):
                v.tensor_tensor(cols[:, i, :], cols[:, i, :], q_scale, ALU.mult).then_inc(w0_ready, 1)
            dve.wait_ge(w0_ready, 2)
            each(xT_split, 0, A0, 0, 1)
            for i in range(4):
                dve.wait_ge(w0_hi, i + 1)
                w = w_qkv0[i] if i < 3 else w_o0
                v.tensor_tensor(w[1], tiles(tank[i // 2][:, i % 2 * KT * D:(i % 2 + 1) * KT * D]), f32(w[0]), ALU.subtract
                                ).then_inc(w0_ready, 1)

            def first_layer(trip, more):
                qT_kT_first(trip)
                v_first(trip, 0)
                self_attention(trip, 0)
                if more:
                    each(xT_split, trip, A0, 1, 1)
                close_layer(A0, trip, 3)

            def last_layer(trip, more):
                each(routes, trip)
                each(routed, trip)
                if more:
                    each(xT_split, trip, FF, 1, 1)
                each(low_split, trip)
                close_layer(FF, trip, 3)

            dve.wait_ge(w0_ready, 2 + 4)
            with dve.Fori(0, TRIPS - 1) as trip:
                first_layer(trip, True)
            taken[A0] = 0
            first_layer(TRIPS - 1, False)
            with dve.Fori(0, TRIPS) as trip:
                each(cross_products, trip)
                for s in both:
                    top_lags(trip, s)
                    lag_softmax(trip, s)
                each(shift_products, trip)
                close_layer(AC, trip, 1)
            each(xT_split, 0, MOE, 0, 3)
            with dve.Fori(0, TRIPS) as trip:
                each(top_gates, trip)
                each(gated, trip)
                each(xT_split, trip, MOE, 1, 3)
                each(gated_split, trip)
                close_layer(MOE, trip, 1)
            with dve.Fori(0, TRIPS) as trip:
                for step in (clip_norm, apply_norm, kT_second):
                    each(step, trip)
                v_second(trip, 0)
                self_attention(trip, 1)
                each(xT_split, trip, A1, 1, 1)
                close_layer(A1, trip, 3)
            with dve.Fori(0, TRIPS) as trip:
                each(context_split, trip)
                each(cross_qT, trip, 0)
                for g in range(XKV):
                    each(cross_max, trip, g)
                    each(cross_norm, trip, g)
                    if g + 1 == XKV:
                        each(xT_split, trip, XA, 1, 2)
                    each(cross_probsT, trip, g)
                    if g + 1 < XKV:
                        each(cross_qT, trip, g + 1)
                    each(cross_heads, trip, g)
                close_layer(XA, trip, 3)
            with dve.Fori(0, TRIPS - 1) as trip:
                last_layer(trip, True)
            taken[FF] = 0
            last_layer(TRIPS - 1, False)
            assert tuple(taken) == DVE_STEPS, taken


def features_first(w):
    n, k = w.shape
    return np.ascontiguousarray(w.T.reshape(k // P, P, n).transpose(1, 0, 2))


def kernel(**inputs):
    import concourse.bacc as bacc
    from concourse.bass_utils import run_bass_kernel_spmd

    i = {k: np.asarray(v) for k, v in inputs.items()}
    consts, slopes = shape_constants()
    turned = i["ctx_4096"].transpose(0, 2, 1).reshape(B, KT, P, L).transpose(0, 2, 1, 3).reshape(B, P, D)
    by_feature = lambda b: b.reshape(KT, P).T
    lora_a = i["L0_ffn_lora_A"].reshape(NE * ER, D)
    lora_b = i["L0_ffn_lora_B"].transpose(0, 2, 1).reshape(2, GH * ER, D).transpose(1, 0, 2)
    head = np.arange(XH).reshape(XKV, XG, 1) * XD
    by_column_tile = np.concatenate([(head + part).reshape(XKV, -1) for part in (np.arange(WIDE), np.arange(WIDE, XD))], 1).ravel()
    arrays = {
        "x": i["x"], "ctx": i["ctx_4096"], "ctxT": turned,
        **{"w0_" + n: features_first(i[f"L0_attn_W{n}"]).reshape(P, KT * D) for n in "qkvo"},
        "cols": np.stack([by_feature(i[n]) for n in (
            "L0_attn_bq", "L0_attn_bk", "L1_attn_q_ln_w", "L1_attn_q_ln_b",
            "L1_attn_k_ln_w", "L1_attn_k_ln_b")], 1),
        "bo": i["L0_attn_bo"], "bv": i["L0_attn_bv"], "br": i["L1_ffn_br"],
        "w_gl": features_first(np.concatenate([i["L0_ffn_gate_W"], lora_a], 0)),
        "w_base": features_first(i["L0_ffn_base_W"]),
        "w_lb": lora_b,
        "w_qkv1": features_first(i["L1_attn_Wqkv"]),
        "w_o1": features_first(i["L1_attn_Wout"]),
        "w_xq": features_first(i["L1_xattn_Wq"]), "w_xk": features_first(i["L1_xattn_Wk"]),
        "w_xv": features_first(i["L1_xattn_Wv"]), "w_xo": features_first(i["L1_xattn_Wo"][:, by_column_tile]),
        "w_al": features_first(np.concatenate([i["L1_ffn_A"].reshape(LH * LR, D), i["L1_ffn_Wr"]], 0)),
        "w_bl": i["L1_ffn_B"].transpose(0, 2, 1).reshape(LH * LR, 1, D),
        **consts,
    }
    arrays = {k: np.ascontiguousarray(v) for k, v in arrays.items()}
    arrays["dft"] = arrays["dft"].reshape(P, 12 * P)
    nc = bacc.Bacc("TRN2", target_bir_lowering=False, num_devices=1)
    aps = {k: nc.dram_tensor(f"{k}_dram", v.shape, F32, kind="ExternalInput").ap() for k, v in arrays.items()}
    out = nc.dram_tensor("out_dram", (B, L, D), F32, kind="ExternalOutput").ap()
    decoder(nc, aps, out, slopes)
    r = run_bass_kernel_spmd(nc, [{f"{k}_dram": v for k, v in arrays.items()}], core_ids=[0])
    return r.results[0]["out_dram"]
```

```python
from contextlib import ExitStack

import numpy as np
import concourse.bass as bass
from concourse import mybir

F32 = mybir.dt.float32
F32R = mybir.dt.float32r
ALU = mybir.AluOpType
ACT = mybir.ActivationFunctionType
AX = mybir.AxisListType.X

P = 128
B, L, D = 8, 128, 512
KT = D // P
SLOTS = 2
TRIPS = B // SLOTS
LAYERS = 6

H, HD = 32, 16
HT = P // HD
PAD = 2 * HD
CH = 4
NCH = H // CH
XH, XKV, XD = 16, 4, 96
XG = XH // XKV
WIDE, NARROW = 64, 32
XT = 2 * L
TOPK = int(2 * np.log(L))
NE, ER = 28, 8
GH = NE // 2
LH, LR = 8, 16
EPS = 1e-5
GONE = -3.0e38
PICKED = -1.0e38

TANK = 4096
PIECE = 512


def shape_constants():
    t = np.arange(L)
    ck, sk = np.arange(L // 2 + 1), np.arange(1, L // 2)
    cos_e = lambda n, f: np.cos(2 * np.pi * np.outer(n, f) / L)
    sin_e = lambda n, f: np.sin(2 * np.pi * np.outer(n, f) / L)
    same = np.concatenate([cos_e(t, ck), sin_e(t, sk)], 1)
    swap = np.concatenate([sin_e(t, ck), cos_e(t, sk)], 1)
    weight = np.where((ck == 0) | (ck == L // 2), 1.0, 2.0)
    inv1 = np.concatenate([weight * cos_e(t, ck), 2 * cos_e(t, sk)], 1).T / L
    inv2 = np.concatenate([-weight * sin_e(t, ck), 2 * sin_e(t, sk)], 1).T / L
    ctx_even = same.copy()
    ctx_even[L - 1, 0] += L
    odd = np.arange(1, 2 * L, 2)[: L // 2]
    ang = lambda n: 2 * np.pi * np.outer(n, odd) / (2 * L)
    lag_odd = np.concatenate([np.cos(ang(t)), np.sin(ang(t))], 1)
    full = np.arange(2 * L)
    co, so = np.cos(ang(full)), np.sin(ang(full))
    hold = lambda m: np.concatenate([m[: L - 1], m[L - 1:].sum(0, keepdims=True)], 0)
    ctx_odd = np.concatenate([hold(co), hold(so)], 1)
    ctx_odd_swap = np.concatenate([hold(so), hold(co)], 1)
    oute1 = np.concatenate([weight * cos_e(t, ck), 2 * cos_e(t, sk)], 1).T / (2 * L)
    oute2 = np.concatenate([weight * sin_e(t, ck), -2 * sin_e(t, sk)], 1).T / (2 * L)
    outo1 = np.concatenate([2 * np.cos(ang(t)), 2 * np.cos(ang(t))], 1).T / (2 * L)
    outo2 = np.concatenate([2 * np.sin(ang(t)), -2 * np.sin(ang(t))], 1).T / (2 * L)
    tables = [same, ctx_even, swap, ctx_odd, ctx_odd_swap, lag_odd, inv1, inv2, oute1, oute2, outo1, outo2]
    dft = np.stack(tables, 1).astype(np.float32)

    slopes = (1.0 / np.power(2.0, np.arange(1, H + 1, dtype=np.float32) * (8.0 / H))).astype(np.float64)
    rel = t[None, :] - t[:, None]
    causal = rel <= 0
    masks = np.stack([np.eye(P), np.where(causal, 0.0, -1e30), np.where(causal, rel, -1e36)], 1)
    even_odd = np.concatenate([np.arange(e, HT, 2) for e in range(HT // CH)])
    head_rows = (np.arange(P)[:, None] // HD == even_odd[None, :]).astype(np.float32)
    neg_scale = np.stack([np.full(H, -1.0 / np.sqrt(HD)), -slopes], 0)
    row_head = np.arange(KT)[None, :] * HT + np.arange(P)[:, None] // HD
    q_scale = (1.0 / np.sqrt(HD)) / slopes[row_head]
    small = np.concatenate([head_rows, np.broadcast_to(neg_scale.reshape(1, -1), (P, 2 * H)), q_scale], 1)
    return {
        "dft": dft, "masks": masks.astype(np.float32),
        "small": np.ascontiguousarray(small.astype(np.float32)),
    }, [float(s) for s in slopes]


def nth(trip, per_trip, j, before=0):
    return trip * per_trip + (j + before)


def decoder(nc, a, out, slopes):
    A0, AC, MOE, A1, XA, FF = range(LAYERS)
    NORMED_BY_ACT = (FF,)
    TURNED = {A0: 0, MOE: 1, A1: 2, XA: 3, FF: 4}
    es = ExitStack()
    with es:
        def sb(name, shape, dt=F32):
            return es.enter_context(nc.sbuf_tensor(name, shape, dt))

        def sem(name):
            return es.enter_context(nc.semaphore(name))

        def per_slot(name):
            return [sem(f"{name}{s}") for s in range(SLOTS)]

        both = range(SLOTS)
        NG = NE + NE * ER
        NX, NKV = XH * XD, XKV * XD
        NXO = NX // P
        NL = LH * LR + LH

        WORDS = 32832
        wr = sb("wr", [P, WORDS], F32R)

        def region(at, k, n, parts=P):
            hi = wr[0:parts, at:at + k * n].rearrange("p (k n) -> p k n", k=k)
            lo = wr[0:parts, at + k * n:at + 2 * k * n].rearrange("p (k n) -> p k n", k=k)
            return hi, lo

        LOW, HIGH = 0, 16384
        AT_Q0, AT_O0 = LOW, LOW + 3 * 2 * KT * D
        AT_GL = HIGH
        AT_BASE = AT_GL + 2 * KT * NG
        AT_LB = AT_BASE + 2 * KT * D
        AT_QKV1 = LOW
        AT_O1 = AT_QKV1 + 2 * KT * 3 * D
        AT_XQ = HIGH
        AT_XK = AT_XQ + 2 * KT * NX
        AT_AL = AT_XK + 2 * KT * NKV
        AT_XV = LOW
        AT_XO = AT_XV + 2 * KT * NKV
        AT_BL = AT_XO + 2 * NXO * D
        w_qkv0 = [region(AT_Q0 + i * 2 * KT * D, KT, D) for i in range(3)]
        w_o0 = region(AT_O0, KT, D)
        w_gl, w_base = region(AT_GL, KT, NG), region(AT_BASE, KT, D)
        w_lb = region(AT_LB, 2, D, GH * ER)
        w_qkv1, w_o1 = region(AT_QKV1, KT, 3 * D), region(AT_O1, KT, D)
        w_xq, w_xk = region(AT_XQ, KT, NX), region(AT_XK, KT, NKV)
        w_xv, w_xo = region(AT_XV, KT, NKV), region(AT_XO, NXO, D)
        w_al, w_bl = region(AT_AL, KT, NL), region(AT_BL, 1, D)
        raw = [sb(f"raw{i}", [P, max(PIECE, KT * NL)]) for i in range(2)]

        table = sb("table", [P, 12 * P])
        bo_row, bv_row = table[:, 0:D], table[:, D:2 * D]
        (DX, DC, DCS, DO, DOS, DL, I1, I2, E1, E2, O1, O2) = [table[:, i * P:(i + 1) * P] for i in range(12)]
        cols = sb("cols_sb", [P, 6, KT])
        br_row = sb("br_row", [P, LH])
        masks = sb("masks_sb", [P, 3, P])
        small = sb("small_sb", [P, HT + 2 * H + KT])
        ident, mask0, rel1 = (masks[:, i, :] for i in range(3))
        head_rows = small[:, 0:HT]
        neg_scale = [small[:, HT + H * l:HT + H * (l + 1)] for l in range(2)]
        q_scale = small[:, HT + 2 * H:]
        half = sb("half", [P, 2])

        xin = [sb(f"xin{s}", [P, D]) for s in both]
        xres = [sb(f"xres{s}", [P, D]) for s in both]
        cin = [sb(f"cin{s}", [P, D]) for s in both]
        tank = [sb(f"tank{s}", [P, TANK]) for s in both]
        st = [sb(f"stats{s}", [P, 160]) for s in both]
        lag2 = [sb(f"lag2_{s}", [P, KT, 8]) for s in both]
        gate2 = [sb(f"gate2_{s}", [P, 8]) for s in both]
        gates = [sb(f"gates{s}", [P, 3, NE + 8]) for s in both]
        hTh = sb("hTh", [P, KT, SLOTS, 2, P], F32R)
        hTl = sb("hTl", [P, KT, SLOTS, 2, P], F32R)
        xk_split = sb("xk_split", [XD, SLOTS, 2, XT], F32R)
        bank = [[es.enter_context(nc.psum_tensor(f"bank{s}_{i}", [P, 512], F32)) for i in range(4)] for s in both]
        between = [nc.dram_tensor(f"between{i}", (B, L, D), F32, kind="Internal").ap() for i in range(2)]

        def view(s, at, n, parts=P):
            return tank[s][0:parts, at:at + n]

        qT = [view(s, 0, 512) for s in both]
        kT = [cin[s][:, :] for s in both]
        kM = [view(s, 512, 512) for s in both]
        pp = [[view(s, 1024 + 512 * i, 512) for i in range(2)] for s in both]
        pT = [[view(s, 2048 + 512 * i, 512) for i in range(2)] for s in both]
        vv = [view(s, 3072, H * PAD) for s in both]
        sums, hd = ([pp[s][i] for s in both] for i in range(2))

        def values_of(s, e):
            return vv[s].rearrange("p (h x) -> p h x", x=2 * PAD)[:, :, e * (PAD + HD):e * (PAD + HD) + HD]

        def every_other(ap, e):
            return ap.rearrange("p (h e d) -> p h e d", e=2, d=HD)[:, :, e, :]
        spec = [[view(s, 512 * i, 512) for i in range(4)] for s in both]
        pr = [[view(s, 2048 + 512 * i, 512) for i in range(2)] for s in both]
        lagv = [view(s, 3072, 512) for s in both]
        lage = [view(s, 3584, 512) for s in both]
        hg = [view(s, 0, NE * ER) for s in both]
        low = [view(s, 0, P) for s in both]
        xkT = [view(s, 0, XKV * XT, XD) for s in both]
        xv = [view(s, 1024, 2 * NKV) for s in both]
        xp = [view(s, 1792, XG * XT) for s in both]
        xpT = [view(s, 2816, XG * XT) for s in both]
        xqT = [region(at, 1, XG * P, XD) for at in (AT_AL, AT_BL)]
        xks = [(xk_split[:, s, 0, :], xk_split[:, s, 1, :]) for s in both]
        places = ([(j * WIDE // P, j * WIDE % P, j, 0, WIDE) for j in range(4)]
                  + [(4 * WIDE // P, j * NARROW, j, WIDE, NARROW) for j in range(4)])
        xq = [cin[s][:, 0:XG * XD] for s in both]

        ld_w0 = [sem(f"ld_w0_{n}") for n in "qkvo"]
        ld_masks = sem("ld_masks")
        ld_c = sem("ld_c")
        consts_ready = sem("consts_ready")
        w0_hi = sem("w0_hi")
        w0_ready = sem("w0_ready")
        raw_loaded = [sem(f"raw_loaded{i}") for i in range(2)]
        w_split = sem("w_split")
        w_hi = sem("w_hi")
        w_hi_rest = sem("w_hi_rest")
        dve_step = sem("dve_step")
        x_loaded = per_slot("x_loaded")
        c_loaded = per_slot("c_loaded")
        stored = per_slot("stored")
        r_loaded = per_slot("r_loaded")
        x_biased = sem("x_biased")
        xT_psum = per_slot("xT_psum")
        xT_hi = per_slot("xT_hi")
        xT_ready = per_slot("xT_ready")
        branch_psum = per_slot("branch_psum")
        ln_var = per_slot("ln_var")
        ln_rstd = per_slot("ln_rstd")
        x_ready = per_slot("x_ready")
        qk0_psum = sem("qk0_psum")
        qk0_ready = sem("qk0_ready")
        v0_psum = per_slot("v0_psum")
        proj_psum = per_slot("proj_psum")
        qkn_ready = per_slot("qkn_ready")
        qk_var = per_slot("qk_var")
        qk_rstd = per_slot("qk_rstd")
        qkT_psum = per_slot("qkT_psum")
        qT_ready = per_slot("qT_ready")
        kT_ready = per_slot("kT_ready")
        v_ready = per_slot("v_ready")
        kM_ready = per_slot("kM_ready")
        scores_psum = per_slot("scores_psum")
        max_ready = per_slot("max_ready")
        probs_ready = per_slot("probs_ready")
        probsT_psum = per_slot("probsT_psum")
        probsT_ready = per_slot("probsT_ready")
        pv_done = per_slot("pv_done")
        sums_ready = per_slot("sums_ready")
        sumsT_psum = per_slot("sumsT_psum")
        sumsT_ready = per_slot("sumsT_ready")
        heads_ready = per_slot("heads_ready")
        oT_ready = per_slot("oT_ready")
        ctxf_psum = per_slot("ctxf_psum")
        ctxf_ready = per_slot("ctxf_ready")
        xf_psum = per_slot("xf_psum")
        cross_ready = per_slot("cross_ready")
        corr_psum = per_slot("corr_psum")
        lagmax_ready = per_slot("lagmax_ready")
        lagexp_ready = per_slot("lagexp_ready")
        lagw_ready = per_slot("lagw_ready")
        lagwT_psum = per_slot("lagwT_psum")
        lagwT_ready = per_slot("lagwT_ready")
        lagf_psum = per_slot("lagf_psum")
        shift_ready = per_slot("shift_ready")
        mix_psum = per_slot("mix_psum")
        mixmax_ready = per_slot("mixmax_ready")
        mixexp_ready = per_slot("mixexp_ready")
        mixed_ready = per_slot("mixed_ready")
        mixedT_psum = per_slot("mixedT_psum")
        mixedT_ready = per_slot("mixedT_ready")
        inner_hi = per_slot("inner_hi")
        cT_ready = per_slot("cT_ready")
        xk_psum = sem("xk_psum")
        xk_ready = sem("xk_ready")
        xv_psum = per_slot("xv_psum")
        xv_ready = per_slot("xv_ready")
        xq_psum = per_slot("xq_psum")
        xq_ready = per_slot("xq_ready")
        xqT_psum = per_slot("xqT_psum")
        xqk_hi = per_slot("xqk_hi")
        xqk_ready = per_slot("xqk_ready")
        xs_psum = per_slot("xs_psum")
        xmax_ready = per_slot("xmax_ready")
        xp_ready = per_slot("xp_ready")
        xpn_ready = per_slot("xpn_ready")
        xpT_psum = per_slot("xpT_psum")
        xpT_ready = per_slot("xpT_ready")
        xo_psum = per_slot("xo_psum")
        xo_hi = per_slot("xo_hi")
        xo_ready = per_slot("xo_ready")

        FREE = len(raw)
        PIECES_A0 = 2 * TRIPS
        PIECES_MOE = PIECES_A0 + 2
        PIECES_A1 = PIECES_MOE + 4 * TRIPS
        PIECES_XQ = PIECES_A1 + 4 * TRIPS
        PIECES_XV = PIECES_XQ + KT
        PIECES_XO = PIECES_XV + NXO
        PIECES_FF = PIECES_XO + 2

        BN, MV, RSTD, SHIFT = slice(0, 6), slice(6, 8), slice(8, 9), slice(9, 10)
        QKBN, QKMV, QKRSTD = slice(12, 24), slice(24, 28), slice(28, 30)
        NEGMAX, ROWMAX, ROWSUM = slice(32, 64), slice(64, 96), slice(96, 128)
        LAGNEG, LAGSUM = slice(128, 132), slice(132, 136)
        TOP2 = slice(136, 144)
        ONE_A, ONE_B, ONE_C = slice(144, 145), slice(145, 146), slice(146, 147)
        EIGHT = slice(148, 156)

        def seq(trip, y, j=1):
            return nth(trip, 1, j, y * TRIPS)

        def turned(trip, y, ahead=0):
            return nth(trip, 1, 1 + ahead, TURNED[y] * TRIPS)

        def normed(trip, y, j):
            per_trip = [2 if z in NORMED_BY_ACT else 1 for z in range(LAYERS)]
            return nth(trip, per_trip[y], j, TRIPS * sum(per_trip[:y]))

        def one_of(trip):
            return nth(trip, 1, 1)

        def heads_of(c):
            first = c * CH // HT * HT + c % (HT // CH)
            return range(first, first + HT - HT // CH + 1, HT // CH)

        def head_columns(at, c):
            h = heads_of(c)
            return slice(at.start + h.start, at.start + h.stop, h.step)

        def chunk(trip, l, j):
            return nth(trip, NCH, j, l * TRIPS * NCH)

        def attn(trip, l):
            return nth(trip, 1, 1, l * TRIPS)

        def mix(trip, y):
            return nth(trip, 1, 1, TRIPS if y == FF else 0)

        def f32(ap):
            return ap.bitcast(F32)

        def tiles(ap, k=KT):
            return ap.rearrange("p (k t) -> p k t", k=k)

        def raw_w0(i, e):
            return tiles(tank[i // 2][:, i % 2 * KT * D:(i % 2 + 1) * KT * D])[:, :, e * D // 2:(e + 1) * D // 2]

        def half_w0(i, lo, e):
            return (*w_qkv0, w_o0)[i][lo][:, :, e * D // 2:(e + 1) * D // 2]

        def tile_of(name, at, n, trip):
            count = -(-n // PIECE)
            w = n // count
            return [(a[name][:, bass.ds(trip, 1), j * w:(j + 1) * w].rearrange("p k n -> p (k n)"), w, P,
                     trip * n + (at + j * w), KT * n) for j in range(count)]

        def all_tiles(name, at, k, n, parts=P):
            return [(a[name][:, i, :], n, parts, at + i * n, k * n) for i in range(k)]

        def pieces_during_A0(trip):
            return tile_of("w_gl", AT_GL, NG, trip) + tile_of("w_base", AT_BASE, D, trip)

        def pieces_after_A0():
            return all_tiles("w_lb", AT_LB, 2, D, GH * ER)

        def pieces_during_AC(trip):
            return tile_of("w_qkv1", AT_QKV1, 3 * D, trip) + tile_of("w_o1", AT_O1, D, trip)

        def pieces_during_A1(trip):
            return tile_of("w_xq", AT_XQ, NX, trip) + tile_of("w_xk", AT_XK, NKV, trip)

        def pieces_from_A1():
            return (all_tiles("w_xv", AT_XV, KT, NKV) + all_tiles("w_xo", AT_XO, NXO, D)
                    + [(a["w_al"].rearrange("p k n -> p (k n)"), KT * NL, P, AT_AL, KT * NL)] + all_tiles("w_bl", AT_BL, 1, D))

        def halves(pieces, p):
            _, n, parts, at, span = pieces[p]
            return raw[p % 2][0:parts, 0:n], wr[0:parts, bass.ds(at, n)], wr[0:parts, bass.ds(at + span, n)]

        def loaded_piece(p, trip, per_trip, before):
            return nth(trip, 8 * per_trip, 16 * (p // 2 + 1), 8 * before)

        block = es.enter_context(nc.Block())

        @block.sync
        def _(sp):
            def row(src, b):
                return src[bass.ds(b, 1)].rearrange("b p d -> (b p) d")

            def load_x(src, b, s):
                sp.dma_start(xin[s][:, :], row(src, b)).then_inc(x_loaded[s], 16)

            def load_residual(src, b, s):
                sp.dma_start(xres[s][:, :], row(src, b)).then_inc(r_loaded[s], 16)

            def fetch(pieces, trip, per_trip, before, which):
                for p, (src, n, parts, _, _) in list(enumerate(pieces))[which]:
                    sp.wait_ge(w_split, nth(trip, per_trip, FREE + p - 1, before))
                    hold()
                    sp.dma_start(raw[p % 2][0:parts, 0:n], src).then_inc(raw_loaded[p % 2], 16)

            def load_context(src, b, s):
                sp.dma_start(cin[s][:, :], row(src, b)).then_inc(c_loaded[s], 16)

            def hold():
                sp.nop(nofuse=True)

            def x_used(y, trip, s):
                if y == AC:
                    sp.wait_ge(xf_psum[s], one_of(trip))
                else:
                    sp.wait_ge(xT_psum[s], turned(trip, y))
                hold()

            def context_used(y, trip, s):
                if y == AC:
                    sp.wait_ge(ctxf_psum[s], nth(trip, 4, 4))
                else:
                    sp.wait_ge(xqT_psum[s], nth(trip, XKV, XKV))
                hold()

            def store(y, trip, s):
                sp.wait_ge(x_ready[s], seq(trip, y))
                dst = out if y == FF else between[y % 2]
                sp.dma_start(row(dst, trip * SLOTS + s), xres[s][:, :]).then_inc(stored[s], 16)

            for s in both:
                load_x(a["x"], s, s)
            sp.dma_start(masks[:, :, :], a["masks"]).then_inc(ld_masks, 16)
            for i, n in enumerate("qkvo"):
                sp.dma_start(tank[i // 2][:, i % 2 * KT * D:(i % 2 + 1) * KT * D], a["w0_" + n]).then_inc(ld_w0[i], 16)
                if i == 0:
                    sp.dma_start(cols[:, :, :], a["cols"]).then_inc(ld_c, 16)
                    sp.dma_start(bo_row, a["bo"].partition_broadcast(P)).then_inc(ld_c, 16)
                    sp.dma_start(bv_row, a["bv"].partition_broadcast(P)).then_inc(ld_c, 16)
                    sp.dma_start(br_row[:, :], a["br"].partition_broadcast(P)).then_inc(ld_c, 16)
                    for s in both:
                        sp.dma_start(small[:, s * 38:(s + 1) * 38], a["small"][:, s * 38:(s + 1) * 38]).then_inc(stored[s], 16)
            for s in both:
                load_residual(a["x"], s, s)
            during = {A0: (pieces_during_A0, 2, 0), AC: (pieces_during_AC, 4, PIECES_MOE), A1: (pieces_during_A1, 4, PIECES_A1)}

            def trips_on(y, t, n):
                return (y + 1, t + n - TRIPS) if isinstance(t, int) and t + n >= TRIPS else (y, t + n)

            def source(y):
                return a["x"] if y == A0 else between[(y - 1) % 2]

            def fetch_during(y, t, which):
                if y in during:
                    pieces, per_trip, before = during[y]
                    fetch(pieces(t), t, per_trip, before, which)

            def load_x_after(y1, t1, y2, t2, s):
                if y2 < LAYERS:
                    x_used(y1, t1, s)
                    load_x(source(y2), t2 * SLOTS + s, s)

            def keep_fed(y, t):
                last = isinstance(t, int) and t == TRIPS - 1
                if y in (AC, XA) and not last:
                    for s in both:
                        context_used(y, t, s)
                        load_context(a["ctx" if y == AC else "ctxT"], t * SLOTS + (SLOTS + s), s)
                fetch_during(y, t, slice(2, 4))
                if y == A0 and last:
                    sp.wait_ge(x_biased, SLOTS * TRIPS)
                    for s in both:
                        sp.wait_ge(v_ready[s], TRIPS)
                    sp.dma_start(table[:, :], a["dft"]).then_inc(ld_c, 16)
                if y == A1 and last:
                    fetch(pieces_from_A1(), 0, 0, PIECES_XQ, slice(0, 2))
                if y in (A0, A1) and last:
                    for s in both:
                        sp.wait_ge(kM_ready[s], (1 if y == A0 else 2) * TRIPS * NCH)
                        load_context(a["ctx" if y == A0 else "ctxT"], s, s)
                if y == A1 and last:
                    fetch(pieces_from_A1(), 0, 0, PIECES_XQ, slice(2, KT))
                y1, t1 = trips_on(y, t, 1)
                y2, t2 = trips_on(y, t, 2)
                if y1 != AC:
                    for s in both:
                        load_x_after(y1, t1, y2, t2, s)
                for s in both:
                    store(y, t, s)
                if y1 == AC:
                    for s in both:
                        load_x_after(y1, t1, y2, t2, s)
                if y == A0 and last:
                    fetch(pieces_after_A0(), 0, 0, PIECES_A0, slice(0, 2))
                if y1 < LAYERS:
                    fetch_during(y1, t1, slice(0, 2))
                    for s in both:
                        sp.wait_ge(stored[s], nth(t, 16, 32, y * TRIPS * 16))
                        hold()
                        load_residual(source(y1), t1 * SLOTS + s, s)
                if y == A1 and last:
                    fetch(pieces_from_A1(), 0, 0, PIECES_XQ, slice(KT, None))

            fetch_during(A0, 0, slice(0, 2))
            for s in both:
                x_used(A0, 0, s)
                load_x(a["x"], SLOTS + s, s)
            for y in range(LAYERS):
                with sp.Fori(0, TRIPS - 2) as trip:
                    keep_fed(y, trip)
                for t in range(TRIPS - 2, TRIPS):
                    keep_fed(y, t)
            for s in both:
                sp.wait_ge(stored[s], 16 + 16 * LAYERS * TRIPS)

        @block.tensor
        def _(pe):
            mm = nc.tensor.matmul

            def mm3(dst, lhs, rhs, start, stop):
                mm(dst, lhs[1], rhs[0], start=start, stop=False)
                mm(dst, lhs[0], rhs[1], start=False, stop=False)
                return mm(dst, lhs[0], rhs[0], start=False, stop=stop)

            def pair(w, *at):
                return w[0][at], w[1][at]

            ALL = slice(None)

            def xT(s, k):
                return hTh[:, k, s, 1, :], hTl[:, k, s, 1, :]

            def x_to_features(trip, s, y, ahead, b):
                pe.wait_ge(x_loaded[s], nth(trip, 16, 16 + 16 * ahead, 16 * y * TRIPS))
                for m in range(KT):
                    ins = nc.tensor.transpose(bank[s][b][:, m * P:(m + 1) * P], xin[s][:, m * P:(m + 1) * P], ident)
                ins.then_inc(xT_psum[s], 1)

            def q_k_first(trip):
                for s in both:
                    pe.wait_ge(xT_ready[s], turned(trip, A0))
                for i in range(2):
                    for m in range(KT):
                        pe.wait_ge(w0_ready, 2 * i + m // 2 + 1)
                        dst = bank[i][m // 2][:, m % 2 * 256:(m % 2 + 1) * 256]
                        for k in range(KT):
                            ins = mm3(dst, pair(w_qkv0[i], ALL, k, slice(m * P, (m + 1) * P)),
                                      (hTh[:, k, :, 1, :], hTl[:, k, :, 1, :]), k == 0, k == KT - 1)
                        if m % 2:
                            ins.then_inc(qk0_psum, 1)

            def v_first(trip, s):
                pe.wait_ge(w0_ready, 6)
                for k in range(KT):
                    ins = mm3(bank[s][2][:, :], xT(s, k), pair(w_qkv0[2], ALL, k), k == 0, k == KT - 1)
                ins.then_inc(v0_psum[s], 1)

            def project_second(trip, s, i, tiles_of=range(KT)):
                if i == 0:
                    pe.wait_ge(xT_ready[s], turned(trip, A1))
                for k in tiles_of:
                    ins = mm3(bank[s][i][:, :], xT(s, k), pair(w_qkv1, ALL, k, slice(i * D, (i + 1) * D)), k == 0, k == KT - 1)
                if KT - 1 in tiles_of:
                    ins.then_inc(proj_psum[s], 1)

            def normed_to_features(trip, s):
                pe.wait_ge(qkn_ready[s], one_of(trip))
                for i in (1, 0):
                    for m in range(KT):
                        ins = nc.tensor.transpose(bank[s][i][:, m * P:(m + 1) * P], pp[s][i][:, m * P:(m + 1) * P], ident)
                    ins.then_inc(qkT_psum[s], 1)

            def scores(trip, s, l, c):
                pe.wait_ge(kM_ready[s], chunk(trip, l, c + 1))
                if c == 0 and l == 1:
                    pe.wait_ge(qT_ready[s], one_of(trip))
                if c >= 2:
                    pe.wait_ge(max_ready[s], chunk(trip, l, c - 1))
                m = c * CH // HT
                mm(bank[s][c % 2][:, :], qT[s][:, m * P:(m + 1) * P], kM[s], start=True, stop=True
                   ).then_inc(scores_psum[s], 1)

            def probs_transpose(trip, s, l, c):
                pe.wait_ge(probs_ready[s], chunk(trip, l, c + 1))
                if c == 0:
                    pe.wait_ge(v_ready[s], attn(trip, l))
                else:
                    pe.wait_ge(probsT_ready[s], chunk(trip, l, c))
                for j in range(CH):
                    ins = nc.tensor.transpose(bank[s][2][:, j * P:(j + 1) * P], pp[s][c % 2][:, j * P:(j + 1) * P], ident)
                ins.then_inc(probsT_psum[s], 1)

            def weigh_values(trip, s, l, c):
                pe.wait_ge(probsT_ready[s], chunk(trip, l, c + 1))
                m, e = c // 2, c % 2
                for j, h in enumerate(heads_of(c)):
                    ins = mm(bank[s][3][j * PAD:(j + 1) * PAD, m * P:(m + 1) * P], vv[s][:, h * PAD:(h + 1) * PAD],
                             pT[s][c % 2][:, j * P:(j + 1) * P], start=e == 0, stop=e == 1)
                ins.then_inc(pv_done[s], 1)

            def sums_to_features(trip, s, l):
                pe.wait_ge(sums_ready[s], nth(trip, 2, 2, 2 * l * TRIPS))
                for m in range(KT):
                    ins = nc.tensor.transpose(bank[s][0][:, m * P:(m + 1) * P], sums[s][:, m * P:(m + 1) * P], ident)
                ins.then_inc(sumsT_psum[s], 1)

            def attention_out(trip, s, l):
                pe.wait_ge(oT_ready[s], attn(trip, l))
                if l == 0:
                    pe.wait_ge(w0_ready, 8)
                w = (w_o0, w_o1)[l]
                for k in range(KT):
                    ins = mm3(bank[s][3][:, :], (hTh[:, k, s, 0, :], hTl[:, k, s, 0, :]), pair(w, ALL, k), k == 0, k == KT - 1)
                ins.then_inc(branch_psum[s], 1)

            def context_spectrum(trip, s, i, ahead=0):
                if i == 0:
                    pe.wait_ge(c_loaded[s], nth(trip, 16, 16 + 16 * ahead))
                    if ahead:
                        pe.wait_ge(lagexp_ready[s], one_of(trip))
                elif i >= 2:
                    pe.wait_ge(cross_ready[s], one_of(trip))
                mm(bank[s][(2, 0, 1, 3)[i]][:, :], (DC, DCS, DO, DOS)[i], cin[s][:, :], start=True, stop=True
                   ).then_inc(ctxf_psum[s], 1)

            def x_spectrum(trip, s):
                pe.wait_ge(x_loaded[s], nth(trip, 16, 16, 16 * AC * TRIPS))
                pe.wait_ge(ln_var[s], TRIPS * AC)
                mm(bank[s][3][:, :], DX, xin[s][:, :], start=True, stop=True).then_inc(xf_psum[s], 1)

            def correlation(trip, s):
                pe.wait_ge(cross_ready[s], one_of(trip))
                for m in range(KT):
                    mm(bank[s][2][:, m * P:(m + 1) * P], pr[s][0][:, m * P:(m + 1) * P], I1, start=True, stop=False)
                    ins = mm(bank[s][2][:, m * P:(m + 1) * P], pr[s][1][:, m * P:(m + 1) * P], I2, start=False, stop=True)
                ins.then_inc(corr_psum[s], 1)

            def lag_weights_to_lags(trip, s):
                pe.wait_ge(lagw_ready[s], one_of(trip))
                for m in range(KT):
                    ins = nc.tensor.transpose(bank[s][0][:, m * P:(m + 1) * P], pr[s][0][:, m * P:(m + 1) * P], ident)
                ins.then_inc(lagwT_psum[s], 1)

            def lag_spectrum(trip, s):
                pe.wait_ge(lagwT_ready[s], one_of(trip))
                pe.wait_ge(ctxf_ready[s], nth(trip, 4, 4))
                mm(bank[s][3][:, :], DX, pr[s][1], start=True, stop=True).then_inc(lagf_psum[s], 1)
                mm(bank[s][0][:, :], DL, pr[s][1], start=True, stop=True).then_inc(lagf_psum[s], 1)

            def shifted_sum(trip, s):
                for i, (t, src) in enumerate(((E1, lagv[s]), (E2, lage[s]), (O1, pr[s][0]), (O2, pr[s][1]))):
                    if i % 2 == 0:
                        pe.wait_ge(shift_ready[s], nth(trip, 2, i // 2 + 1))
                    ins = mm(bank[s][1][:, :], t, src, start=i == 0, stop=i == 3)
                ins.then_inc(branch_psum[s], 1)

            def gates_and_rank(trip, s):
                pe.wait_ge(xT_ready[s], turned(trip, MOE))
                for k in range(KT):
                    ins = mm3(bank[s][0][:, 0:NG], xT(s, k), pair(w_gl, ALL, k), k == 0, k == KT - 1)
                ins.then_inc(mix_psum[s], 1)

            def base(trip, s):
                pe.wait_ge(ln_var[s], seq(trip, MOE, 0))
                for k in range(KT):
                    mm3(bank[s][3][:, :], xT(s, k), pair(w_base, ALL, k), k == 0, False)

            def gated_to_rank(trip, s):
                pe.wait_ge(mixed_ready[s], mix(trip, MOE))
                n = GH * ER
                for i in range(2):
                    ins = nc.tensor.transpose(bank[s][2][0:n, i * P:(i + 1) * P], hg[s][:, i * n:(i + 1) * n], ident)
                ins.then_inc(mixedT_psum[s], 1)

            def experts_out(trip, s):
                pe.wait_ge(mixedT_ready[s], mix(trip, MOE))
                for i in range(2):
                    lhs = hTh[0:GH * ER, i, s, 0, :], hTl[0:GH * ER, i, s, 0, :]
                    ins = mm3(bank[s][3][:, :], lhs, pair(w_lb, ALL, i), False, i == 1)
                ins.then_inc(branch_psum[s], 1)

            def cross_keys(trip):
                for s in both:
                    pe.wait_ge(cT_ready[s], one_of(trip))
                for i in range(NKV // P):
                    for k in range(KT):
                        ins = mm3(bank[i % 2][i // 2][:, :], pair(w_xk, ALL, k, slice(i * P, (i + 1) * P)),
                                  (hTh[:, k].rearrange("p s h t -> p (s h t)"), hTl[:, k].rearrange("p s h t -> p (s h t)")),
                                  k == 0, k == KT - 1)
                    ins.then_inc(xk_psum, 1)

            def cross_kept_values(trip, s, n):
                t = 1 - n
                if n == 0:
                    pe.wait_ge(ln_var[s], seq(trip, XA, 0))
                else:
                    pe.wait_ge(xv_ready[s], nth(trip, 2, 1))
                for k in range(KT):
                    ins = mm3(bank[s][3][:, 0:NKV], (hTh[:, k, s, t, :], hTl[:, k, s, t, :]), pair(w_xv, ALL, k), k == 0, k == KT - 1)
                ins.then_inc(xv_psum[s], 1)

            def cross_q(trip, s, g):
                if g == 0:
                    pe.wait_ge(xT_ready[s], turned(trip, XA))
                else:
                    pe.wait_ge(xqk_ready[s], nth(trip, XKV, g))
                n = XG * XD
                for k in range(KT):
                    ins = mm3(bank[s][2][:, 0:n], xT(s, k), pair(w_xq, ALL, k, slice(g * n, (g + 1) * n)), k == 0, k == KT - 1)
                ins.then_inc(xq_psum[s], 1)

            def cross_qT(trip, s, g):
                pe.wait_ge(xq_ready[s], nth(trip, XKV, g + 1))
                for j in range(XG):
                    ins = nc.tensor.transpose(bank[s][2][0:XD, j * P:(j + 1) * P], xq[s][:, j * XD:(j + 1) * XD], ident)
                ins.then_inc(xqT_psum[s], 1)

            def cross_scores(trip, s, g):
                pe.wait_ge(xqk_ready[s], nth(trip, XKV, g + 1))
                if g == 0:
                    pe.wait_ge(xk_ready, nth(trip, NKV // P, NKV // P))
                if g > 0:
                    pe.wait_ge(xo_ready[s], nth(trip, XKV, g))
                for i in range(2):
                    for j in range(2):
                        ins = mm3(bank[s][i][:, j * XT:(j + 1) * XT], pair(xqT[s], ALL, 0, slice((2 * i + j) * P, (2 * i + j + 1) * P)),
                                  xks[s], True, True)
                    ins.then_inc(xs_psum[s], 1)

            def cross_probsT(trip, s, g):
                for i in range(2):
                    pe.wait_ge(xpn_ready[s], nth(trip, 2 * XKV, 2 * g + i + 1))
                    for j in range(4):
                        at = (4 * i + j) * P
                        ins = nc.tensor.transpose(bank[s][i][:, j * P:(j + 1) * P], xp[s][:, at:at + P], ident)
                    ins.then_inc(xpT_psum[s], 1)

            def cross_values(trip, s, g):
                pe.wait_ge(xpT_ready[s], nth(trip, 2 * XKV, 2 * g + 2))
                if g == 0:
                    pe.wait_ge(xv_ready[s], nth(trip, 2, 2))
                for tile in range(XG * XD // P):
                    for t in range(2):
                        for _, row, j, first, n in [at for at in places if at[0] == tile]:
                            ins = mm(bank[s][0][row:row + n, tile * P:(tile + 1) * P],
                                     xv[s][:, t * NKV + g * XD + first:t * NKV + g * XD + first + n],
                                     xpT[s][:, (2 * j + t) * P:(2 * j + t + 1) * P], start=t == 0, stop=t == 1)
                ins.then_inc(xo_psum[s], 1)

            def cross_out(trip, s, g):
                pe.wait_ge(xo_ready[s], nth(trip, XKV, g + 1))
                pe.wait_ge(w_split, FREE + PIECES_XV + XG * XD // P * (g + 1))
                n = XG * XD // P
                for m in range(n):
                    ins = mm3(bank[s][3][:, :], (hTh[:, m, s, 0, :], hTl[:, m, s, 0, :]), pair(w_xo, ALL, g * n + m),
                              g == 0 and m == 0, g == XKV - 1 and m == n - 1)
                if g == XKV - 1:
                    ins.then_inc(branch_psum[s], 1)

            def routes_and_low(trip, s):
                pe.wait_ge(xT_ready[s], turned(trip, FF))
                for k in range(KT):
                    ins = mm3(bank[s][0][:, 0:NL], xT(s, k), pair(w_al, ALL, k), k == 0, k == KT - 1)
                ins.then_inc(mix_psum[s], 1)

            def low_to_rank(trip, s):
                pe.wait_ge(mixed_ready[s], mix(trip, FF))
                nc.tensor.transpose(bank[s][2][:, 0:P], low[s], ident).then_inc(mixedT_psum[s], 1)

            def heads_out(trip, s):
                pe.wait_ge(mixedT_ready[s], mix(trip, FF))
                mm3(bank[s][3][:, :], (hTh[:, 0, s, 0, :], hTl[:, 0, s, 0, :]), pair(w_bl, ALL, 0), True, True).then_inc(branch_psum[s], 1)

            def each(step, trip, *args):
                for s in both:
                    step(trip, s, *args)

            def self_attention(trip, l, next_x):
                for c in range(1, NCH):
                    each(scores, trip, l, c)
                    each(probs_transpose, trip, l, c - 1)
                    if c >= 2:
                        each(weigh_values, trip, l, c - 2)
                probs_transpose(trip, 0, l, NCH - 1)
                each(weigh_values, trip, l, NCH - 2)
                sums_to_features(trip, 0, l)
                probs_transpose(trip, 1, l, NCH - 1)
                weigh_values(trip, 0, l, NCH - 1)
                sums_to_features(trip, 1, l)
                weigh_values(trip, 1, l, NCH - 1)
                if next_x is not None:
                    each(x_to_features, trip, next_x, 1, 1)
                each(attention_out, trip, l)

            def first_layer(trip, more):
                q_k_first(trip)
                v_first(trip, 0)
                each(scores, trip, 0, 0)
                v_first(trip, 1)
                self_attention(trip, 0, A0 if more else None)

            def autocorrelation(trip, more):
                each(x_spectrum, trip)
                each(context_spectrum, trip, 1)
                each(correlation, trip)
                for s in both:
                    for i in (2, 3):
                        context_spectrum(trip, s, i)
                lag_weights_to_lags(trip, 0)
                lag_spectrum(trip, 0)
                if more:
                    each(context_spectrum, trip, 0, 1)
                else:
                    for s in both:
                        pe.wait_ge(lagexp_ready[s], one_of(trip))
                        x_to_features(0, s, MOE, 0, 2)
                lag_weights_to_lags(trip, 1)
                lag_spectrum(trip, 1)
                each(shifted_sum, trip)

            def last_layer(trip, more):
                each(routes_and_low, trip)
                if more:
                    each(x_to_features, trip, FF, 1, 1)
                each(low_to_rank, trip)
                each(heads_out, trip)

            pe.wait_ge(ld_masks, 16)
            each(x_to_features, 0, A0, 0, 1)
            with pe.Fori(0, TRIPS - 1) as trip:
                first_layer(trip, True)
            first_layer(TRIPS - 1, False)
            pe.wait_ge(ld_c, 80)
            each(context_spectrum, 0, 0)
            with pe.Fori(0, TRIPS - 1) as trip:
                autocorrelation(trip, True)
            autocorrelation(TRIPS - 1, False)
            pe.wait_ge(w_split, FREE + PIECES_MOE)
            with pe.Fori(0, TRIPS) as trip:
                each(gates_and_rank, trip)
                each(base, trip)
                each(gated_to_rank, trip)
                each(x_to_features, trip, MOE, 1, 1)
                each(experts_out, trip)
            pe.wait_ge(w_split, FREE + PIECES_A1)
            with pe.Fori(0, TRIPS) as trip:
                for s in both:
                    for i in range(2):
                        project_second(trip, s, i)
                project_second(trip, 0, 2)
                normed_to_features(trip, 0)
                project_second(trip, 1, 2, range(KT // 2))
                normed_to_features(trip, 1)
                scores(trip, 0, 1, 0)
                project_second(trip, 1, 2, range(KT // 2, KT))
                scores(trip, 1, 1, 0)
                self_attention(trip, 1, A1)
            pe.wait_ge(w_split, FREE + PIECES_XQ)
            with pe.Fori(0, TRIPS) as trip:
                each(cross_q, trip, 0)
                pe.wait_ge(w_split, FREE + PIECES_XV)
                each(cross_kept_values, trip, 0)
                cross_keys(trip)
                each(cross_qT, trip, 0)
                each(cross_kept_values, trip, 1)
                for g in range(XKV):
                    each(cross_scores, trip, g)
                    if g + 1 < XKV:
                        each(cross_q, trip, g + 1)
                    else:
                        each(x_to_features, trip, XA, 1, 2)
                    if g > 0:
                        each(cross_out, trip, g - 1)
                    each(cross_probsT, trip, g)
                    for s in both:
                        if g + 1 < XKV:
                            cross_qT(trip, s, g + 1)
                        cross_values(trip, s, g)
                each(cross_out, trip, XKV - 1)
            pe.wait_ge(w_split, FREE + PIECES_FF)
            with pe.Fori(0, TRIPS - 1) as trip:
                last_layer(trip, True)
            last_layer(TRIPS - 1, False)

        @block.scalar
        def _(act):
            av = nc.scalar.activation
            copy = nc.scalar.copy

            def xT_split(trip, s, y, ahead, b):
                act.wait_ge(xT_psum[s], turned(trip, y, ahead))
                copy(hTh[:, :, s, 1, :], tiles(bank[s][b][:, :])).then_inc(xT_hi[s], 1)

            def norm_x(y, trip, s):
                act.wait_ge(ln_rstd[s], normed(trip, y, 2))
                av(xres[s][:, :], xres[s][:, :], ACT.Identity, bias=st[s][:, SHIFT], scale=st[s][:, RSTD]).then_inc(x_ready[s], 1)

            def split_hi(pieces, p, trip, per_trip, before):
                src, hi, _ = halves(pieces, p)
                act.wait_ge(raw_loaded[p % 2], loaded_piece(p, trip, per_trip, before))
                copy(hi, src).then_inc(w_hi, 1)

            def close_layer(y, trip):
                for s in both:
                    if y in NORMED_BY_ACT:
                        norm_x(y, trip, s)

            def qT_second(trip, s):
                act.wait_ge(qkT_psum[s], nth(trip, 2, 2))
                for m in range(KT):
                    ins = av(qT[s][:, m * P:(m + 1) * P], bank[s][0][:, m * P:(m + 1) * P], ACT.Identity,
                             bias=cols[:, 3, m:m + 1], scale=cols[:, 2, m:m + 1])
                ins.then_inc(qT_ready[s], 1)

            def probs(trip, s, l, c):
                act.wait_ge(max_ready[s], chunk(trip, l, c + 1))
                for j, h in enumerate(heads_of(c)):
                    blockp = pp[s][c % 2][:, j * P:(j + 1) * P]
                    ins = av(blockp, blockp, ACT.Exp, bias=st[s][:, NEGMAX.start + h:NEGMAX.start + h + 1],
                             scale=(HD ** -0.5 if l == 0 else slopes[h]),
                             accum_out=st[s][:, ROWSUM.start + h:ROWSUM.start + h + 1])
                ins.then_inc(probs_ready[s], 1)

            def sumsT(trip, s, l):
                act.wait_ge(sumsT_psum[s], attn(trip, l))
                copy(sums[s], bank[s][0][:, :]).then_inc(sumsT_ready[s], 1)

            def oT_split(trip, s, l):
                act.wait_ge(heads_ready[s], attn(trip, l))
                copy(hTh[:, :, s, 0, :], tiles(hd[s])).then_inc(inner_hi[s], 1)

            def context_spectrum(trip, s, i, ahead=0):
                act.wait_ge(ctxf_psum[s], nth(trip, 4, i + 1 + 4 * ahead))
                if ahead:
                    act.wait_ge(shift_ready[s], nth(trip, 2, 1))
                copy(spec[s][i], bank[s][(2, 0, 1, 3)[i]][:, :]).then_inc(ctxf_ready[s], 1)

            def lag_exp(trip, s):
                act.wait_ge(lagmax_ready[s], one_of(trip))
                for m in range(KT):
                    ins = av(lage[s][:, m * P:(m + 1) * P], bank[s][2][:, m * P:(m + 1) * P], ACT.Exp,
                             bias=st[s][:, LAGNEG.start + m:LAGNEG.start + m + 1], scale=1.0)
                ins.then_inc(lagexp_ready[s], 1)

            def lag_weightsT(trip, s):
                act.wait_ge(lagwT_psum[s], one_of(trip))
                copy(pr[s][1], bank[s][0][:, :]).then_inc(lagwT_ready[s], 1)

            def gate_exp(trip, s):
                act.wait_ge(mixmax_ready[s], mix(trip, MOE))
                av(gates[s][:, 2, 0:NE], gates[s][:, 0, 0:NE], ACT.Exp, bias=st[s][:, ONE_A], scale=1.0
                   ).then_inc(mixexp_ready[s], 1)

            def gated_split(trip, s):
                act.wait_ge(mixedT_psum[s], mix(trip, MOE))
                copy(hTh[0:GH * ER, 0:2, s, 0, :], tiles(bank[s][2][0:GH * ER, 0:2 * P], 2)).then_inc(inner_hi[s], 1)

            def context_split(trip, s):
                act.wait_ge(c_loaded[s], nth(trip, 16, 16, 16 * TRIPS))
                act.wait_ge(branch_psum[s], seq(trip, XA, 0))
                copy(hTh[:, :, s, 0, :], tiles(cin[s][:, :])).then_inc(inner_hi[s], 1)

            def cross_keys(trip):
                for i in range(NKV // P):
                    act.wait_ge(xk_psum, nth(trip, NKV // P, i + 1))
                    for tile, row, g, first, n in places:
                        for s in both:
                            if tile == i:
                                ins = copy(xkT[s][first:first + n, g * XT:(g + 1) * XT],
                                           bank[i % 2][i // 2][row:row + n, s * XT:(s + 1) * XT])
                    ins.then_inc(xk_ready, 1)

            def cross_kept_values(trip, s, n):
                act.wait_ge(xv_psum[s], nth(trip, 2, n + 1))
                t = 1 - n
                copy(xv[s][:, t * NKV:(t + 1) * NKV], bank[s][3][:, 0:NKV]).then_inc(xv_ready[s], 1)

            def cross_q(trip, s, g):
                act.wait_ge(xq_psum[s], nth(trip, XKV, g + 1))
                if g == 0:
                    act.wait_ge(cT_ready[s], one_of(trip))
                copy(xq[s], bank[s][2][:, 0:XG * XD]).then_inc(xq_ready[s], 1)

            def cross_split(trip, s, g):
                act.wait_ge(xqT_psum[s], nth(trip, XKV, g + 1))
                if g == 0:
                    act.wait_ge(xk_ready, nth(trip, NKV // P, NKV // P))
                copy(xks[s][0], xkT[s][:, g * XT:(g + 1) * XT])
                copy(xqT[s][0][:, 0, :], bank[s][2][0:XD, :]).then_inc(xqk_hi[s], 1)

            def cross_probs(trip, s, g):
                for i in range(2):
                    act.wait_ge(xmax_ready[s], nth(trip, 2 * XKV, 2 * g + i + 1))
                    for j in range(2):
                        h = 2 * i + j
                        ins = av(xp[s][:, h * XT:(h + 1) * XT], bank[s][i][:, j * XT:(j + 1) * XT], ACT.Exp,
                                 bias=st[s][:, NEGMAX.start + h:NEGMAX.start + h + 1], scale=XD ** -0.5,
                                 accum_out=st[s][:, ROWSUM.start + h:ROWSUM.start + h + 1])
                    ins.then_inc(xp_ready[s], 1)

            def cross_heads(trip, s, g):
                act.wait_ge(xo_psum[s], nth(trip, XKV, g + 1))
                n = XG * XD // P
                copy(hTh[:, 0:n, s, 0, :], tiles(bank[s][0][:, 0:XG * XD], n)).then_inc(xo_hi[s], 1)

            def route_exp(trip, s):
                act.wait_ge(mixmax_ready[s], mix(trip, FF))
                av(st[s][:, EIGHT], st[s][:, EIGHT], ACT.Exp, bias=st[s][:, ONE_A], scale=1.0,
                   accum_out=st[s][:, ONE_B]).then_inc(mixexp_ready[s], 1)

            def low_split(trip, s):
                act.wait_ge(mixedT_psum[s], mix(trip, FF))
                copy(hTh[:, 0, s, 0, :], bank[s][2][:, 0:P]).then_inc(inner_hi[s], 1)

            def each(step, trip, *args):
                for s in both:
                    step(trip, s, *args)

            def first_layer(trip, more):
                for p in range(2):
                    split_hi(pieces_during_A0(trip), p, trip, 2, 0)
                for c in range(NCH):
                    each(probs, trip, 0, c)
                each(sumsT, trip, 0)
                each(oT_split, trip, 0)
                if more:
                    each(xT_split, trip, A0, 1, 1)
                close_layer(A0, trip)

            def autocorrelation(trip, more):
                each(context_spectrum, trip, 1)
                lag_exp(trip, 0)
                for s in both:
                    for i in (2, 3):
                        context_spectrum(trip, s, i)
                lag_weightsT(trip, 0)
                lag_exp(trip, 1)
                lag_weightsT(trip, 1)
                if more:
                    each(context_spectrum, trip, 0, 1)
                else:
                    each(xT_split, 0, MOE, 0, 2)
                close_layer(AC, trip)

            def last_layer(trip, more):
                each(route_exp, trip)
                if more:
                    each(xT_split, trip, FF, 1, 1)
                each(low_split, trip)
                close_layer(FF, trip)

            each(xT_split, 0, A0, 0, 1)
            for i in range(4):
                act.wait_ge(ld_w0[i], 16)
                for e in range(2):
                    copy(half_w0(i, 0, e), raw_w0(i, e)).then_inc(w0_hi, 1)
            with act.Fori(0, TRIPS - 1) as trip:
                first_layer(trip, True)
            first_layer(TRIPS - 1, False)
            each(context_spectrum, 0, 0)
            with act.Fori(0, TRIPS - 1) as trip:
                autocorrelation(trip, True)
            autocorrelation(TRIPS - 1, False)
            with act.Fori(0, TRIPS) as trip:
                each(gate_exp, trip)
                each(gated_split, trip)
                each(xT_split, trip, MOE, 1, 1)
                close_layer(MOE, trip)
            with act.Fori(0, TRIPS) as trip:
                for p in range(4):
                    split_hi(pieces_during_A1(trip), p, trip, 4, PIECES_A1)
                each(qT_second, trip)
                for c in range(NCH):
                    each(probs, trip, 1, c)
                each(sumsT, trip, 1)
                each(oT_split, trip, 1)
                each(xT_split, trip, A1, 1, 1)
                close_layer(A1, trip)
            with act.Fori(0, TRIPS) as trip:
                each(context_split, trip)
                each(cross_q, trip, 0)
                each(cross_kept_values, trip, 0)
                cross_keys(trip)
                each(cross_split, trip, 0)
                each(cross_kept_values, trip, 1)
                for g in range(XKV):
                    each(cross_probs, trip, g)
                    if g + 1 < XKV:
                        each(cross_q, trip, g + 1)
                    else:
                        each(xT_split, trip, XA, 1, 2)
                    for s in both:
                        if g + 1 < XKV:
                            cross_split(trip, s, g + 1)
                        cross_heads(trip, s, g)
                close_layer(XA, trip)
            with act.Fori(0, TRIPS - 1) as trip:
                last_layer(trip, True)
            last_layer(TRIPS - 1, False)

        @block.gpsimd
        def _(pool):
            nc.gpsimd.memset(half[:, :], -0.5).then_inc(consts_ready, 1)
            for i in range(FREE):
                nc.gpsimd.memset(raw[i][:, 0:1], 0.0).then_inc(w_split, 1)
            for s in both:
                nc.gpsimd.memset(lag2[s][:, :, :], GONE).then_inc(consts_ready, 1)
                nc.gpsimd.memset(gate2[s][:, :], GONE).then_inc(consts_ready, 1)
                nc.gpsimd.memset(gates[s][:, :, :], GONE).then_inc(consts_ready, 1)
            pool.wait_ge(consts_ready, 1 + 3 * SLOTS)
            pool.wait_ge(ld_c, 64)

            def hold():
                pool.nop(nofuse=True)

            def add_bias(trip, s):
                pool.wait_ge(r_loaded[s], nth(trip, 16, 16))
                nc.gpsimd.tensor_tensor(xres[s][:, :], xres[s][:, :], bo_row, ALU.add).then_inc(x_biased, 1)

            def mask_keys(trip, s, l, c):
                if c > 0:
                    pool.wait_ge(scores_psum[s], chunk(trip, l, c))
                elif l == 0:
                    pool.wait_ge(qk0_ready, nth(trip, 2, 2))
                if l == 1 and c < 2:
                    pool.wait_ge(kT_ready[s], nth(trip, 2, c + 1))
                m, j = c * CH // HT, c * CH % HT
                nc.gpsimd.tensor_tensor(kM[s].rearrange("p (h t) -> p h t", h=CH),
                                        kT[s][:, m * P:(m + 1) * P].unsqueeze(1).broadcast_to([P, CH, P]),
                                        head_rows[:, j:j + CH].unsqueeze(2).broadcast_to([P, CH, P]),
                                        ALU.mult).then_inc(kM_ready[s], 1)

            def rstd(y, trip, s):
                pool.wait_ge(ln_var[s], seq(trip, y))
                nc.gpsimd.tensor_tensor(st[s][:, RSTD], st[s][:, MV][:, 1:2], half[:, 0:1], ALU.pow
                                        ).then_inc(ln_rstd[s], 1)
                if y in NORMED_BY_ACT:
                    pool.wait_ge(ln_rstd[s], normed(trip, y, 1))
                    hold()
                    nc.gpsimd.tensor_scalar(st[s][:, SHIFT], st[s][:, MV][:, 0:1], st[s][:, RSTD], -1.0, ALU.mult, ALU.mult
                                            ).then_inc(ln_rstd[s], 1)

            def rstd_qk(trip, s):
                pool.wait_ge(qk_var[s], one_of(trip))
                nc.gpsimd.tensor_tensor(st[s][:, QKRSTD], st[s][:, QKMV].rearrange("p (a b) -> p a b", b=2)[:, :, 1],
                                        half[:, 0:2], ALU.pow).then_inc(qk_rstd[s], 1)

            def split_lo(pieces, p, trip, per_trip, before):
                src, hi, lo = halves(pieces, p)
                pool.wait_ge(w_hi, nth(trip, per_trip, p + 1, before))
                nc.gpsimd.tensor_tensor(lo, src, f32(hi), ALU.subtract).then_inc(w_split, 1)

            def split(pieces, p, trip, per_trip, before, alone):
                src, hi, lo = halves(pieces, p)
                pool.wait_ge(raw_loaded[p % 2], loaded_piece(p, trip, per_trip, before))
                hold()
                nc.gpsimd.tensor_copy(hi, src).then_inc(w_hi_rest, 1)
                pool.wait_ge(w_hi_rest, nth(trip, per_trip, p + 1, alone))
                nc.gpsimd.tensor_tensor(lo, src, f32(hi), ALU.subtract).then_inc(w_split, 1)

            def each(step, *args):
                for s in both:
                    step(*args, s) if step is rstd else step(args[0], s, *args[1:])

            def zeros_around_values():
                for s in both:
                    nc.gpsimd.memset(vv[s], 0.0).then_inc(consts_ready, 1)

            pool.wait_ge(w0_ready, 8)
            zeros_around_values()
            with pool.Fori(0, TRIPS) as trip:
                for p in range(2):
                    split_lo(pieces_during_A0(trip), p, trip, 2, 0)
                for c in range(NCH):
                    each(mask_keys, trip, 0, c)
                    if c == 1:
                        each(add_bias, trip)
                each(rstd, A0, trip)
            for p in range(2):
                split(pieces_after_A0(), p, 0, 0, PIECES_A0, 0)
            for s in both:
                pool.wait_ge(branch_psum[s], TRIPS * (A0 + 1))
            with pool.Fori(0, TRIPS) as trip:
                for p in range(4):
                    split(pieces_during_AC(trip), p, trip, 4, PIECES_MOE, 2)
                each(rstd, AC, trip)
            with pool.Fori(0, TRIPS) as trip:
                each(rstd, MOE, trip)
            for s in both:
                pool.wait_ge(branch_psum[s], TRIPS * (MOE + 1))
            zeros_around_values()

            def second_attention(trip):
                for p in range(2):
                    split_lo(pieces_during_A1(trip), p, trip, 4, PIECES_A0)
                    rstd_qk(trip, p)
                for c in range(NCH):
                    each(mask_keys, trip, 1, c)
                    if c in (1, 2):
                        split_lo(pieces_during_A1(trip), c + 1, trip, 4, PIECES_A0)

            with pool.Fori(0, TRIPS - 1) as trip:
                second_attention(trip)
                each(rstd, A1, trip)
            second_attention(TRIPS - 1)
            rest = pieces_from_A1()
            for s in both:
                pool.wait_ge(proj_psum[s], 3 * TRIPS)
            for p in range(KT):
                split(rest, p, 0, 0, PIECES_XQ, 2 + 4 * TRIPS)
            each(rstd, A1, TRIPS - 1)
            for s in both:
                pool.wait_ge(branch_psum[s], TRIPS * (A1 + 1))
            for p in range(KT, KT + NXO):
                split(rest, p, 0, 0, PIECES_XQ, 2 + 4 * TRIPS)
            with pool.Fori(0, TRIPS - 1) as trip:
                each(rstd, XA, trip)
            for s in both:
                pool.wait_ge(xs_psum[s], 2 * XKV * TRIPS)
            for p in range(KT + NXO, len(rest)):
                split(rest, p, 0, 0, PIECES_XQ, 2 + 4 * TRIPS)
            each(rstd, XA, TRIPS - 1)
            with pool.Fori(0, TRIPS) as trip:
                each(rstd, FF, trip)

        @block.vector
        def _(dve):
            DVE_STEPS = (22, 20, 20, 34, 38, 14)
            v = nc.vector
            taken = [0] * LAYERS

            def steps_done(y, trip, ins):
                taken[y] += 1
                ins.then_inc(dve_step, 1)
                dve.wait_ge(dve_step, nth(trip, DVE_STEPS[y], taken[y], TRIPS * sum(DVE_STEPS[:y])))

            def hold():
                dve.nop(nofuse=True)

            def xT_split(trip, s, y, ahead, b):
                dve.wait_ge(xT_hi[s], turned(trip, y, ahead))
                v.tensor_tensor(hTl[:, :, s, 1, :], tiles(bank[s][b][:, :]), f32(hTh[:, :, s, 1, :]), ALU.subtract
                                ).then_inc(xT_ready[s], 1)

            def v_first(trip, s):
                dve.wait_ge(v0_psum[s], one_of(trip))
                dve.wait_ge(consts_ready, 1 + 4 * SLOTS)
                for e in range(2):
                    ins = v.tensor_tensor(values_of(s, e), every_other(bank[s][2][:, :], e), every_other(bv_row, e), ALU.add)
                ins.then_inc(v_ready[s], 1)

            def qT_kT_first(trip):
                for i, dst in enumerate((qT, kT)):
                    for b in range(2):
                        dve.wait_ge(qk0_psum, nth(trip, 4, 2 * i + b + 1))
                        src = bank[i][b][:, :].rearrange("p (m s t) -> p m s t", m=2, s=SLOTS)
                        for s in both:
                            ins = v.tensor_tensor(tiles(dst[s])[:, 2 * b:2 * b + 2, :], src[:, :, s, :],
                                                  cols[:, i, 2 * b:2 * b + 2].unsqueeze(2).broadcast_to([P, 2, P]), ALU.add)
                    ins.then_inc(qk0_ready, 1)

            def clip_norm(trip, s, i):
                dve.wait_ge(proj_psum[s], nth(trip, 3, 1 + i))
                steps_done(A1, trip, v.tensor_scalar(pp[s][i], bank[s][i][:, :], -8.0, 8.0, ALU.max, ALU.min))
                bn = st[s][:, QKBN.start + 6 * i:QKBN.start + 6 * i + 6]
                mv = st[s][:, QKMV.start + 2 * i:QKMV.start + 2 * i + 2]
                steps_done(A1, trip, v.bn_stats(bn, pp[s][i]))
                hold()
                steps_done(A1, trip, v.bn_aggr(mv, bn))
                if i == 1:
                    var = st[s][:, QKMV].rearrange("p (a b) -> p a b", b=2)[:, :, 1]
                    v.tensor_scalar(var, var, EPS, None, ALU.add).then_inc(qk_var[s], 1)

            def v_second(trip, s):
                dve.wait_ge(proj_psum[s], nth(trip, 3, 3))
                dve.wait_ge(consts_ready, 1 + 5 * SLOTS)
                for e in range(2):
                    ins = v.tensor_scalar(values_of(s, e), every_other(bank[s][2][:, :], e), -8.0, 8.0, ALU.max, ALU.min)
                ins.then_inc(v_ready[s], 1)

            def apply_norm(trip, s):
                dve.wait_ge(qk_rstd[s], one_of(trip))
                for i in range(2):
                    ins = v.tensor_scalar(pp[s][i], pp[s][i], st[s][:, QKMV.start + 2 * i:QKMV.start + 2 * i + 1],
                                          st[s][:, QKRSTD.start + i:QKRSTD.start + i + 1], ALU.subtract, ALU.mult)
                ins.then_inc(qkn_ready[s], 1)

            def kT_second(trip, s, tiles_of):
                dve.wait_ge(qkT_psum[s], nth(trip, 2, 1))
                for m in tiles_of:
                    ins = v.tensor_scalar(kT[s][:, m * P:(m + 1) * P], bank[s][1][:, m * P:(m + 1) * P],
                                          cols[:, 4, m:m + 1], cols[:, 5, m:m + 1], ALU.mult, ALU.add)
                ins.then_inc(kT_ready[s], 1)

            def maxima(trip, s, l, c):
                dve.wait_ge(scores_psum[s], chunk(trip, l, c + 1))
                if c >= 2:
                    dve.wait_ge(probsT_psum[s], chunk(trip, l, c - 1))
                hold()
                for j, h in enumerate(heads_of(c)):
                    ins = v.tensor_tensor_reduce(pp[s][c % 2][:, j * P:(j + 1) * P], bank[s][c % 2][:, j * P:(j + 1) * P],
                                                 (mask0, rel1)[l], 1.0, GONE, ALU.add, ALU.max,
                                                 st[s][:, ROWMAX.start + h:ROWMAX.start + h + 1])
                steps_done((A0, A1)[l], trip, ins)
                v.tensor_tensor(st[s][:, head_columns(NEGMAX, c)], st[s][:, head_columns(ROWMAX, c)],
                                neg_scale[l][:, head_columns(slice(0, H), c)], ALU.mult).then_inc(max_ready[s], 1)

            def probsT(trip, s, l, c):
                dve.wait_ge(probsT_psum[s], chunk(trip, l, c + 1))
                if c >= 2:
                    dve.wait_ge(pv_done[s], chunk(trip, l, c - 1))
                v.tensor_copy(pT[s][c % 2], bank[s][2][:, :]).then_inc(probsT_ready[s], 1)

            def reciprocal_sums(trip, s, l):
                dve.wait_ge(probs_ready[s], chunk(trip, l, NCH))
                v.reciprocal(st[s][:, ROWSUM], st[s][:, ROWSUM]).then_inc(sums_ready[s], 1)
                dve.wait_ge(sums_ready[s], nth(trip, 2, 1, 2 * l * TRIPS))
                v.tensor_copy(sums[s].rearrange("p (h d) -> p h d", h=H), st[s][:, ROWSUM].unsqueeze(2).broadcast_to([P, H, HD])
                              ).then_inc(sums_ready[s], 1)

            def heads(trip, s, l):
                dve.wait_ge(sumsT_ready[s], attn(trip, l))
                dve.wait_ge(pv_done[s], chunk(trip, l, NCH))
                v.tensor_tensor(hd[s], bank[s][3][:, :], sums[s], ALU.mult).then_inc(heads_ready[s], 1)

            def oT_split(trip, s, l):
                dve.wait_ge(inner_hi[s], turned(trip, (A0, A1)[l]))
                v.tensor_tensor(hTl[:, :, s, 0, :], tiles(hd[s]), f32(hTh[:, :, s, 0, :]), ALU.subtract).then_inc(oT_ready[s], 1)

            def residual(y, trip, s, at):
                dve.wait_ge(branch_psum[s], seq(trip, y))
                if y == A0:
                    dve.wait_ge(x_biased, nth(trip, SLOTS, s + 1))
                else:
                    dve.wait_ge(r_loaded[s], nth(trip, 16, 16, 16 * y * TRIPS))
                steps_done(y, trip, v.tensor_tensor(xres[s][:, :], bank[s][at][:, :], xres[s][:, :], ALU.add))
                steps_done(y, trip, v.bn_stats(st[s][:, BN], xres[s][:, :]))
                hold()
                steps_done(y, trip, v.bn_aggr(st[s][:, MV], st[s][:, BN]))
                var = st[s][:, MV][:, 1:2]
                v.tensor_scalar(var, var, EPS, None, ALU.add).then_inc(ln_var[s], 1)

            def cross_products(trip, s):
                dve.wait_ge(xf_psum[s], one_of(trip))
                dve.wait_ge(ctxf_ready[s], nth(trip, 4, 2))
                v.tensor_tensor(pr[s][0], bank[s][3][:, :], spec[s][0], ALU.mult)
                v.tensor_tensor(pr[s][1], bank[s][3][:, :], spec[s][1], ALU.mult).then_inc(cross_ready[s], 1)

            def top_lags(trip, s):
                dve.wait_ge(corr_psum[s], one_of(trip))
                hold()
                m8 = st[s][:, NEGMAX].rearrange("p (k e) -> p k e", k=KT)
                n8 = st[s][:, ROWMAX].rearrange("p (k e) -> p k e", k=KT)
                for m in range(KT):
                    ins = v.max(m8[:, m, :], bank[s][2][:, m * P:(m + 1) * P])
                steps_done(AC, trip, ins)
                steps_done(AC, trip, v.tensor_scalar(st[s][:, LAGNEG], m8[:, :, 0], -1.0, None, ALU.mult))
                hold()
                for m in range(KT):
                    ins = v.match_replace(lagv[s][:, m * P:(m + 1) * P], m8[:, m, :], bank[s][2][:, m * P:(m + 1) * P], GONE)
                ins.then_inc(lagmax_ready[s], 1)
                dve.wait_ge(lagmax_ready[s], one_of(trip))
                hold()
                for m in range(KT):
                    ins = v.max(n8[:, m, :], lagv[s][:, m * P:(m + 1) * P])
                steps_done(AC, trip, ins)
                steps_done(AC, trip, v.tensor_copy(lag2[s][:, :, 0:TOPK - 8], n8[:, :, 0:TOPK - 8]))
                hold()
                for m in range(KT):
                    ins = v.match_replace(lagv[s][:, m * P:(m + 1) * P], lag2[s][:, m, :], lagv[s][:, m * P:(m + 1) * P], GONE)
                steps_done(AC, trip, ins)

            def lag_softmax(trip, s):
                dve.wait_ge(lagexp_ready[s], one_of(trip))
                for m in range(KT):
                    at = slice(m * P, (m + 1) * P)
                    ins = v.scalar_tensor_tensor(out=lage[s][:, at], in0=lagv[s][:, at], scalar=PICKED, in1=lage[s][:, at],
                                                 op0=ALU.is_le, op1=ALU.mult,
                                                 accum_out=st[s][:, LAGSUM.start + m:LAGSUM.start + m + 1])
                steps_done(AC, trip, ins)
                steps_done(AC, trip, v.reciprocal(st[s][:, LAGSUM], st[s][:, LAGSUM]))
                v.tensor_tensor(tiles(pr[s][0]), tiles(lage[s]), st[s][:, LAGSUM].unsqueeze(2).broadcast_to([P, KT, P]), ALU.mult
                                ).then_inc(lagw_ready[s], 1)

            def shift_products(trip, s):
                dve.wait_ge(ctxf_ready[s], nth(trip, 4, 4))
                dve.wait_ge(lagf_psum[s], nth(trip, 2, 2))
                for i, (d0, d1) in enumerate(((lagv[s], lage[s]), pr[s])):
                    src = bank[s][(3, 0)[i]][:, :]
                    v.tensor_tensor(d0, src, spec[s][2 * i], ALU.mult)
                    v.tensor_tensor(d1, src, spec[s][2 * i + 1], ALU.mult).then_inc(shift_ready[s], 1)

            def top_gates(trip, s):
                dve.wait_ge(mix_psum[s], mix(trip, MOE))
                logits = gates[s][:, 0, :]
                steps_done(MOE, trip, v.tensor_copy(logits[:, 0:NE], bank[s][0][:, 0:NE]))
                hold()
                steps_done(MOE, trip, v.max(st[s][:, TOP2], logits))
                v.tensor_scalar(st[s][:, ONE_A], st[s][:, TOP2][:, 0:1], -1.0, None, ALU.mult).then_inc(mixmax_ready[s], 1)
                steps_done(MOE, trip, v.tensor_copy(gate2[s][:, 0:2], st[s][:, TOP2][:, 0:2]))
                hold()
                steps_done(MOE, trip, v.match_replace(gates[s][:, 1, :], gate2[s][:, :], logits, GONE))

            def gated(trip, s):
                dve.wait_ge(mixexp_ready[s], mix(trip, MOE))
                e = gates[s][:, 2, 0:NE]
                steps_done(MOE, trip, v.scalar_tensor_tensor(out=e, in0=gates[s][:, 1, 0:NE], scalar=PICKED, in1=e,
                                                             op0=ALU.is_le, op1=ALU.mult, accum_out=st[s][:, ONE_B]))
                steps_done(MOE, trip, v.reciprocal(st[s][:, ONE_C], st[s][:, ONE_B]))
                steps_done(MOE, trip, v.tensor_scalar(e, e, st[s][:, ONE_C], 16.0 / ER, ALU.mult, ALU.mult))
                v.tensor_tensor(hg[s].rearrange("p (e r) -> p e r", e=NE), bank[s][0][:, NE:NG].rearrange("p (e r) -> p e r", e=NE),
                                e.unsqueeze(2).broadcast_to([P, NE, ER]), ALU.mult).then_inc(mixed_ready[s], 1)

            def gated_split(trip, s):
                dve.wait_ge(inner_hi[s], turned(trip, MOE))
                n = GH * ER
                v.tensor_tensor(hTl[0:n, 0:2, s, 0, :], tiles(bank[s][2][0:n, 0:2 * P], 2), f32(hTh[0:n, 0:2, s, 0, :]),
                                ALU.subtract).then_inc(mixedT_ready[s], 1)

            def context_split(trip, s):
                dve.wait_ge(inner_hi[s], turned(trip, XA))
                v.tensor_tensor(hTl[:, :, s, 0, :], tiles(cin[s][:, :]), f32(hTh[:, :, s, 0, :]), ALU.subtract
                                ).then_inc(cT_ready[s], 1)

            def cross_split(trip, s, g):
                dve.wait_ge(xqk_hi[s], nth(trip, XKV, g + 1))
                v.tensor_tensor(xks[s][1], xkT[s][:, g * XT:(g + 1) * XT], f32(xks[s][0]), ALU.subtract)
                v.tensor_tensor(xqT[s][1][:, 0, :], bank[s][2][0:XD, :], f32(xqT[s][0][:, 0, :]), ALU.subtract
                                ).then_inc(xqk_ready[s], 1)

            def cross_max(trip, s, g):
                for i in range(2):
                    dve.wait_ge(xs_psum[s], nth(trip, 2 * XKV, 2 * g + i + 1))
                    r = st[s][:, ROWMAX.start + 2 * i:ROWMAX.start + 2 * i + 2]
                    steps_done(XA, trip, v.tensor_reduce(r, bank[s][i][:, :].rearrange("p (h t) -> p h t", h=2), AX, ALU.max))
                    v.tensor_scalar(st[s][:, NEGMAX.start + 2 * i:NEGMAX.start + 2 * i + 2], r, -(XD ** -0.5), None, ALU.mult
                                    ).then_inc(xmax_ready[s], 1)

            def cross_probsT(trip, s, g):
                for i in range(2):
                    dve.wait_ge(xpT_psum[s], nth(trip, 2 * XKV, 2 * g + i + 1))
                    v.tensor_copy(xpT[s][:, i * 512:(i + 1) * 512], bank[s][i][:, :]).then_inc(xpT_ready[s], 1)

            def cross_norm(trip, s, g):
                for i in range(2):
                    dve.wait_ge(xp_ready[s], nth(trip, 2 * XKV, 2 * g + i + 1))
                    sums = st[s][:, ROWSUM.start + 2 * i:ROWSUM.start + 2 * i + 2]
                    steps_done(XA, trip, v.reciprocal(sums, sums))
                    for j in range(2):
                        block = xp[s][:, (2 * i + j) * XT:(2 * i + j + 1) * XT]
                        ins = v.tensor_scalar(block, block, sums[:, j:j + 1], None, ALU.mult)
                    ins.then_inc(xpn_ready[s], 1)

            def cross_heads(trip, s, g):
                dve.wait_ge(xo_hi[s], nth(trip, XKV, g + 1))
                n = XG * XD // P
                v.tensor_tensor(hTl[:, 0:n, s, 0, :], tiles(bank[s][0][:, 0:XG * XD], n), f32(hTh[:, 0:n, s, 0, :]), ALU.subtract
                                ).then_inc(xo_ready[s], 1)

            def routes(trip, s):
                dve.wait_ge(mix_psum[s], mix(trip, FF))
                e = st[s][:, EIGHT]
                steps_done(FF, trip, v.tensor_tensor(e, bank[s][0][:, LH * LR:NL], br_row[:, :], ALU.add))
                steps_done(FF, trip, v.tensor_reduce(st[s][:, ONE_C], e, AX, ALU.max))
                v.tensor_scalar(st[s][:, ONE_A], st[s][:, ONE_C], -1.0, None, ALU.mult).then_inc(mixmax_ready[s], 1)

            def routed(trip, s):
                dve.wait_ge(mixexp_ready[s], mix(trip, FF))
                e = st[s][:, EIGHT]
                steps_done(FF, trip, v.reciprocal(st[s][:, ONE_C], st[s][:, ONE_B]))
                steps_done(FF, trip, v.tensor_scalar(e, e, st[s][:, ONE_C], LH * 32.0 / LR, ALU.mult, ALU.mult))
                v.tensor_tensor(low[s].rearrange("p (h r) -> p h r", h=LH), bank[s][0][:, 0:LH * LR].rearrange("p (h r) -> p h r", h=LH),
                                e.unsqueeze(2).broadcast_to([P, LH, LR]), ALU.mult).then_inc(mixed_ready[s], 1)

            def low_split(trip, s):
                dve.wait_ge(inner_hi[s], turned(trip, FF))
                v.tensor_tensor(hTl[:, 0, s, 0, :], bank[s][2][:, 0:P], f32(hTh[:, 0, s, 0, :]), ALU.subtract
                                ).then_inc(mixedT_ready[s], 1)

            def each(step, trip, *args):
                for s in both:
                    step(trip, s, *args)

            def self_attention(trip, l):
                for c in range(NCH):
                    each(maxima, trip, l, c)
                    if c == 0:
                        (v_first, v_second)[l](trip, 1)
                    else:
                        each(probsT, trip, l, c - 1)
                for s in both:
                    reciprocal_sums(trip, s, l)
                    probsT(trip, s, l, NCH - 1)
                each(heads, trip, l)
                each(oT_split, trip, l)

            def norm_x(y, trip, s):
                dve.wait_ge(ln_rstd[s], normed(trip, y, 1))
                v.tensor_scalar(xres[s][:, :], xres[s][:, :], st[s][:, MV][:, 0:1], st[s][:, RSTD], ALU.subtract, ALU.mult
                                ).then_inc(x_ready[s], 1)

            def close_layer(y, trip, at):
                for s in both:
                    residual(y, trip, s, at)
                for s in both:
                    if y not in NORMED_BY_ACT:
                        norm_x(y, trip, s)

            each(xT_split, 0, A0, 0, 1)
            for i in range(4):
                for e in range(2):
                    dve.wait_ge(w0_hi, 2 * i + e + 1)
                    v.tensor_tensor(half_w0(i, 1, e), raw_w0(i, e), f32(half_w0(i, 0, e)), ALU.subtract).then_inc(w0_ready, 1)
            dve.wait_ge(ld_masks, 16)
            dve.wait_ge(ld_c, 64)
            dve.wait_ge(consts_ready, 1 + 3 * SLOTS)
            for s in both:
                dve.wait_ge(stored[s], 16)
            for i in (2, 3):
                v.tensor_tensor(cols[:, i, :], cols[:, i, :], q_scale, ALU.mult).then_inc(w0_ready, 1)
            dve.wait_ge(w0_ready, 8 + 2)

            def first_layer(trip, more):
                qT_kT_first(trip)
                v_first(trip, 0)
                self_attention(trip, 0)
                if more:
                    each(xT_split, trip, A0, 1, 1)
                close_layer(A0, trip, 3)

            def last_layer(trip, more):
                each(routes, trip)
                each(routed, trip)
                if more:
                    each(xT_split, trip, FF, 1, 1)
                each(low_split, trip)
                close_layer(FF, trip, 3)

            dve.wait_ge(w0_ready, 8)
            with dve.Fori(0, TRIPS - 1) as trip:
                first_layer(trip, True)
            taken[A0] = 0
            first_layer(TRIPS - 1, False)
            def autocorrelation(trip, more):
                each(cross_products, trip)
                for s in both:
                    top_lags(trip, s)
                    lag_softmax(trip, s)
                each(shift_products, trip)
                if not more:
                    each(xT_split, 0, MOE, 0, 2)
                close_layer(AC, trip, 1)

            with dve.Fori(0, TRIPS - 1) as trip:
                autocorrelation(trip, True)
            taken[AC] = 0
            autocorrelation(TRIPS - 1, False)
            with dve.Fori(0, TRIPS) as trip:
                each(top_gates, trip)
                each(gated, trip)
                each(gated_split, trip)
                each(xT_split, trip, MOE, 1, 1)
                close_layer(MOE, trip, 3)
            with dve.Fori(0, TRIPS) as trip:
                clip_norm(trip, 0, 0)
                clip_norm(trip, 0, 1)
                clip_norm(trip, 1, 0)
                apply_norm(trip, 0)
                clip_norm(trip, 1, 1)
                kT_second(trip, 0, range(1))
                apply_norm(trip, 1)
                kT_second(trip, 0, range(1, KT))
                kT_second(trip, 1, range(1))
                kT_second(trip, 1, range(1, KT))
                v_second(trip, 0)
                self_attention(trip, 1)
                each(xT_split, trip, A1, 1, 1)
                close_layer(A1, trip, 3)
            with dve.Fori(0, TRIPS) as trip:
                each(context_split, trip)
                each(cross_split, trip, 0)
                for g in range(XKV):
                    each(cross_max, trip, g)
                    each(cross_norm, trip, g)
                    each(cross_probsT, trip, g)
                    if g + 1 == XKV:
                        each(xT_split, trip, XA, 1, 2)
                    for s in both:
                        if g + 1 < XKV:
                            cross_split(trip, s, g + 1)
                        cross_heads(trip, s, g)
                close_layer(XA, trip, 3)
            with dve.Fori(0, TRIPS - 1) as trip:
                last_layer(trip, True)
            taken[FF] = 0
            last_layer(TRIPS - 1, False)
            assert tuple(taken) == DVE_STEPS, taken


def features_first(w):
    n, k = w.shape
    return np.ascontiguousarray(w.T.reshape(k // P, P, n).transpose(1, 0, 2))


def kernel(**inputs):
    import concourse.bacc as bacc
    from concourse.bass_utils import run_bass_kernel_spmd

    i = {k: np.asarray(v) for k, v in inputs.items()}
    consts, slopes = shape_constants()
    turned = i["ctx_4096"].transpose(0, 2, 1).reshape(B, KT, P, L).transpose(0, 2, 1, 3).reshape(B, P, D)
    by_feature = lambda b: b.reshape(KT, P).T
    lora_a = i["L0_ffn_lora_A"].reshape(NE * ER, D)
    lora_b = i["L0_ffn_lora_B"].transpose(0, 2, 1).reshape(2, GH * ER, D).transpose(1, 0, 2)
    head = np.arange(XH).reshape(XH // 4, 4, 1) * XD
    by_column_tile = np.concatenate([(head + part).reshape(XH // 4, -1) for part in (np.arange(WIDE), np.arange(WIDE, XD))], 1).ravel()
    arrays = {
        "x": i["x"], "ctx": i["ctx_4096"], "ctxT": turned,
        **{"w0_" + n: features_first(i[f"L0_attn_W{n}"]).reshape(P, KT * D) for n in "qkvo"},
        "cols": np.stack([by_feature(i[n]) for n in (
            "L0_attn_bq", "L0_attn_bk", "L1_attn_q_ln_w", "L1_attn_q_ln_b",
            "L1_attn_k_ln_w", "L1_attn_k_ln_b")], 1),
        "bo": i["L0_attn_bo"], "bv": i["L0_attn_bv"], "br": i["L1_ffn_br"],
        "w_gl": features_first(np.concatenate([i["L0_ffn_gate_W"], lora_a], 0)),
        "w_base": features_first(i["L0_ffn_base_W"]),
        "w_lb": lora_b,
        "w_qkv1": features_first(i["L1_attn_Wqkv"]),
        "w_o1": features_first(i["L1_attn_Wout"]),
        "w_xq": features_first(i["L1_xattn_Wq"]), "w_xk": features_first(i["L1_xattn_Wk"][by_column_tile[:XKV * XD]]),
        "w_xv": features_first(i["L1_xattn_Wv"]), "w_xo": features_first(i["L1_xattn_Wo"][:, by_column_tile]),
        "w_al": features_first(np.concatenate([i["L1_ffn_A"].reshape(LH * LR, D), i["L1_ffn_Wr"]], 0)),
        "w_bl": i["L1_ffn_B"].transpose(0, 2, 1).reshape(LH * LR, 1, D),
        **consts,
    }
    arrays = {k: np.ascontiguousarray(v) for k, v in arrays.items()}
    arrays["dft"] = arrays["dft"].reshape(P, 12 * P)
    nc = bacc.Bacc("TRN2", target_bir_lowering=False, num_devices=1)
    aps = {k: nc.dram_tensor(f"{k}_dram", v.shape, F32, kind="ExternalInput").ap() for k, v in arrays.items()}
    out = nc.dram_tensor("out_dram", (B, L, D), F32, kind="ExternalOutput").ap()
    decoder(nc, aps, out, slopes)
    r = run_bass_kernel_spmd(nc, [{f"{k}_dram": v for k, v in arrays.items()}], core_ids=[0])
    return r.results[0]["out_dram"]
```
